# Optimizing a Trainium2 kernel written in Bass

```python
import numpy as np
import jax
import jax.numpy as jnp

def _softmax(x, axis=-1):
    return jax.nn.softmax(x, axis=axis)

def _gelu(x):
    return jax.nn.gelu(x, approximate=True)

def _silu(x):
    return jax.nn.silu(x)

def _sigmoid(x):
    return jax.nn.sigmoid(x)

def _layernorm(x, axis=-1, eps=1e-05):
    m = jnp.mean(x, axis=axis, keepdims=True)
    v = jnp.var(x, axis=axis, keepdims=True)
    return (x - m) / jnp.sqrt(v + eps)

def _scatter_add(tgt, idx, src, axis=0):
    return tgt.at[idx].add(src)

def _segment_sum(src, seg, n):
    return jax.ops.segment_sum(src, seg, n)
kernel_name = 'mk_decoder_preln_d2_seqx_r8_baee93'

def setup_inputs(seed: int=0):
    np.random.seed(seed)
    _w = jnp.asarray

    def _rec_inputs():
        import jax
        import jax.numpy as jnp
        _rk = jax.random.key(seed)
        x = -0.0002928 + 1 * jax.random.normal(jax.random.fold_in(_rk, 1), (64, 128, 128), jnp.float32)
        _lenS = 128 - jax.random.randint(jax.random.fold_in(_rk, 7), (64,), 0, max(1, 128 // 4) + 1, jnp.int32)
        _lenS2 = 77 - jax.random.randint(jax.random.fold_in(_rk, 8), (64,), 0, max(1, 77 // 4) + 1, jnp.int32)
        _ctx_1024P = jax.random.normal(jax.random.fold_in(_rk, 11), (64, 16, 128), jnp.float32)
        _ctx_1024c = jax.random.dirichlet(jax.random.fold_in(_rk, 511), 0.3 * jnp.ones((16,), jnp.float32), (64, 77))
        _ctx_1024t = jnp.einsum('bsk,bkd->bsd', _ctx_1024c, _ctx_1024P)
        _ctx_1024t = _ctx_1024t * jax.lax.rsqrt(jnp.mean(jnp.square(_ctx_1024t)) + 1e-12) * 0.953939
        ctx_1024 = 4.13588e-05 + 0.999923 * (_ctx_1024t + 0.3 * jax.random.normal(jax.random.fold_in(_rk, 611), (64, 77, 128), jnp.float32))
        return (x, ctx_1024)
    x, ctx_1024 = _rec_inputs()

    def _L0_attn_setup():
        import math
        import jax, jax.numpy as jnp
        import numpy as np
        D_MODEL = 128
        N_HEADS = 16
        D_K = D_MODEL // N_HEADS
        D_C = 32
        B, S = (2, 256)
        key = jax.random.key(seed)
        ks = jax.random.split(key, 7)
        sd = lambda fan_in: 1.0 / math.sqrt(fan_in)
        return {'x': jax.random.normal(ks[0], (B, S, D_MODEL), dtype=jnp.float32), 'W_dq': jax.random.uniform(ks[1], (D_MODEL, D_C), minval=-sd(D_MODEL), maxval=sd(D_MODEL), dtype=jnp.float32), 'W_uq': jax.random.uniform(ks[2], (D_C, N_HEADS * D_K), minval=-sd(D_C), maxval=sd(D_C), dtype=jnp.float32), 'W_dkv': jax.random.uniform(ks[3], (D_MODEL, D_C), minval=-sd(D_MODEL), maxval=sd(D_MODEL), dtype=jnp.float32), 'W_uk': jax.random.uniform(ks[4], (D_C, N_HEADS * D_K), minval=-sd(D_C), maxval=sd(D_C), dtype=jnp.float32), 'W_uv': jax.random.uniform(ks[5], (D_C, N_HEADS * D_K), minval=-sd(D_C), maxval=sd(D_C), dtype=jnp.float32), 'W_o': jax.random.uniform(ks[6], (N_HEADS * D_K, D_MODEL), minval=-sd(N_HEADS * D_K), maxval=sd(N_HEADS * D_K), dtype=jnp.float32)}
    _L0_attn_all = _L0_attn_setup()
    _L0_attn_in = {k: v for k, v in _L0_attn_all.items() if k in ('W_dq', 'W_uq', 'W_dkv', 'W_uk', 'W_uv', 'W_o')}
    del _L0_attn_all

    def _L0_xattn_setup():
        import jax, jax.numpy as jnp
        import numpy as np
        DIM = 128
        NUM_HEADS = 16
        DIM_HEAD = 64
        INNER = NUM_HEADS * DIM_HEAD
        SCALE = DIM_HEAD ** (-0.5)

        def _layernorm(x, gamma, beta, eps=1e-05):
            mu = jnp.mean(x, axis=-1, keepdims=True)
            var = jnp.mean(jnp.square(x - mu), axis=-1, keepdims=True)
            return (x - mu) * jax.lax.rsqrt(var + eps) * gamma + beta
        key = jax.random.key(seed)
        ks = jax.random.split(key, 8)
        B, SQ, SK = (2, 256, 512)
        x = jax.random.normal(ks[0], (B, SQ, DIM), dtype=jnp.float32)
        context = jax.random.normal(ks[1], (B, SK, DIM), dtype=jnp.float32)
        ln_gamma = jnp.ones((DIM,), jnp.float32)
        ln_beta = jnp.zeros((DIM,), jnp.float32)
        w_q = jax.random.normal(ks[2], (DIM, INNER), dtype=jnp.float32) / np.sqrt(DIM)
        w_kv = jax.random.normal(ks[3], (DIM, 2 * INNER), dtype=jnp.float32) / np.sqrt(DIM)
        w_out = jax.random.normal(ks[4], (INNER, DIM), dtype=jnp.float32) / np.sqrt(INNER)
        b_out = jnp.zeros((DIM,), jnp.float32)
        gate = jnp.array([0.5], jnp.float32)
        return {'x': x, 'context': context, 'ln_gamma': ln_gamma, 'ln_beta': ln_beta, 'w_q': w_q, 'w_kv': w_kv, 'w_out': w_out, 'b_out': b_out, 'gate': gate}
    _L0_xattn_all = _L0_xattn_setup()
    _L0_xattn_in = {k: v for k, v in _L0_xattn_all.items() if k in ('ln_gamma', 'ln_beta', 'w_q', 'w_kv', 'w_out', 'b_out', 'gate')}
    del _L0_xattn_all

    def _L0_ffn_setup():
        import jax, jax.numpy as jnp
        import numpy as np
        TOP_K = 2
        key = jax.random.key(seed)
        ks = jax.random.split(key, 5)
        B, S, D, H, E = (2, 256, 128, 352, 8)
        x = jax.random.normal(ks[0], (B, S, D), dtype=jnp.float32)
        Wg = jax.random.normal(ks[1], (E, D), dtype=jnp.float32) * 0.02
        W1 = jax.random.normal(ks[2], (E, H, D), dtype=jnp.float32) * 0.02
        W2 = jax.random.normal(ks[3], (E, H, D), dtype=jnp.float32) * 0.02
        W3 = jax.random.normal(ks[4], (E, D, H), dtype=jnp.float32) * 0.02
        return {'x': x, 'Wg': Wg, 'W1': W1, 'W2': W2, 'W3': W3}
    _L0_ffn_all = _L0_ffn_setup()
    _L0_ffn_in = {k: v for k, v in _L0_ffn_all.items() if k in ('Wg', 'W1', 'W2', 'W3')}
    del _L0_ffn_all

    def _L1_attn_setup():
        import jax, jax.numpy as jnp
        import numpy as np
        N_HEADS = 16
        key = jax.random.key(seed)
        k_x, k_q, k_k, k_v, k_o = jax.random.split(key, 5)
        N, S, D = (8, 512, 128)
        scale = 0.02
        return {'x': jax.random.normal(k_x, (N, S, D), dtype=jnp.float32), 'Wq': jax.random.normal(k_q, (D, D), dtype=jnp.float32) * scale, 'Wk': jax.random.normal(k_k, (D, D), dtype=jnp.float32) * scale, 'Wv': jax.random.normal(k_v, (D, D), dtype=jnp.float32) * scale, 'Wo': jax.random.normal(k_o, (D, D), dtype=jnp.float32) * scale, 'bo': jnp.zeros((D,), dtype=jnp.float32)}
    _L1_attn_all = _L1_attn_setup()
    _L1_attn_in = {k: v for k, v in _L1_attn_all.items() if k in ('Wq', 'Wk', 'Wv', 'Wo', 'bo')}
    del _L1_attn_all

    def _L1_xattn_setup():
        import jax, jax.numpy as jnp
        import numpy as np
        import math
        B, S, D, H = (1, 256, 128, 16)
        DK = D // H
        DH = 64
        LOG_T_MIN = math.log(0.1)
        LOG_T_MAX = math.log(10.0)

        def _linear(x, W, b):
            return x @ W.T + b
        key = jax.random.key(seed)
        ks = jax.random.split(key, 20)
        p = 0.02
        return {'query': jax.random.normal(ks[0], (B, S, D), jnp.float32), 'key': jax.random.normal(ks[1], (B, S, D), jnp.float32), 'value': jax.random.normal(ks[2], (B, S, D), jnp.float32), 'Wq': jax.random.normal(ks[3], (D, D), jnp.float32) * p, 'bq': jax.random.normal(ks[4], (D,), jnp.float32) * p, 'Wk': jax.random.normal(ks[5], (D, D), jnp.float32) * p, 'bk': jax.random.normal(ks[6], (D,), jnp.float32) * p, 'Wv': jax.random.normal(ks[7], (D, D), jnp.float32) * p, 'bv': jax.random.normal(ks[8], (D,), jnp.float32) * p, 'Wo': jax.random.normal(ks[9], (D, D), jnp.float32) * p, 'bo': jax.random.normal(ks[10], (D,), jnp.float32) * p, 'w1': jax.random.normal(ks[11], (DH, 3), jnp.float32) * 0.3, 'b1': jax.random.normal(ks[12], (DH,), jnp.float32) * 0.1, 'w2': jax.random.normal(ks[13], (DH, DH), jnp.float32) * 0.1, 'b2': jax.random.normal(ks[14], (DH,), jnp.float32) * 0.1, 'w3': jax.random.normal(ks[15], (1, DH), jnp.float32) * 0.1, 'b3': jnp.full((1,), (LOG_T_MIN + LOG_T_MAX) / 2, jnp.float32)}
    _L1_xattn_all = _L1_xattn_setup()
    _L1_xattn_in = {k: v for k, v in _L1_xattn_all.items() if k in ('Wq', 'bq', 'Wk', 'bk', 'Wv', 'bv', 'Wo', 'bo', 'w1', 'b1', 'w2', 'b2', 'w3', 'b3')}
    del _L1_xattn_all

    def _L1_ffn_setup():
        import jax, jax.numpy as jnp
        import numpy as np
        B, S, H, I, E, K = (4, 256, 128, 512, 4, 2)

        def _layer_norm(h, g, b, eps=1e-05):
            mu = h.mean(-1, keepdims=True)
            var = ((h - mu) ** 2).mean(-1, keepdims=True)
            return (h - mu) * jax.lax.rsqrt(var + eps) * g + b
        key = jax.random.key(seed)
        ks = jax.random.split(key, 24)
        rn = lambda k, shape, s=0.02: jax.random.normal(k, shape, dtype=jnp.float32) * s
        z = lambda shape: jnp.zeros(shape, jnp.float32)
        o = lambda shape: jnp.ones(shape, jnp.float32)
        return {'x': rn(ks[0], (B, S, H), 1.0), 'router_w': rn(ks[1], (H, E)), 'router_b': z((E,)), 'load_balancer': o((E,)), 'sw_w1': rn(ks[2], (H, I)), 'sw_w3': rn(ks[3], (H, I)), 'sw_w2': rn(ks[4], (I, H)), 'me_eq_w': rn(ks[5], (H, H)), 'me_eq_b': z((H,)), 'me_wv': rn(ks[6], (H, H)), 'me_bv': z((H,)), 'me_wo': rn(ks[7], (H, H)), 'me_bo': z((H,)), 'me_c1w': rn(ks[8], (H, 2 * H)), 'me_c1b': z((2 * H,)), 'me_c2w': rn(ks[9], (2 * H, H)), 'me_c2b': z((H,)), 'ce_syn_w': rn(ks[10], (H, H)), 'ce_syn_b': z((H,)), 'ce_wv': rn(ks[11], (H, H)), 'ce_bv': z((H,)), 'ce_wo': rn(ks[12], (H, H)), 'ce_bo': z((H,)), 'ce_n1g': o((H,)), 'ce_n1b': z((H,)), 'ce_f1w': rn(ks[13], (H, 2 * H)), 'ce_f1b': z((2 * H,)), 'ce_f2w': rn(ks[14], (2 * H, H)), 'ce_f2b': z((H,)), 'ce_n2g': o((H,)), 'ce_n2b': z((H,)), 'ce_gen_w': rn(ks[15], (H, H)), 'ce_gen_b': z((H,)), 'ml_w1': rn(ks[16], (H, I)), 'ml_b1': z((I,)), 'ml_w2': rn(ks[17], (I, H)), 'ml_b2': z((H,))}
    _L1_ffn_all = _L1_ffn_setup()
    _L1_ffn_in = {k: v for k, v in _L1_ffn_all.items() if k in ('router_w', 'router_b', 'load_balancer', 'sw_w1', 'sw_w3', 'sw_w2', 'me_eq_w', 'me_eq_b', 'me_wv', 'me_bv', 'me_wo', 'me_bo', 'me_c1w', 'me_c1b', 'me_c2w', 'me_c2b', 'ce_syn_w', 'ce_syn_b', 'ce_wv', 'ce_bv', 'ce_wo', 'ce_bo', 'ce_n1g', 'ce_n1b', 'ce_f1w', 'ce_f1b', 'ce_f2w', 'ce_f2b', 'ce_n2g', 'ce_n2b', 'ce_gen_w', 'ce_gen_b', 'ml_w1', 'ml_b1', 'ml_w2', 'ml_b2')}
    del _L1_ffn_all
    return {'x': x, 'ctx_1024': ctx_1024, 'L0_attn_W_dq': _L0_attn_in['W_dq'], 'L0_attn_W_uq': _L0_attn_in['W_uq'], 'L0_attn_W_dkv': _L0_attn_in['W_dkv'], 'L0_attn_W_uk': _L0_attn_in['W_uk'], 'L0_attn_W_uv': _L0_attn_in['W_uv'], 'L0_attn_W_o': _L0_attn_in['W_o'], 'L0_xattn_ln_gamma': _L0_xattn_in['ln_gamma'], 'L0_xattn_ln_beta': _L0_xattn_in['ln_beta'], 'L0_xattn_w_q': _L0_xattn_in['w_q'], 'L0_xattn_w_kv': _L0_xattn_in['w_kv'], 'L0_xattn_w_out': _L0_xattn_in['w_out'], 'L0_xattn_b_out': _L0_xattn_in['b_out'], 'L0_xattn_gate': _L0_xattn_in['gate'], 'L0_ffn_Wg': _L0_ffn_in['Wg'], 'L0_ffn_W1': _L0_ffn_in['W1'], 'L0_ffn_W2': _L0_ffn_in['W2'], 'L0_ffn_W3': _L0_ffn_in['W3'], 'L1_attn_Wq': _L1_attn_in['Wq'], 'L1_attn_Wk': _L1_attn_in['Wk'], 'L1_attn_Wv': _L1_attn_in['Wv'], 'L1_attn_Wo': _L1_attn_in['Wo'], 'L1_attn_bo': _L1_attn_in['bo'], 'L1_xattn_Wq': _L1_xattn_in['Wq'], 'L1_xattn_bq': _L1_xattn_in['bq'], 'L1_xattn_Wk': _L1_xattn_in['Wk'], 'L1_xattn_bk': _L1_xattn_in['bk'], 'L1_xattn_Wv': _L1_xattn_in['Wv'], 'L1_xattn_bv': _L1_xattn_in['bv'], 'L1_xattn_Wo': _L1_xattn_in['Wo'], 'L1_xattn_bo': _L1_xattn_in['bo'], 'L1_xattn_w1': _L1_xattn_in['w1'], 'L1_xattn_b1': _L1_xattn_in['b1'], 'L1_xattn_w2': _L1_xattn_in['w2'], 'L1_xattn_b2': _L1_xattn_in['b2'], 'L1_xattn_w3': _L1_xattn_in['w3'], 'L1_xattn_b3': _L1_xattn_in['b3'], 'L1_ffn_router_w': _L1_ffn_in['router_w'], 'L1_ffn_router_b': _L1_ffn_in['router_b'], 'L1_ffn_load_balancer': _L1_ffn_in['load_balancer'], 'L1_ffn_sw_w1': _L1_ffn_in['sw_w1'], 'L1_ffn_sw_w3': _L1_ffn_in['sw_w3'], 'L1_ffn_sw_w2': _L1_ffn_in['sw_w2'], 'L1_ffn_me_eq_w': _L1_ffn_in['me_eq_w'], 'L1_ffn_me_eq_b': _L1_ffn_in['me_eq_b'], 'L1_ffn_me_wv': _L1_ffn_in['me_wv'], 'L1_ffn_me_bv': _L1_ffn_in['me_bv'], 'L1_ffn_me_wo': _L1_ffn_in['me_wo'], 'L1_ffn_me_bo': _L1_ffn_in['me_bo'], 'L1_ffn_me_c1w': _L1_ffn_in['me_c1w'], 'L1_ffn_me_c1b': _L1_ffn_in['me_c1b'], 'L1_ffn_me_c2w': _L1_ffn_in['me_c2w'], 'L1_ffn_me_c2b': _L1_ffn_in['me_c2b'], 'L1_ffn_ce_syn_w': _L1_ffn_in['ce_syn_w'], 'L1_ffn_ce_syn_b': _L1_ffn_in['ce_syn_b'], 'L1_ffn_ce_wv': _L1_ffn_in['ce_wv'], 'L1_ffn_ce_bv': _L1_ffn_in['ce_bv'], 'L1_ffn_ce_wo': _L1_ffn_in['ce_wo'], 'L1_ffn_ce_bo': _L1_ffn_in['ce_bo'], 'L1_ffn_ce_n1g': _L1_ffn_in['ce_n1g'], 'L1_ffn_ce_n1b': _L1_ffn_in['ce_n1b'], 'L1_ffn_ce_f1w': _L1_ffn_in['ce_f1w'], 'L1_ffn_ce_f1b': _L1_ffn_in['ce_f1b'], 'L1_ffn_ce_f2w': _L1_ffn_in['ce_f2w'], 'L1_ffn_ce_f2b': _L1_ffn_in['ce_f2b'], 'L1_ffn_ce_n2g': _L1_ffn_in['ce_n2g'], 'L1_ffn_ce_n2b': _L1_ffn_in['ce_n2b'], 'L1_ffn_ce_gen_w': _L1_ffn_in['ce_gen_w'], 'L1_ffn_ce_gen_b': _L1_ffn_in['ce_gen_b'], 'L1_ffn_ml_w1': _L1_ffn_in['ml_w1'], 'L1_ffn_ml_b1': _L1_ffn_in['ml_b1'], 'L1_ffn_ml_w2': _L1_ffn_in['ml_w2'], 'L1_ffn_ml_b2': _L1_ffn_in['ml_b2']}

def reference(x, ctx_1024, L0_attn_W_dq, L0_attn_W_uq, L0_attn_W_dkv, L0_attn_W_uk, L0_attn_W_uv, L0_attn_W_o, L0_xattn_ln_gamma, L0_xattn_ln_beta, L0_xattn_w_q, L0_xattn_w_kv, L0_xattn_w_out, L0_xattn_b_out, L0_xattn_gate, L0_ffn_Wg, L0_ffn_W1, L0_ffn_W2, L0_ffn_W3, L1_attn_Wq, L1_attn_Wk, L1_attn_Wv, L1_attn_Wo, L1_attn_bo, L1_xattn_Wq, L1_xattn_bq, L1_xattn_Wk, L1_xattn_bk, L1_xattn_Wv, L1_xattn_bv, L1_xattn_Wo, L1_xattn_bo, L1_xattn_w1, L1_xattn_b1, L1_xattn_w2, L1_xattn_b2, L1_xattn_w3, L1_xattn_b3, L1_ffn_router_w, L1_ffn_router_b, L1_ffn_load_balancer, L1_ffn_sw_w1, L1_ffn_sw_w3, L1_ffn_sw_w2, L1_ffn_me_eq_w, L1_ffn_me_eq_b, L1_ffn_me_wv, L1_ffn_me_bv, L1_ffn_me_wo, L1_ffn_me_bo, L1_ffn_me_c1w, L1_ffn_me_c1b, L1_ffn_me_c2w, L1_ffn_me_c2b, L1_ffn_ce_syn_w, L1_ffn_ce_syn_b, L1_ffn_ce_wv, L1_ffn_ce_bv, L1_ffn_ce_wo, L1_ffn_ce_bo, L1_ffn_ce_n1g, L1_ffn_ce_n1b, L1_ffn_ce_f1w, L1_ffn_ce_f1b, L1_ffn_ce_f2w, L1_ffn_ce_f2b, L1_ffn_ce_n2g, L1_ffn_ce_n2b, L1_ffn_ce_gen_w, L1_ffn_ce_gen_b, L1_ffn_ml_w1, L1_ffn_ml_b1, L1_ffn_ml_w2, L1_ffn_ml_b2):
    import jax
    import jax.numpy as jnp

    def _L0_attn_ref(x, W_dq, W_uq, W_dkv, W_uk, W_uv, W_o):
        import math
        import jax, jax.numpy as jnp
        import numpy as np
        D_MODEL = 128
        N_HEADS = 16
        D_K = D_MODEL // N_HEADS
        D_C = 32
        B, S = (2, 256)
        Bx, Sx, _ = x.shape
        c_q = x @ W_dq
        Q = (c_q @ W_uq).reshape(Bx, Sx, N_HEADS, D_K)
        c_kv = x @ W_dkv
        K = (c_kv @ W_uk).reshape(Bx, Sx, N_HEADS, D_K)
        V = (c_kv @ W_uv).reshape(Bx, Sx, N_HEADS, D_K)
        scores = jnp.einsum('bqhd,bkhd->bhqk', Q, K) / math.sqrt(D_K)
        causal = jnp.tril(jnp.ones((Sx, Sx), dtype=bool))
        scores = jnp.where(causal, scores, -jnp.inf)
        attn = jax.nn.softmax(scores, axis=-1)
        out = jnp.einsum('bhqk,bkhd->bqhd', attn, V).reshape(Bx, Sx, N_HEADS * D_K)
        return out @ W_o

    def _L0_xattn_ref(x, context, ln_gamma, ln_beta, w_q, w_kv, w_out, b_out, gate):
        import jax, jax.numpy as jnp
        import numpy as np
        DIM = 128
        NUM_HEADS = 16
        DIM_HEAD = 64
        INNER = NUM_HEADS * DIM_HEAD
        SCALE = DIM_HEAD ** (-0.5)

        def _layernorm(x, gamma, beta, eps=1e-05):
            mu = jnp.mean(x, axis=-1, keepdims=True)
            var = jnp.mean(jnp.square(x - mu), axis=-1, keepdims=True)
            return (x - mu) * jax.lax.rsqrt(var + eps) * gamma + beta
        B, SQ, _ = x.shape
        SK = context.shape[1]
        xn = _layernorm(x, ln_gamma, ln_beta)
        q = (xn @ w_q).reshape(B, SQ, NUM_HEADS, DIM_HEAD)
        kv = context @ w_kv
        k, v = jnp.split(kv, 2, axis=-1)
        k = k.reshape(B, SK, NUM_HEADS, DIM_HEAD)
        v = v.reshape(B, SK, NUM_HEADS, DIM_HEAD)
        scores = jnp.einsum('bqhd,bkhd->bhqk', q * SCALE, k)
        attn = jax.nn.softmax(scores, axis=-1)
        out = jnp.einsum('bhqk,bkhd->bqhd', attn, v).reshape(B, SQ, INNER)
        out = out @ w_out + b_out
        return out * jnp.tanh(gate[0])

    def _L0_ffn_ref(x, Wg, W1, W2, W3):
        import jax, jax.numpy as jnp
        import numpy as np
        TOP_K = 2
        B, S, D = x.shape
        E = Wg.shape[0]
        xt = x.reshape(B * S, D)
        scores = xt @ Wg.T
        topk_scores, topk_idx = jax.lax.top_k(scores, TOP_K)
        gate = jax.nn.silu(jnp.einsum('td,ehd->teh', xt, W1))
        up = jnp.einsum('td,ehd->teh', xt, W2)
        y = jnp.einsum('teh,edh->ted', gate * up, W3)
        onehot = jax.nn.one_hot(topk_idx, E, dtype=x.dtype)
        w = jnp.einsum('tke,tk->te', onehot, topk_scores)
        out = jnp.einsum('te,ted->td', w, y)
        return out.reshape(B, S, D)

    def _L1_attn_ref(x, Wq, Wk, Wv, Wo, bo):
        import jax, jax.numpy as jnp
        import numpy as np
        N_HEADS = 16
        N, S, D = x.shape
        H = N_HEADS
        hd = D // H
        q = (x @ Wq.T).reshape(N, S, H, hd).transpose(0, 2, 1, 3)
        k = (x @ Wk.T).reshape(N, S, H, hd).transpose(0, 2, 1, 3)
        v = (x @ Wv.T).reshape(N, S, H, hd).transpose(0, 2, 1, 3)
        att = jnp.einsum('nqhd,nkhd->nhqk', q, k)
        att = jax.nn.softmax(att / jnp.sqrt(jnp.asarray(hd, x.dtype)), axis=3)
        out = jnp.einsum('nhqk,nkhd->nqhd', att, v).reshape(N, S, D)
        return out @ Wo.T + bo

    def _L1_xattn_ref(query, key, value, Wq, bq, Wk, bk, Wv, bv, Wo, bo, w1, b1, w2, b2, w3, b3):
        import jax, jax.numpy as jnp
        import numpy as np
        import math
        B, S, D, H = (1, 256, 128, 16)
        DK = D // H
        DH = 64
        LOG_T_MIN = math.log(0.1)
        LOG_T_MAX = math.log(10.0)

        def _linear(x, W, b):
            return x @ W.T + b
        b, sq, d = query.shape
        sk = key.shape[1]
        h, dk = (H, DK)
        Q = _linear(query, Wq, bq).reshape(b, sq, h, dk).transpose(0, 2, 1, 3)
        K = _linear(key, Wk, bk).reshape(b, sk, h, dk).transpose(0, 2, 1, 3)
        V = _linear(value, Wv, bv).reshape(b, sk, h, dk).transpose(0, 2, 1, 3)
        qk = jnp.einsum('bhqd,bhkd->bhqk', Q, K)
        scores = qk / math.sqrt(dk)
        mean_sim = scores.mean(axis=(-2, -1))
        max_sim = scores.max(axis=-1).mean(axis=-1)
        probs = jax.nn.softmax(scores, axis=-1)
        entropy_proxy = jnp.var(probs, axis=-1, ddof=1).mean(axis=-1)
        feats = jnp.stack([mean_sim, max_sim, entropy_proxy], axis=-1)
        hidden = jax.nn.gelu(_linear(feats, w1, b1), approximate=False)
        hidden = jax.nn.gelu(_linear(hidden, w2, b2), approximate=False)
        log_t = jnp.clip(_linear(hidden, w3, b3), LOG_T_MIN, LOG_T_MAX)
        t = jnp.exp(log_t)[..., None]
        attn_scores = qk / (2.0 * t)
        attn = jax.nn.softmax(attn_scores, axis=-1)
        attn = jnp.nan_to_num(attn, nan=0.0)
        out = jnp.einsum('bhqk,bhkd->bhqd', attn, V)
        out = out.transpose(0, 2, 1, 3).reshape(b, sq, d)
        return _linear(out, Wo, bo)

    def _L1_ffn_ref(x, router_w, router_b, load_balancer, sw_w1, sw_w3, sw_w2, me_eq_w, me_eq_b, me_wv, me_bv, me_wo, me_bo, me_c1w, me_c1b, me_c2w, me_c2b, ce_syn_w, ce_syn_b, ce_wv, ce_bv, ce_wo, ce_bo, ce_n1g, ce_n1b, ce_f1w, ce_f1b, ce_f2w, ce_f2b, ce_n2g, ce_n2b, ce_gen_w, ce_gen_b, ml_w1, ml_b1, ml_w2, ml_b2):
        import jax, jax.numpy as jnp
        import numpy as np
        B, S, H, I, E, K = (4, 256, 128, 512, 4, 2)

        def _layer_norm(h, g, b, eps=1e-05):
            mu = h.mean(-1, keepdims=True)
            var = ((h - mu) ** 2).mean(-1, keepdims=True)
            return (h - mu) * jax.lax.rsqrt(var + eps) * g + b
        logits = jnp.einsum('bsh,he->bse', x, router_w) + router_b + load_balancer
        rw, sel = jax.lax.top_k(logits, K)
        rw = jax.nn.softmax(rw, axis=-1)
        e0 = jax.nn.silu(x @ sw_w1) * (x @ sw_w3) @ sw_w2
        eq = x @ me_eq_w + me_eq_b
        sym = (eq @ me_wv + me_bv) @ me_wo + me_bo
        e1 = jax.nn.gelu(sym @ me_c1w + me_c1b, approximate=False) @ me_c2w + me_c2b
        syn = x @ ce_syn_w + ce_syn_b
        attn = (syn @ ce_wv + ce_bv) @ ce_wo + ce_bo
        h2 = _layer_norm(syn + attn, ce_n1g, ce_n1b)
        ff = jax.nn.relu(h2 @ ce_f1w + ce_f1b) @ ce_f2w + ce_f2b
        h2 = _layer_norm(h2 + ff, ce_n2g, ce_n2b)
        e2 = h2 @ ce_gen_w + ce_gen_b
        e3 = jax.nn.gelu(x @ ml_w1 + ml_b1, approximate=False) @ ml_w2 + ml_b2
        stack = jnp.stack([e0, e1, e2, e3], axis=2)
        gathered = jnp.take_along_axis(stack, sel[..., None], axis=2)
        return (rw[..., None] * gathered).sum(axis=2)
    x = x + _L0_attn_ref(_layernorm(x, axis=-1), L0_attn_W_dq, L0_attn_W_uq, L0_attn_W_dkv, L0_attn_W_uk, L0_attn_W_uv, L0_attn_W_o)
    x = x + _L0_xattn_ref(_layernorm(x, axis=-1), ctx_1024, L0_xattn_ln_gamma, L0_xattn_ln_beta, L0_xattn_w_q, L0_xattn_w_kv, L0_xattn_w_out, L0_xattn_b_out, L0_xattn_gate)
    x = x + _L0_ffn_ref(_layernorm(x, axis=-1), L0_ffn_Wg, L0_ffn_W1, L0_ffn_W2, L0_ffn_W3)
    x = x + _L1_attn_ref(_layernorm(x, axis=-1), L1_attn_Wq, L1_attn_Wk, L1_attn_Wv, L1_attn_Wo, L1_attn_bo)
    x = x + _L1_xattn_ref(_layernorm(x, axis=-1), ctx_1024, ctx_1024, L1_xattn_Wq, L1_xattn_bq, L1_xattn_Wk, L1_xattn_bk, L1_xattn_Wv, L1_xattn_bv, L1_xattn_Wo, L1_xattn_bo, L1_xattn_w1, L1_xattn_b1, L1_xattn_w2, L1_xattn_b2, L1_xattn_w3, L1_xattn_b3)
    x = x + _L1_ffn_ref(_layernorm(x, axis=-1), L1_ffn_router_w, L1_ffn_router_b, L1_ffn_load_balancer, L1_ffn_sw_w1, L1_ffn_sw_w3, L1_ffn_sw_w2, L1_ffn_me_eq_w, L1_ffn_me_eq_b, L1_ffn_me_wv, L1_ffn_me_bv, L1_ffn_me_wo, L1_ffn_me_bo, L1_ffn_me_c1w, L1_ffn_me_c1b, L1_ffn_me_c2w, L1_ffn_me_c2b, L1_ffn_ce_syn_w, L1_ffn_ce_syn_b, L1_ffn_ce_wv, L1_ffn_ce_bv, L1_ffn_ce_wo, L1_ffn_ce_bo, L1_ffn_ce_n1g, L1_ffn_ce_n1b, L1_ffn_ce_f1w, L1_ffn_ce_f1b, L1_ffn_ce_f2w, L1_ffn_ce_f2b, L1_ffn_ce_n2g, L1_ffn_ce_n2b, L1_ffn_ce_gen_w, L1_ffn_ce_gen_b, L1_ffn_ml_w1, L1_ffn_ml_b1, L1_ffn_ml_w2, L1_ffn_ml_b2)
    return x

_drawn_inputs = setup_inputs


def setup_inputs(seed=0):
    import zlib

    import numpy as np

    out = dict(_drawn_inputs(seed))
    spreads = {'L0_xattn_ln_gamma': (1.0, 0.6),
     'L0_xattn_ln_beta': (0.0, 0.686),
     'L0_xattn_b_out': (0.0, 0.1),
     'L1_attn_bo': (0.0, 0.677),
     'L1_ffn_router_b': (0.0, 0.1),
     'L1_ffn_load_balancer': (1.0, 0.2),
     'L1_ffn_me_eq_b': (0.0, 0.8),
     'L1_ffn_me_bv': (0.0, 2.0),
     'L1_ffn_me_bo': (0.0, 2.0),
     'L1_ffn_me_c1b': (0.0, 2.0),
     'L1_ffn_me_c2b': (0.0, 2.0),
     'L1_ffn_ce_syn_b': (0.0, 2.0),
     'L1_ffn_ce_bv': (0.0, 2.0),
     'L1_ffn_ce_bo': (0.0, 2.0),
     'L1_ffn_ce_n1g': (1.0, 0.6),
     'L1_ffn_ce_n1b': (0.0, 2.0),
     'L1_ffn_ce_f1b': (0.0, 2.0),
     'L1_ffn_ce_f2b': (0.0, 2.0),
     'L1_ffn_ce_n2g': (1.0, 0.6),
     'L1_ffn_ce_n2b': (0.0, 2.0),
     'L1_ffn_ce_gen_b': (0.0, 2.0),
     'L1_ffn_ml_b1': (0.0, 2.0),
     'L1_ffn_ml_b2': (0.0, 2.0)}
    factors = {'L0_attn_W_dq': 8.0,
     'L0_attn_W_uq': 8.0,
     'L0_attn_W_uk': 8.0,
     'L0_ffn_Wg': 8.0,
     'L0_ffn_W1': 8.0,
     'L0_ffn_W2': 8.0,
     'L0_ffn_W3': 8.0,
     'L1_attn_Wq': 8.0,
     'L1_attn_Wk': 8.0,
     'L1_attn_Wv': 4.555,
     'L1_attn_Wo': 4.337,
     'L1_xattn_Wq': 62.522,
     'L1_xattn_bq': 64.0,
     'L1_xattn_Wk': 62.337,
     'L1_xattn_bk': 200.0,
     'L1_xattn_bv': 50.287,
     'L1_xattn_w1': 64.0,
     'L1_xattn_b1': 8.0,
     'L1_xattn_w2': 8.0,
     'L1_xattn_b2': 8.0,
     'L1_xattn_w3': 8.0,
     'L1_ffn_sw_w1': 8.0,
     'L1_ffn_sw_w3': 8.0,
     'L1_ffn_sw_w2': 8.0,
     'L1_ffn_me_eq_w': 8.0,
     'L1_ffn_me_wv': 8.0,
     'L1_ffn_me_wo': 8.0,
     'L1_ffn_me_c1w': 8.0,
     'L1_ffn_me_c2w': 8.0,
     'L1_ffn_ce_wv': 64.0,
     'L1_ffn_ce_wo': 36.304,
     'L1_ffn_ce_f1w': 64.0,
     'L1_ffn_ce_f2w': 57.509,
     'L1_ffn_ml_w1': 23.352,
     'L1_xattn_Wv': 5.561,
     'L1_xattn_Wo': 5.92,
     'L1_xattn_bo': 25.452,
     'L1_ffn_ce_syn_w': 8.0,
     'L1_ffn_ce_gen_w': 7.101,
     'L1_ffn_ml_w2': 8.0}
    for name, (base, spread) in spreads.items():
        noise = np.random.default_rng([zlib.crc32(name.encode()), seed]).standard_normal(out[name].shape)
        drawn = base * np.exp(spread * noise) if base else spread * noise
        out[name] = jnp.asarray(drawn.astype(out[name].dtype))
    for name, factor in factors.items():
        out[name] = (out[name] * factor).astype(out[name].dtype)
    return out
```

```python
from contextlib import ExitStack

import numpy as np

import concourse.bass as bass
import concourse.mybir as mybir

F32 = mybir.dt.float32
F32R = mybir.dt.float32r
BF16 = mybir.dt.bfloat16
ALU = mybir.AluOpType
ACT = mybir.ActivationFunctionType
AX = mybir.AxisListType

P = 128
D = 128
HEADS = 16
HD = 8
GROUPS = 4
GROUP = 4
STRIP = 32
EPS = 1e-5
MASKED = -1e30
UNROLL = 4


class Slot:

    def __init__(self, t, odd, steps, fixed):
        self.t, self.odd, self.steps, self.fixed = t, odd, steps, fixed

    def step(self, lag):
        if self.fixed and not 0 <= self.t - lag < self.steps:
            return None
        return self.t - lag, (self.odd - lag) % UNROLL


def run_slots(eng, slot, steps, lag, unroll=UNROLL):
    first = min(-(-(lag + 2) // unroll) * unroll, steps)
    last = steps - (steps - first) % unroll
    for t in range(first):
        slot(Slot(t, t % UNROLL, steps, True))
    if last > first:
        with eng.Fori(first // unroll, last // unroll) as i:
            for k in range(unroll):
                slot(Slot(i * unroll + k, k, steps, False))
    for t in range(last, steps + lag):
        slot(Slot(t, t % UNROLL, steps, True))


def wait(eng, sem, value):
    if not (isinstance(value, int) and value <= 0):
        eng.wait_ge(sem, value)


class Core:

    def __init__(self, nc, inputs, out, batches):
        self.nc, self.inp, self.out, self.B = nc, inputs, out, batches


def stage_scope(c):
    ctx = ExitStack()

    def sb(name, shape, dt=F32):
        return ctx.enter_context(c.nc.sbuf_tensor(f"{stage}_{name}", shape, dt))

    def ps(name, shape=(P, 512), dt=F32):
        return ctx.enter_context(c.nc.psum_tensor(f"{stage}_{name}", list(shape), dt))

    sems = []

    def sem(name):
        sems.append(c.nc.alloc_semaphore(name=f"{stage}_{name}"))
        return sems[-1]

    stage = c.stage

    def clear():
        c.nc.clear_and_free_semaphores(sems)
        c.nc.all_engine_barrier()

    ctx.callback(clear)
    return ctx, sb, ps, sem


def norm_scalars(c, second):
    nc = c.nc
    ctx, sb, ps, sem = stage_scope(c)
    with ctx:
        dif, var, vpe, root, rec, t1, t2 = (sb(n, [P, c.B]) for n in ("dif", "var", "vpe", "root", "rec", "t1", "t2"))
        dv = sem("dv")
        var_ready, root_ready = sem("var_ready"), sem("root_ready")
        block = ctx.enter_context(nc.Block())
        me, mo, ve, vo = (c.stats[:, :, k] for k in (1, 4, 2, 5))

        @block.vector
        def _(dve):
            n = [0]

            def own(ins):
                n[0] += 1
                ins.then_inc(dv, 1)
                dve.wait_ge(dv, n[0])

            def rsqrt(out, x, k):
                nc.vector.tensor_copy(vpe[:, :], x).then_inc(var_ready, 1)
                dve.wait_ge(root_ready, k)
                own(nc.vector.reciprocal(rec[:, :], root[:, :]))
                own(nc.vector.tensor_tensor(t1[:, :], rec[:, :], rec[:, :], ALU.mult))
                own(nc.vector.tensor_tensor(t2[:, :], t1[:, :], vpe[:, :], ALU.mult))
                own(nc.vector.tensor_scalar(t1[:, :], t2[:, :], -0.5, 1.5, ALU.mult, ALU.add))
                own(nc.vector.tensor_tensor(out, t1[:, :], rec[:, :], ALU.mult))

            own(nc.vector.tensor_tensor(t1[:, :], me, mo, ALU.add))
            own(nc.vector.tensor_scalar(c.mean[:, :], t1[:, :], 0.5, None, ALU.mult))
            own(nc.vector.tensor_tensor(dif[:, :], me, mo, ALU.subtract))
            own(nc.vector.tensor_tensor(t1[:, :], dif[:, :], dif[:, :], ALU.mult))
            own(nc.vector.tensor_tensor(t2[:, :], ve, vo, ALU.add))
            own(nc.vector.scalar_tensor_tensor(out=dif[:, :], in0=t1[:, :], scalar=D / 4, in1=t2[:, :],
                                               op0=ALU.mult, op1=ALU.add))
            own(nc.vector.tensor_scalar(var[:, :], dif[:, :], 1.0 / D, None, ALU.mult))
            own(nc.vector.tensor_scalar(t1[:, :], var[:, :], EPS, None, ALU.add))
            rsqrt(c.rstd[:, :], t1[:, :], 1)
            if second:
                own(nc.vector.tensor_tensor(t1[:, :], c.rstd[:, :], c.rstd[:, :], ALU.mult))
                own(nc.vector.tensor_tensor(t2[:, :], t1[:, :], var[:, :], ALU.mult))
                own(nc.vector.tensor_scalar(t1[:, :], t2[:, :], EPS, None, ALU.add))
                rsqrt(dif[:, :], t1[:, :], 2)
                own(nc.vector.tensor_tensor(t1[:, :], c.rstd[:, :], dif[:, :], ALU.mult))
                own(nc.vector.tensor_copy(c.rstd[:, :], t1[:, :]))

        @block.scalar
        def _(act):
            for k in range(2 if second else 1):
                act.wait_ge(var_ready, k + 1)
                nc.scalar.activation(root[:, :], vpe[:, :], ACT.Sqrt).then_inc(root_ready, 1)


def load_inputs(c, keep):
    nc = c.nc
    ctx, sb, ps, sem = stage_scope(c)
    with ctx:
        parts = max(1, c.B // 16)
        per = c.B // parts
        x_in = [sem(f"x_in{n}") for n in range(parts)]
        w_in, made = sem("w_in"), sem("made")
        block = ctx.enter_context(nc.Block())
        xs = c.inp["x"].rearrange("b p d -> p b d")

        @block.sync
        def _(sp):
            for n in range(parts):
                sp.dma_start(c.x[:, n * per:(n + 1) * per, :], xs[:, n * per:(n + 1) * per, :]).then_inc(x_in[n], 16)
            for name, tile in keep:
                sp.dma_start(tile, c.inp[name]).then_inc(w_in, 16)
            sp.wait_ge(w_in, 16 * len(keep))

        @block.vector
        def _(dve):
            for n in range(parts):
                dve.wait_ge(x_in[n], 16)
                for s in range(n * per, (n + 1) * per):
                    ins = nc.vector.bn_stats(c.stats[:, s, :], c.x[:, s, :])
            ins.then_inc(made, 1)
            dve.wait_ge(made, 1)


def self_attention(c, weights, scale):
    nc, B = c.nc, c.B
    ctx, sb, ps, sem = stage_scope(c)
    with ctx:
        wq, wk, wv, wo = weights
        xn = sb("xn", [P, 2, D])
        xT = sb("xT", [P, P])
        qkv = sb("qkv", [P, 2, 3, P])
        q_bd, k_bd = sb("q_bd", [P, 2, GROUP, P]), sb("k_bd", [P, 2, GROUP, P])
        v1 = sb("v1", [P, UNROLL, HEADS, STRIP])
        nmax = sb("nmax", [P, HEADS])
        rest = sb("rest", [P, 2, HEADS])
        part = sb("part", [P, 2, HEADS], BF16)
        pad = sb("pad", [P, P])
        fold = sb("fold", [P, 2, GROUP, P], BF16)
        e = sb("e", [P, 2, HEADS, P])
        oz = sb("oz", [P, 512])
        rz = sb("rz", [P, HEADS])
        o = sb("o", [P, 2, D])
        oT = sb("oT", [D, P])

        ps_misc, ps_qkv, ps_o, ps_z = ps("ps_misc"), ps("ps_qkv"), ps("ps_o"), ps("ps_z")
        ps_x, ps_f, ps_oT, ps_y = (ps_misc[:, n * P:n * P + P] for n in range(4))
        ps_n = [ps(f"ps_n{i}") for i in range(2)]
        ps_t = [ps(f"ps_t{i}") for i in range(2)]

        made = sem("made")
        xn_ready, xT_ps, xT_ready, qkv_ps, qkv_ready = (sem(n) for n in ("xn_ready", "xT_ps", "xT_ready", "qkv_ps", "qkv_ready"))
        k_bd_ready, q_bd_ready, v_ready = sem("k_bd_ready"), sem("q_bd_ready"), sem("v_ready")
        nat_ps, max_done, own, pad_ready, pad_ps, fold_ready = (
            sem(n) for n in ("nat_ps", "max_done", "own", "pad_ready", "pad_ps", "fold_ready"))
        sT_ps, exp_done = sem("sT_ps"), sem("exp_done")
        o_ps, oz_ready, z_ps, rz_ready, o_ready, oT_ps, oT_ready, y_ps, x_done = (
            sem(n) for n in ("o_ps", "oz_ready", "z_ps", "rz_ready", "o_ready", "oT_ps", "oT_ready", "y_ps", "x_done"))
        block = ctx.enter_context(nc.Block())
        LAG = 5

        def strip(g):
            return slice(STRIP * g, STRIP * g + STRIP)

        @block.tensor
        def _(pe):
            def slot(sl):
                if at := sl.step(4):
                    s, u = at
                    pe.wait_ge(exp_done, (s + 1) * GROUPS)
                    pe.wait_ge(v_ready, s + 1)
                    for n in range(HEADS):
                        j, g = divmod(n, GROUPS)
                        h = GROUP * g + j
                        ins = nc.tensor.matmul(ps_o[strip(g), j * P:j * P + P], v1[:, u, h, :], e[:, u % 2, h, :],
                                               start=True, stop=True)
                    ins.then_inc(o_ps, 1)
                if at := sl.step(1):
                    s, u = at
                    pe.wait_ge(xn_ready, s + 1)
                    wait(pe, fold_ready, s - 1)
                    wait(pe, x_done, s - 4)
                    nc.tensor.transpose(ps_x, xn[:, u % 2, :], c.ident[:, :]).then_inc(xT_ps, 1)
                if at := sl.step(2):
                    s, u = at
                    pe.wait_ge(k_bd_ready, s + 1)
                    for g in range(GROUPS):
                        wait(pe, max_done, s * GROUPS + g - 1)
                        nc.tensor.matmul(ps_n[g % 2][:, :], qkv[strip(g), u % 2, 0, :],
                                               k_bd[strip(g), u % 2, :, :], start=True, stop=False)
                        nc.tensor.matmul(ps_n[g % 2][:, :].rearrange("p (t k) -> p t k", t=GROUP), c.ident16[:, :],
                                         c.mask_q[:, :].unsqueeze(1).broadcast_to([P, GROUP, P]),
                                         start=False, stop=True).then_inc(nat_ps, 1)
                if at := sl.step(4):
                    s, u = at
                    pe.wait_ge(oz_ready, s + 1)
                    wait(pe, o_ready, s)
                    for j in range(GROUP):
                        ins = nc.tensor.transpose(ps_z[:, j * P:j * P + P], oz[:, j * P:j * P + P], c.ident[:, :])
                    ins.then_inc(z_ps, 1)
                if at := sl.step(5):
                    s, u = at
                    pe.wait_ge(o_ready, s + 1)
                    wait(pe, xT_ready, min(s + 5, B) if sl.fixed else s + 5)
                    wait(pe, x_done, s)
                    nc.tensor.transpose(ps_oT, o[:, u % 2, :], c.ident[:, :]).then_inc(oT_ps, 1)
                if at := sl.step(3):
                    s, u = at
                    pe.wait_ge(q_bd_ready, s + 1)
                    pe.wait_ge(fold_ready, s + 1)
                    for g in range(GROUPS):
                        wait(pe, exp_done, s * GROUPS + g - 1)
                        nc.tensor.matmul(ps_t[g % 2][:, :], qkv[strip(g), u % 2, 1, :], q_bd[strip(g), u % 2, :, :],
                                         start=True, stop=False)
                        nc.tensor.matmul(ps_t[g % 2][:, :].rearrange("p (t k) -> p t k", t=GROUP), c.ident16[:, :],
                                         c.mask_k[:, :].unsqueeze(1).broadcast_to([P, GROUP, P]),
                                         start=False, stop=False)
                        nc.tensor.matmul(ps_t[g % 2][:, :], c.ones16[strip(g), :], fold[strip(g), u % 2, :, :],
                                         start=False, stop=True).then_inc(sT_ps, 1)
                if at := sl.step(2):
                    s, u = at
                    pe.wait_ge(pad_ready, s + 1)
                    wait(pe, xT_ready, min(s + 2, B) if sl.fixed else s + 2)
                    wait(pe, oT_ready, s - 2)
                    nc.tensor.transpose(ps_f, pad[:, :], c.ident[:, :]).then_inc(pad_ps, 1)
                if at := sl.step(1):
                    s, u = at
                    pe.wait_ge(xT_ready, s + 1)
                    wait(pe, qkv_ready, s)
                    nc.tensor.matmul(ps_qkv[:, 0:P], wq, xT[:, :], start=True, stop=True)
                    nc.tensor.matmul(ps_qkv[:, P:2 * P], wk, xT[:, :], start=True, stop=True)
                    nc.tensor.matmul(ps_qkv[:, 2 * P:3 * P], xT[:, :], wv, start=True, stop=True).then_inc(qkv_ps, 1)
                if at := sl.step(5):
                    s, u = at
                    pe.wait_ge(oT_ready, s + 1)
                    wait(pe, fold_ready, min(s + 4, B) if sl.fixed else s + 4)
                    nc.tensor.matmul(ps_y, oT[:, :], wo, start=True, stop=True).then_inc(y_ps, 1)

            run_slots(pe, slot, B, LAG)

        @block.scalar
        def _(act):
            def slot(sl):
                if at := sl.step(4):
                    s, u = at
                    act.wait_ge(o_ps, s + 1)
                    wait(act, z_ps, s)
                    nc.scalar.activation(oz[:, :], ps_o[:, :], ACT.Copy).then_inc(oz_ready, 1)
                if at := sl.step(1):
                    s, u = at
                    act.wait_ge(xT_ps, s + 1)
                    nc.scalar.activation(xT[:, :], ps_x, ACT.Copy).then_inc(xT_ready, 1)
                if at := sl.step(5):
                    s, u = at
                    act.wait_ge(oT_ps, s + 1)
                    nc.scalar.activation(oT[:, :], ps_oT, ACT.Copy).then_inc(oT_ready, 1)
                if at := sl.step(3):
                    s, u = at
                    for g in range(GROUPS):
                        act.wait_ge(sT_ps, s * GROUPS + g + 1)
                        nc.scalar.activation(e[:, u % 2, GROUP * g:GROUP * g + GROUP, :],
                                             ps_t[g % 2][:, :].rearrange("p (t q) -> p t q", t=GROUP),
                                             ACT.Exp, scale=scale).then_inc(exp_done, 1)
                if at := sl.step(1):
                    s, u = at
                    act.wait_ge(qkv_ps, s + 1)
                    wait(act, v_ready, s - 1)
                    nc.scalar.activation(qkv[:, u % 2, :, :], ps_qkv[:, 0:3 * P].rearrange("p (n k) -> p n k", n=3),
                                         ACT.Copy).then_inc(qkv_ready, 1)

            run_slots(act, slot, B, LAG)

        @block.gpsimd
        def _(pool):
            nc.gpsimd.memset(v1[:, :, :, :], 1.0).then_inc(made, 1)
            pool.wait_ge(made, 1)

            def slot(sl):
                if at := sl.step(1):
                    s, u = at
                    pool.wait_ge(qkv_ready, s + 1)
                    for n, bd, ready in ((1, k_bd, k_bd_ready), (0, q_bd, q_bd_ready)):
                        nc.gpsimd.tensor_tensor(bd[:, u % 2, :, :], qkv[:, u % 2, n, :].unsqueeze(1).broadcast_to([P, GROUP, P]),
                                                c.block[:, 0:GROUP].unsqueeze(2).broadcast_to([P, GROUP, P]),
                                                ALU.mult).then_inc(ready, 1)
                    nc.gpsimd.tensor_copy(v1[:, u, :, 0:HD], qkv[:, u % 2, 2, :].rearrange("p (h d) -> p h d", d=HD)).then_inc(v_ready, 1)

            run_slots(pool, slot, B, LAG)

        @block.vector
        def _(dve):
            nc.vector.memset(pad[:, :], 0.0)
            rows = pad[:, :].rearrange("p (g r) -> p g r", g=GROUPS)

            def heads(t):
                return t.rearrange("p (g j) -> p g j", g=GROUPS)

            def slot(sl):
                if at := sl.step(0):
                    s, u = at
                    wait(dve, xT_ps, s - 1)
                    nc.vector.tensor_scalar(xn[:, u % 2, :], c.x[:, s, :], c.mean[:, bass.ds(s, 1)], c.rstd[:, bass.ds(s, 1)],
                                            ALU.subtract, ALU.mult).then_inc(xn_ready, 1)
                if at := sl.step(2):
                    s, u = at
                    for g in range(GROUPS):
                        dve.wait_ge(nat_ps, s * GROUPS + g + 1)
                        nc.vector.tensor_reduce(nmax[:, GROUP * g:GROUP * g + GROUP],
                                                ps_n[g % 2][:, :].rearrange("p (t k) -> p t k", t=GROUP),
                                                AX.X, ALU.max, negate=True).then_inc(max_done, 1)
                    dve.wait_ge(max_done, (s + 1) * GROUPS)
                    left = nmax[:, :]
                    for n in range(2):
                        nc.vector.tensor_copy(part[:, n, :], left).then_inc(own, 1)
                        dve.wait_ge(own, 4 * s + 2 * n + 1)
                        nc.vector.tensor_copy(rows[:, :, GROUP * n:GROUP * n + GROUP], heads(part[:, n, :]))
                        nc.vector.tensor_tensor(rest[:, n, :], left, part[:, n, :], ALU.subtract).then_inc(own, 1)
                        left = rest[:, n, :]
                        dve.wait_ge(own, 4 * s + 2 * n + 2)
                    nc.vector.tensor_copy(rows[:, :, 2 * GROUP:3 * GROUP], heads(left)).then_inc(pad_ready, 1)
                if at := sl.step(4):
                    s, u = at
                    dve.wait_ge(z_ps, s + 1)
                    z = ps_z[:, :].rearrange("p (j g r) -> p g j r", j=GROUP, g=GROUPS)
                    nc.vector.reciprocal(heads(rz[:, :]), z[:, :, :, HD]).then_inc(rz_ready, 1)
                    dve.wait_ge(rz_ready, s + 1)
                    nc.vector.tensor_tensor(o[:, u % 2, :].rearrange("p (g j d) -> p g j d", g=GROUPS, j=GROUP), z[:, :, :, 0:HD],
                                            heads(rz[:, :]).unsqueeze(3).broadcast_to([P, GROUPS, GROUP, HD]),
                                            ALU.mult).then_inc(o_ready, 1)
                if at := sl.step(2):
                    s, u = at
                    dve.wait_ge(pad_ps, s + 1)
                    nc.vector.tensor_tensor(fold[:, u % 2, :, :], ps_f.unsqueeze(1).broadcast_to([P, GROUP, P]),
                                            c.block[:, GROUP:2 * GROUP].unsqueeze(2).broadcast_to([P, GROUP, P]),
                                            ALU.mult).then_inc(fold_ready, 1)
                if at := sl.step(5):
                    s, u = at
                    dve.wait_ge(y_ps, s + 1)
                    nc.vector.tensor_tensor(c.x[:, s, :], c.x[:, s, :], ps_y, ALU.add).then_inc(x_done, 1)
                    dve.wait_ge(x_done, s + 1)
                    nc.vector.bn_stats(c.stats[:, s, :], c.x[:, s, :])

            run_slots(dve, slot, B, LAG)


def wide_weights(c):
    nc = c.nc
    ctx, sb, ps, sem = stage_scope(c)
    with ctx:
        bank = [ps(f"bank{n}") for n in range(4)]
        tg = sb("tg", [P, 1])
        ready, copied, gated, done = sem("ready"), sem("copied"), sem("gated"), sem("done")
        block = ctx.enter_context(nc.Block())

        @block.tensor
        def _(pe):
            for h in range(HEADS):
                ins = nc.tensor.matmul(bank[h // 4][:, (h % 4) * P:(h % 4) * P + P], c.w["x0_k"][:, h, :], c.w["x0_q"][:, h, :],
                                       start=True, stop=True)
                if h % 4 == 3:
                    ins.then_inc(ready, 1)

        @block.scalar
        def _(act):
            nc.scalar.activation(tg[:, :], c.w["x0_gate"][:, :], ACT.Tanh).then_inc(gated, 1)
            for n in range(4):
                act.wait_ge(ready, n + 1)
                nc.scalar.activation(c.x0_a[:, 4 * n:4 * n + 4, :], bank[n][:, :].rearrange("p (h d) -> p h d", h=4),
                                     ACT.Copy).then_inc(copied, 1)

        @block.vector
        def _(dve):
            dve.wait_ge(gated, 1)
            nc.vector.tensor_scalar(c.x0_o[:, :, :], c.w["x0_out"][:, :, :], tg[:, 0:1], None, ALU.mult).then_inc(done, 1)
            nc.vector.tensor_scalar(c.x0_b[:, :], c.w["x0_bias"][:, :], tg[0:1, 0:1], None, ALU.mult).then_inc(done, 1)


def cross_attention_wide(c):
    nc, B = c.nc, c.B
    K = c.keys
    DH = 64
    PAIRS = HEADS // 2
    ctx, sb, ps, sem = stage_scope(c)
    with ctx:
        cx = sb("cx", [P, 2, K])
        xn = sb("xn", [P, 2, D])
        xT = sb("xT", [P, 2, P])
        uu = sb("uu", [P, 2, HEADS, K])
        v = sb("v", [K, UNROLL, HEADS * DH])
        nmax = sb("nmax", [P, HEADS])
        d = sb("d", [P, 2, HEADS, K])
        e = sb("e", [P, 2, HEADS, K])
        z, rz = sb("z", [P, HEADS]), sb("rz", [P, HEADS])
        p = sb("p", [P, 2, HEADS, K])
        pT = sb("pT", [K, 2, HEADS, P])
        oT = sb("oT", [P, 2, PAIRS, P])

        ps_misc, ps_o = ps("ps_misc"), ps("ps_o")
        ps_x, ps_y = ps_misc[:, 0:P], ps_misc[:, P:2 * P]
        ps_u = [ps(f"ps_u{i}") for i in range(2)]
        ps_n = [ps(f"ps_n{i}") for i in range(2)]
        ps_t = [ps(f"ps_t{i}") for i in range(2)]

        names = ("xn_ready", "xT_ps", "xT_ready", "u_ps", "u_ready", "v_ps", "v_ready", "s_ps", "max_done", "d_ready",
                 "exp_done", "z_done", "rz_done", "p_ready", "pT_ps", "pT_ready", "o_ps", "oT_ready", "y_ps", "x_done", "cx_ready")
        (xn_ready, xT_ps, xT_ready, u_ps, u_ready, v_ps, v_ready, s_ps, max_done, d_ready,
         exp_done, z_done, rz_done, p_ready, pT_ps, pT_ready, o_ps, oT_ready, y_ps, x_done, cx_ready) = (sem(n) for n in names)
        block = ctx.enter_context(nc.Block())
        LAG = 5

        def four(t, g):
            return t[:, 4 * g:4 * g + 4]

        def bank_heads(bank, rows=P, cols=K):
            return bank[0:rows, 0:4 * cols].rearrange("p (h k) -> p h k", h=4)

        @block.tensor
        def _(pe):
            def values_of(at, half):
                s, u = at
                if half == 0:
                    pe.wait_ge(pT_ready, (s + 1) * 4)
                    pe.wait_ge(v_ready, 2 * (s + 1))
                wait(pe, oT_ready, 2 * s + half)
                for n in range(PAIRS // 2):
                    for odd in range(2):
                        h = half * PAIRS + 2 * n + odd
                        ins = nc.tensor.matmul(ps_o[DH * odd:DH * odd + DH, n * P:n * P + P], v[:, u, h * DH:h * DH + DH],
                                               pT[:, u % 2, h, :], start=True, stop=True)
                ins.then_inc(o_ps, 1)

            def slot(sl):
                if at := sl.step(4):
                    values_of(at, 0)
                if at := sl.step(2):
                    s, u = at
                    pe.wait_ge(xT_ready, s + 1)
                    pe.wait_ge(u_ready, 4 * (s + 1))
                    for g in range(4):
                        wait(pe, d_ready, 4 * s + g - 1)
                        nc.tensor.matmul(ps_n[g % 2][:, 0:4 * K], xT[:, u % 2, :], four(uu[:, u % 2], g),
                                         start=True, stop=True).then_inc(s_ps, 1)
                if at := sl.step(4):
                    values_of(at, 1)
                if at := sl.step(1):
                    s, u = at
                    pe.wait_ge(xn_ready, s + 1)
                    wait(pe, x_done, s - 4)
                    nc.tensor.transpose(ps_x, xn[:, u % 2, :], c.ident[:, :]).then_inc(xT_ps, 1)
                if at := sl.step(3):
                    s, u = at
                    pe.wait_ge(p_ready, s + 1)
                    for g in range(4):
                        wait(pe, pT_ready, 4 * s + g - 1)
                        for n in range(4):
                            ins = nc.tensor.transpose(ps_t[g % 2][0:K, n * P:n * P + P], p[:, u % 2, 4 * g + n, :], c.ident[:, :])
                        ins.then_inc(pT_ps, 1)
                if at := sl.step(5):
                    s, u = at
                    pe.wait_ge(oT_ready, 2 * (s + 1))
                    wait(pe, xT_ready, min(s + 5, B) if sl.fixed else s + 5)
                    wait(pe, x_done, s)
                    nc.tensor.matmul(ps_y, c.ones_row[0:1, 0:P], c.x0_b[0:1, :], start=True, stop=False)
                    for n in range(PAIRS):
                        ins = nc.tensor.matmul(ps_y, oT[:, u % 2, n, :], c.x0_o[:, n, :], start=False, stop=n == PAIRS - 1)
                    ins.then_inc(y_ps, 1)
                if at := sl.step(1):
                    s, u = at
                    pe.wait_ge(cx_ready, s + 1)
                    for g in range(4):
                        if g < 2:
                            wait(pe, v_ready, 2 * s - 1 + g)
                        else:
                            pe.wait_ge(u_ready, 4 * s + g - 1)
                        for n in range(4):
                            ins = nc.tensor.matmul(ps_u[g % 2][:, n * K:n * K + K], c.x0_a[:, 4 * g + n, :], cx[:, u % 2, :],
                                                   start=True, stop=True)
                        ins.then_inc(u_ps, 1)
                    for half in range(2):
                        pe.wait_ge(u_ready, 4 * s + 3 + half)
                        nc.tensor.matmul(ps_u[half][0:K, :], cx[:, u % 2, :], c.w["x0_v"][:, half * 512:half * 512 + 512],
                                         start=True, stop=True).then_inc(v_ps, 1)

            run_slots(pe, slot, B, LAG)

        @block.scalar
        def _(act):
            def outputs(at, half):
                s, u = at
                act.wait_ge(o_ps, 2 * s + half + 1)
                if half == 0:
                    wait(act, y_ps, s - 1)
                nc.scalar.activation(oT[:, u % 2, 4 * half:4 * half + 4, :], ps_o[:, :].rearrange("p (n q) -> p n q", n=4),
                                     ACT.Copy).then_inc(oT_ready, 1)

            def slot(sl):
                if at := sl.step(4):
                    outputs(at, 0)
                if at := sl.step(4):
                    outputs(at, 1)
                if at := sl.step(1):
                    s, u = at
                    act.wait_ge(xT_ps, s + 1)
                    nc.scalar.activation(xT[:, u % 2, :], ps_x, ACT.Identity, scale=c.w["x0_ln"][:, 0:1],
                                         bias=c.w["x0_ln"][:, 1:2]).then_inc(xT_ready, 1)
                if at := sl.step(2):
                    s, u = at
                    act.wait_ge(d_ready, 4 * (s + 1))
                    nc.scalar.activation(e[:, u % 2, :, :], d[:, u % 2, :, :], ACT.Exp, scale=DH ** -0.5).then_inc(exp_done, 1)
                if at := sl.step(3):
                    s, u = at
                    for g in range(4):
                        act.wait_ge(pT_ps, 4 * s + g + 1)
                        nc.scalar.activation(four(pT[:, u % 2], g), bank_heads(ps_t[g % 2], K, P), ACT.Copy).then_inc(pT_ready, 1)
                if at := sl.step(1):
                    s, u = at
                    for half in range(2):
                        act.wait_ge(v_ps, 2 * s + half + 1)
                        nc.scalar.activation(v[:, u, half * 512:half * 512 + 512], ps_u[half][0:K, :], ACT.Copy).then_inc(v_ready, 1)

            run_slots(act, slot, B, LAG)

        @block.gpsimd
        def _(pool):
            def slot(sl):
                if at := sl.step(0):
                    s, u = at
                    wait(pool, v_ps, 2 * (s - 1))
                    nc.gpsimd.tensor_copy(cx[:, u % 2, :], c.ctx[:, s, :]).then_inc(cx_ready, 1)
                if at := sl.step(2):
                    s, u = at
                    pool.wait_ge(rz_done, s + 1)
                    wait(pool, pT_ps, 4 * (s - 1))
                    nc.gpsimd.tensor_tensor(p[:, u % 2, :, :], e[:, u % 2, :, :], rz[:, :].unsqueeze(2).broadcast_to([P, HEADS, K]),
                                            ALU.mult).then_inc(p_ready, 1)

            run_slots(pool, slot, B, LAG)

        @block.vector
        def _(dve):
            def slot(sl):
                if at := sl.step(0):
                    s, u = at
                    wait(dve, xT_ps, s - 1)
                    nc.vector.tensor_scalar(xn[:, u % 2, :], c.x[:, s, :], c.mean[:, bass.ds(s, 1)], c.rstd[:, bass.ds(s, 1)],
                                            ALU.subtract, ALU.mult).then_inc(xn_ready, 1)
                if at := sl.step(2):
                    s, u = at
                    for g in range(4):
                        dve.wait_ge(s_ps, 4 * s + g + 1)
                        nc.vector.tensor_reduce(four(nmax, g), bank_heads(ps_n[g % 2]), AX.X, ALU.max).then_inc(max_done, 1)
                        dve.wait_ge(max_done, 4 * s + g + 1)
                        nc.vector.tensor_tensor(four(d[:, u % 2], g), bank_heads(ps_n[g % 2]),
                                                four(nmax, g).unsqueeze(2).broadcast_to([P, 4, K]),
                                                ALU.subtract).then_inc(d_ready, 1)
                if at := sl.step(5):
                    s, u = at
                    dve.wait_ge(y_ps, s + 1)
                    nc.vector.tensor_tensor(c.x[:, s, :], c.x[:, s, :], ps_y, ALU.add).then_inc(x_done, 1)
                    dve.wait_ge(x_done, s + 1)
                    nc.vector.bn_stats(c.stats[:, s, :], c.x[:, s, :])
                if at := sl.step(1):
                    s, u = at
                    for g in range(4):
                        dve.wait_ge(u_ps, 4 * s + g + 1)
                        nc.vector.tensor_copy(four(uu[:, u % 2], g), bank_heads(ps_u[g % 2])).then_inc(u_ready, 1)
                if at := sl.step(2):
                    s, u = at
                    dve.wait_ge(exp_done, s + 1)
                    nc.vector.tensor_reduce(z[:, :], e[:, u % 2, :, :], AX.X, ALU.add).then_inc(z_done, 1)
                    dve.wait_ge(z_done, s + 1)
                    wait(dve, p_ready, s)
                    nc.vector.reciprocal(rz[:, :], z[:, :]).then_inc(rz_done, 1)

            run_slots(dve, slot, B, LAG)


def top_two(c, dve, own, base, score, sel, gt, ge, rank, tri, out):
    nc = c.nc
    T, E = score.shape[1], score.shape[2]
    other = score.unsqueeze(2).broadcast_to([P, T, E, E])
    mine = score.unsqueeze(3).broadcast_to([P, T, E, E])
    behind, ahead = (tri[:, n, :, :].unsqueeze(1).broadcast_to([P, T, E, E]) for n in range(2))
    nc.vector.tensor_tensor(gt, other, mine, ALU.is_gt)
    nc.vector.tensor_tensor(ge, other, mine, ALU.is_ge).then_inc(own, 1)
    dve.wait_ge(own, base + 1)
    nc.vector.tensor_tensor(gt, gt, behind, ALU.mult)
    nc.vector.tensor_tensor(ge, ge, ahead, ALU.mult).then_inc(own, 1)
    dve.wait_ge(own, base + 2)
    nc.vector.tensor_tensor(gt, gt, ge, ALU.add).then_inc(own, 1)
    dve.wait_ge(own, base + 3)
    nc.vector.tensor_reduce(rank, gt, AX.X, ALU.add).then_inc(own, 1)
    dve.wait_ge(own, base + 4)
    return nc.vector.scalar_tensor_tensor(out=out, in0=rank, scalar=2.0, in1=sel, op0=ALU.is_lt, op1=ALU.mult)


def scored_experts(c):
    nc = c.nc
    T = 4
    N = T * P
    steps = c.B // T
    E, H = 8, 352
    CH = [P, P, H - 2 * P]
    ctx, sb, ps, sem = stage_scope(c)
    with ctx:
        w_hi = [sb(f"w{n}_hi", [D, E * H], F32R) for n in range(2)]
        w_lo = [sb(f"w{n}_lo", [D, E * H], F32R) for n in range(2)]
        w3 = sb("w3", [P, E, 3, D])
        raw_in, w3_in, split_hi, split_lo = sem("raw_in0"), sem("w3_in"), sem("split_hi"), sem("split_lo")
        raw_in2 = sem("raw_in1")
        with nc.sbuf_tensor("f0_raw", [D, 2, E * H], F32) as raw, nc.Block() as block:
            @block.sync
            def _(sp):
                for n, (name, arrived) in enumerate((("late_f0_1", raw_in), ("late_f0_2", raw_in2))):
                    sp.dma_start(raw[:, n, :], c.inp[name]).then_inc(arrived, 16)
                sp.dma_start(w3[:, :, :, :], c.inp["late_f0_3"]).then_inc(w3_in, 16)
                sp.wait_ge(w3_in, 16)

            @block.scalar
            def _(act):
                for n, arrived in enumerate((raw_in, raw_in2)):
                    act.wait_ge(arrived, 16)
                    nc.scalar.activation(w_hi[n][:, :], raw[:, n, :], ACT.Copy).then_inc(split_hi, 1)

            @block.vector
            def _(dve):
                for n in range(2):
                    dve.wait_ge(split_hi, n + 1)
                    nc.vector.tensor_tensor(w_lo[n][:, :], raw[:, n, :], w_hi[n][:, :].bitcast(F32), ALU.subtract).then_inc(split_lo, 1)
                dve.wait_ge(split_lo, 2)

        xn = sb("xn", [P, 2, T, D])
        xT = sb("xT", [D, N])
        x_hi, x_lo = sb("x_hi", [D, 2, N], F32R), sb("x_lo", [D, 2, N], F32R)
        sg = sb("sg", [P, 2, N])
        act_in = sb("act", [P, 2, 3, N])
        sc, rank, wt = sb("sc", [P, T, E]), sb("rank", [P, T, E]), sb("wt", [P, 2, T, E])
        gt, ge = sb("gt", [P, T, E, E]), sb("ge", [P, T, E, E])

        ps_g, ps_u, ps_y = ([ps(f"ps_{n}{i}") for i in range(2)] for n in "guy")
        ps_x, ps_r = ps("ps_x"), ps("ps_r")
        names = ("xn_ready", "xT_ps", "xT_ready", "hi_ready", "lo_ready", "r_ps", "sc_ready", "own", "w_ready",
                 "g_ps", "u_ps", "sg_ready", "act_ready", "y_ps", "y_taken", "stats_done")
        (xn_ready, xT_ps, xT_ready, hi_ready, lo_ready, r_ps, sc_ready, own, w_ready,
         g_ps, u_ps, sg_ready, act_ready, y_ps, y_taken, stats_done) = (sem(n) for n in names)
        block = ctx.enter_context(nc.Block())
        LAG, TURN = 2, 4
        NCH = 3 * E
        x4 = c.x[:, :, :].rearrange("p (s i) d -> p s i d", i=T)
        st4 = c.stats[:, :, :].rearrange("p (s i) k -> p s i k", i=T)
        mean4 = c.mean[:, :].rearrange("p (s i) -> p s i", i=T)
        rstd4 = c.rstd[:, :].rearrange("p (s i) -> p s i", i=T)

        @block.tensor
        def _(pe):
            def hidden(at, e):
                s, u = at
                if e == 0:
                    pe.wait_ge(hi_ready, s + 1)
                    pe.wait_ge(lo_ready, s + 1)
                for k, m in enumerate(CH):
                    n = 3 * e + k
                    cols = slice(e * H + k * P, e * H + k * P + m)
                    for w, bank, taken, ready in ((0, ps_g, sg_ready, g_ps), (1, ps_u, act_ready, u_ps)):
                        wait(pe, taken, s * NCH + n - 1)
                        out = bank[n % 2][0:m, :]
                        nc.tensor.matmul(out, w_hi[w][:, cols], x_hi[:, u % 2, :], start=True, stop=False)
                        nc.tensor.matmul(out, w_hi[w][:, cols], x_lo[:, u % 2, :], start=False, stop=False)
                        nc.tensor.matmul(out, w_lo[w][:, cols], x_hi[:, u % 2, :], start=False, stop=True).then_inc(ready, 1)

            def down(at, e):
                s, u = at
                pe.wait_ge(act_ready, s * NCH + 3 * e + 3)
                wait(pe, y_taken, s * E + e - 1)
                for i in range(T):
                    for k, m in enumerate(CH):
                        ins = nc.tensor.matmul(ps_y[e % 2][:, i * P:i * P + P], act_in[0:m, e % 2, k, i * P:i * P + P],
                                               w3[0:m, e, k, :], start=k == 0, stop=k == 2)
                ins.then_inc(y_ps, 1)

            def transposes(at):
                s, u = at
                pe.wait_ge(xn_ready, s + 1)
                wait(pe, lo_ready, s)
                for i in range(T):
                    ins = nc.tensor.transpose(ps_x[:, i * P:i * P + P], xn[:, u % 2, i, :], c.ident[:, :])
                ins.then_inc(xT_ps, 1)

            def router(at):
                s, u = at
                pe.wait_ge(xT_ready, s + 1)
                wait(pe, sc_ready, s)
                for i in range(T):
                    ins = nc.tensor.matmul(ps_r[:, i * E:i * E + E], xT[:, i * P:i * P + P], c.w["f0_router"][:, :],
                                           start=True, stop=True)
                ins.then_inc(r_ps, 1)

            def slot(sl):
                main, ahead = sl.step(2), sl.step(1)
                for e in range(E):
                    if main:
                        hidden(main, e)
                        if e:
                            down(main, e - 1)
                    if ahead and e == TURN:
                        transposes(ahead)
                    if ahead and e == TURN + 2:
                        router(ahead)
                if main:
                    down(main, E - 1)

            run_slots(pe, slot, steps, LAG, 2)

        @block.scalar
        def _(act):
            def slot(sl):
                main, ahead = sl.step(2), sl.step(1)
                for e in range(E):
                    if main:
                        s, u = main
                        for k, m in enumerate(CH):
                            n = 3 * e + k
                            act.wait_ge(g_ps, s * NCH + n + 1)
                            wait(act, act_ready, s * NCH + n - 1)
                            nc.scalar.activation(sg[0:m, n % 2, :], ps_g[n % 2][0:m, :], ACT.Silu).then_inc(sg_ready, 1)
                    if ahead and e == TURN:
                        s, u = ahead
                        act.wait_ge(xT_ps, s + 1)
                        wait(act, r_ps, s)
                        nc.scalar.activation(xT[:, :], ps_x[:, :], ACT.Copy).then_inc(xT_ready, 1)
                        nc.scalar.activation(x_hi[:, u % 2, :], ps_x[:, :], ACT.Copy).then_inc(hi_ready, 1)

            run_slots(act, slot, steps, LAG, 2)

        @block.vector
        def _(dve):
            def add(at, e):
                s, u = at
                dve.wait_ge(y_ps, s * E + e + 1)
                wait(dve, y_taken, s * E + e)
                for i in range(T):
                    ins = nc.vector.scalar_tensor_tensor(out=x4[:, s, i, :], in0=ps_y[e % 2][:, i * P:i * P + P],
                                                         scalar=wt[:, u % 2, i, e:e + 1], in1=x4[:, s, i, :],
                                                         op0=ALU.mult, op1=ALU.add)
                ins.then_inc(y_taken, 1)

            def slot(sl):
                if at := sl.step(0):
                    s, u = at
                    wait(dve, xT_ps, s - 1)
                    for i in range(T):
                        ins = nc.vector.tensor_scalar(xn[:, u % 2, i, :], x4[:, s, i, :], mean4[:, s, i:i + 1], rstd4[:, s, i:i + 1],
                                                      ALU.subtract, ALU.mult)
                    ins.then_inc(xn_ready, 1)
                main, ahead = sl.step(2), sl.step(1)
                for e in range(E):
                    if main:
                        s, u = main
                        if e == 0:
                            dve.wait_ge(w_ready, s + 1)
                        for k, m in enumerate(CH):
                            n = 3 * e + k
                            dve.wait_ge(sg_ready, s * NCH + n + 1)
                            dve.wait_ge(u_ps, s * NCH + n + 1)
                            if k == 0:
                                wait(dve, y_ps, s * E + e - 1)
                            nc.vector.tensor_tensor(act_in[0:m, e % 2, k, :], sg[0:m, n % 2, :], ps_u[n % 2][0:m, :],
                                                    ALU.mult).then_inc(act_ready, 1)
                        if e:
                            add(main, e - 1)
                    if ahead and e == TURN:
                        s, u = ahead
                        dve.wait_ge(hi_ready, s + 1)
                        nc.vector.tensor_tensor(x_lo[:, u % 2, :], ps_x[:, :], x_hi[:, u % 2, :].bitcast(F32),
                                                ALU.subtract).then_inc(lo_ready, 1)
                    if ahead and e == TURN + 2:
                        s, u = ahead
                        dve.wait_ge(r_ps, s + 1)
                        nc.vector.tensor_copy(sc[:, :, :], ps_r[:, 0:T * E].rearrange("p (i e) -> p i e", i=T)).then_inc(sc_ready, 1)
                        dve.wait_ge(sc_ready, s + 1)
                        top_two(c, dve, own, 4 * s, sc[:, :, :], sc[:, :, :], gt[:, :, :, :], ge[:, :, :, :], rank[:, :, :],
                                c.w["tri8"][:, :, :, :], wt[:, u % 2, :, :]).then_inc(w_ready, 1)
                if main:
                    add(main, E - 1)
                    s, u = main
                    dve.wait_ge(y_taken, (s + 1) * E)
                    for i in range(T):
                        nc.vector.bn_stats(st4[:, s, i, :], x4[:, s, i, :])

            run_slots(dve, slot, steps, LAG, 2)


def attention_over_heads(c):
    nc, B = c.nc, c.B
    A = P // HEADS
    ctx, sb, ps, sem = stage_scope(c)
    with ctx:
        xn, xT = sb("xn", [P, 2, D]), sb("xT", [P, P])
        qkv = sb("qkv", [P, UNROLL, 3, HEADS, HD])
        qk = sb("qk", [P, 2, HEADS, HEADS, HD])
        sc, top, dif = sb("sc", [P, HEADS, HEADS]), sb("top", [P, HEADS]), sb("dif", [P, 2, HEADS, HEADS])
        e = sb("e", [P, 2, HEADS, HEADS])
        z, rz = sb("z", [P, HEADS]), sb("rz", [P, HEADS])
        ev = sb("ev", [P, HEADS, HD, HEADS])
        sums, o = sb("sums", [P, HEADS, HD]), sb("o", [P, 2, HEADS, HD])
        r = sb("r", [P, 2, HD, HEADS, A])
        ps_x, ps_qkv, ps_y = ps("ps_x"), ps("ps_qkv"), ps("ps_y")
        names = ("xn_ready", "xT_ps", "xT_ready", "qkv_ps", "qkv_ready", "qk_ready", "sc_done", "top_done", "dif_ready", "exp_done",
                 "z_done", "rz_done", "ev_done", "sums_done", "o_ready", "r_ready", "y_ps", "x_done")
        (xn_ready, xT_ps, xT_ready, qkv_ps, qkv_ready, qk_ready, sc_done, top_done, dif_ready, exp_done,
         z_done, rz_done, ev_done, sums_done, o_ready, r_ready, y_ps, x_done) = (sem(n) for n in names)
        block = ctx.enter_context(nc.Block())
        LAG = 4
        full = [P, HEADS, HEADS, HD]

        @block.tensor
        def _(pe):
            def slot(sl):
                if at := sl.step(1):
                    s, u = at
                    pe.wait_ge(xn_ready, s + 1)
                    wait(pe, xT_ready, s)
                    nc.tensor.transpose(ps_x[:, 0:P], xn[:, u % 2, :], c.ident[:, :]).then_inc(xT_ps, 1)
                    pe.wait_ge(xT_ready, s + 1)
                    wait(pe, qkv_ready, s)
                    nc.tensor.matmul(ps_qkv[:, 0:3 * D], xT[:, :], c.w["a1_qkv"][:, :], start=True, stop=True).then_inc(qkv_ps, 1)
                if at := sl.step(4):
                    s, u = at
                    pe.wait_ge(r_ready, s + 1)
                    wait(pe, x_done, s)
                    nc.tensor.matmul(ps_y[:, 0:D], c.ones_row[0:1, 0:P], c.w["a1_b"][0:1, :], start=True, stop=False)
                    for k in range(HD):
                        ins = nc.tensor.matmul(ps_y[:, 0:D], r[:, u % 2, k, :, :], c.w["a1_o"][:, k, :], start=False, stop=k == HD - 1)
                    ins.then_inc(y_ps, 1)

            run_slots(pe, slot, B, LAG)

        @block.scalar
        def _(act):
            def slot(sl):
                if at := sl.step(1):
                    s, u = at
                    act.wait_ge(xT_ps, s + 1)
                    nc.scalar.activation(xT[:, :], ps_x[:, 0:P], ACT.Copy).then_inc(xT_ready, 1)
                    act.wait_ge(qkv_ps, s + 1)
                    wait(act, ev_done, s - 3)
                    nc.scalar.activation(qkv[:, u, :, :, :], ps_qkv[:, 0:3 * D].rearrange("p (n h d) -> p n h d", n=3, h=HEADS),
                                         ACT.Copy).then_inc(qkv_ready, 1)
                if at := sl.step(2):
                    s, u = at
                    act.wait_ge(dif_ready, s + 1)
                    wait(act, ev_done, s - 1)
                    nc.scalar.activation(e[:, u % 2, :, :], dif[:, u % 2, :, :], ACT.Exp, scale=HD ** -0.5).then_inc(exp_done, 1)
                if at := sl.step(3):
                    s, u = at
                    act.wait_ge(o_ready, s + 1)
                    wait(act, y_ps, s - 1)
                    for a in range(A):
                        ins = nc.scalar.activation(r[:, u % 2, :, :, a], o[:, u % 2, :, :].rearrange("p h d -> p d h"), ACT.Copy,
                                                   scale=c.w["a1_rows"][:, a:a + 1])
                    ins.then_inc(r_ready, 1)

            run_slots(act, slot, B, LAG)

        @block.gpsimd
        def _(pool):
            def slot(sl):
                if at := sl.step(1):
                    s, u = at
                    pool.wait_ge(qkv_ready, s + 1)
                    wait(pool, sc_done, s - 1)
                    nc.gpsimd.tensor_tensor(qk[:, u % 2, :, :, :], qkv[:, u, 0, :, :].unsqueeze(2).broadcast_to(full),
                                            qkv[:, u, 1, :, :].unsqueeze(1).broadcast_to(full), ALU.mult).then_inc(qk_ready, 1)

            run_slots(pool, slot, B, LAG)

        @block.vector
        def _(dve):
            def slot(sl):
                if at := sl.step(0):
                    s, u = at
                    wait(dve, xT_ps, s - 1)
                    nc.vector.tensor_scalar(xn[:, u % 2, :], c.x[:, s, :], c.mean[:, bass.ds(s, 1)], c.rstd[:, bass.ds(s, 1)],
                                            ALU.subtract, ALU.mult).then_inc(xn_ready, 1)
                if at := sl.step(2):
                    s, u = at
                    dve.wait_ge(qk_ready, s + 1)
                    wait(dve, dif_ready, s)
                    nc.vector.tensor_reduce(sc[:, :, :], qk[:, u % 2, :, :, :], AX.X, ALU.add).then_inc(sc_done, 1)
                    dve.wait_ge(sc_done, s + 1)
                    nc.vector.tensor_reduce(top[:, :], sc[:, :, :], AX.X, ALU.max).then_inc(top_done, 1)
                    dve.wait_ge(top_done, s + 1)
                    wait(dve, exp_done, s - 1)
                    nc.vector.tensor_tensor(dif[:, u % 2, :, :], sc[:, :, :], top[:, :].unsqueeze(2).broadcast_to([P, HEADS, HEADS]),
                                            ALU.subtract).then_inc(dif_ready, 1)
                if at := sl.step(3):
                    s, u = at
                    dve.wait_ge(exp_done, s + 1)
                    wait(dve, o_ready, s)
                    nc.vector.tensor_reduce(z[:, :], e[:, u % 2, :, :], AX.X, ALU.add).then_inc(z_done, 1)
                    nc.vector.tensor_tensor(ev[:, :, :, :], e[:, u % 2, :, :].unsqueeze(2).broadcast_to([P, HEADS, HD, HEADS]),
                                            qkv[:, u, 2, :, :].rearrange("p h d -> p d h").unsqueeze(1).broadcast_to([P, HEADS, HD, HEADS]),
                                            ALU.mult).then_inc(ev_done, 1)
                    dve.wait_ge(z_done, s + 1)
                    nc.vector.reciprocal(rz[:, :], z[:, :]).then_inc(rz_done, 1)
                    dve.wait_ge(ev_done, s + 1)
                    nc.vector.tensor_reduce(sums[:, :, :], ev[:, :, :, :], AX.X, ALU.add).then_inc(sums_done, 1)
                    dve.wait_ge(rz_done, s + 1)
                    dve.wait_ge(sums_done, s + 1)
                    wait(dve, r_ready, s - 1)
                    nc.vector.tensor_tensor(o[:, u % 2, :, :], sums[:, :, :], rz[:, :].unsqueeze(2).broadcast_to([P, HEADS, HD]),
                                            ALU.mult).then_inc(o_ready, 1)
                if at := sl.step(4):
                    s, u = at
                    dve.wait_ge(y_ps, s + 1)
                    nc.vector.tensor_tensor(c.x[:, s, :], c.x[:, s, :], ps_y[:, 0:D], ALU.add).then_inc(x_done, 1)
                    dve.wait_ge(x_done, s + 1)
                    nc.vector.bn_stats(c.stats[:, s, :], c.x[:, s, :])

            run_slots(dve, slot, B, LAG)


def cross_attention_tempered(c):
    B = c.B
    c.stage = "x1"
    ctx, sb, ps, sem = stage_scope(c)
    with ctx:
        c.t_max, c.t_z, c.t_sq = (sb(n, [P, B, HEADS]) for n in ("t_max", "t_z", "t_sq"))
        c.t_q, c.t_k = sb("t_q", [P, B]), sb("t_k", [P, B])
        c.t_g, c.t_qb = sb("t_g", [P, B]), sb("t_qb", [P, B])
        c.stage = "x1s"
        tempered_pass(c, False)
        c.stage = "x1t"
        temperatures(c)
        c.stage = "x1a"
        tempered_pass(c, True)


def temperatures(c):
    nc, B = c.nc, c.B
    N = B * HEADS
    COLS = min(N, 512)
    parts = N // COLS
    H = c.w["x1_w2"].shape[0]
    ctx, sb, ps, sem = stage_scope(c)
    with ctx:
        z2, rec, ent, prod = sb("z2", [P, N]), sb("rec", [P, N]), sb("ent", [P, N]), sb("prod", [P, B])
        sims = sb("sims", [P, B, HEADS])
        feats = sb("feats", [3, N])
        h1, h2 = sb("h1", [H, N]), sb("h2", [H, N])
        own_t = sb("own_t", [P, B, HEADS])
        lt, t = sb("lt", [P, B]), sb("t", [P, B])
        bank = [ps(f"bank{n}") for n in range(parts)]
        last = [ps(f"last{n}") for n in range(parts)]
        dv, in_ready, f_ps, f_ready, h_ps, h_ready, t_ps, lt_ready, t_ready = (
            sem(n) for n in ("dv", "in_ready", "f_ps", "f_ready", "h_ps", "h_ready", "t_ps", "lt_ready", "t_ready"))
        block = ctx.enter_context(nc.Block())
        flat = lambda tile: tile[:, :, :].rearrange("p b h -> p (b h)")
        head_mask = c.w["x1_heads"][:, :].unsqueeze(1).broadcast_to([P, B, HEADS])
        cols = lambda n: slice(n * COLS, n * COLS + COLS)

        @block.vector
        def _(dve):
            n_own = [0]

            def own(ins):
                n_own[0] += 1
                ins.then_inc(dv, 1)
                dve.wait_ge(dv, n_own[0])

            own(nc.vector.tensor_tensor(prod[:, :], c.t_q[:, :], c.t_k[:, :], ALU.mult))
            own(nc.vector.tensor_tensor(sims[:, :, :], prod[:, :].unsqueeze(2).broadcast_to([P, B, HEADS]), head_mask, ALU.mult))
            own(nc.vector.tensor_tensor(z2[:, :], flat(c.t_z), flat(c.t_z), ALU.mult))
            own(nc.vector.reciprocal(rec[:, :], z2[:, :]))
            nc.vector.tensor_tensor(ent[:, :], rec[:, :], flat(c.t_sq), ALU.mult).then_inc(in_ready, 1)
            for n in range(parts):
                dve.wait_ge(t_ps, n + 1)
                b = COLS // HEADS
                own(nc.vector.tensor_tensor(own_t[:, n * b:n * b + b, :], last[n][:, 0:COLS].rearrange("p (b h) -> p b h", h=HEADS),
                                            c.w["x1_heads"][:, :].unsqueeze(1).broadcast_to([P, b, HEADS]), ALU.mult))
            own(nc.vector.tensor_reduce(lt[:, :], own_t[:, :, :], AX.X, ALU.add))
            own(nc.vector.tensor_scalar(t[:, :], lt[:, :], c.w["x1_b3"][:, 0:1], float(np.log(0.1)), ALU.add, ALU.max))
            nc.vector.tensor_scalar(lt[:, :], t[:, :], float(np.log(10.0)), None, ALU.min).then_inc(lt_ready, 1)
            dve.wait_ge(t_ready, 1)
            own(nc.vector.tensor_scalar(lt[:, :], t[:, :], 2.0, None, ALU.mult))
            own(nc.vector.reciprocal(c.t_g[:, :], lt[:, :]))
            own(nc.vector.tensor_scalar(c.t_qb[:, :], c.t_g[:, :], c.w["x1_bias"][:, 0:1], None, ALU.mult))

        @block.tensor
        def _(pe):
            pe.wait_ge(in_ready, 1)
            for n in range(parts):
                for k, data in enumerate((flat(sims), flat(c.t_max), ent[:, :])):
                    nc.tensor.matmul(bank[n][0:3, 0:COLS], c.w["x1_pick"][:, 3 * k:3 * k + 3], data[:, cols(n)],
                                     start=k == 0, stop=False)
                nc.tensor.matmul(bank[n][0:3, 0:COLS], c.w["x1_less"][0:1, :], c.ones_row[0:1, 0:COLS],
                                 start=False, stop=True).then_inc(f_ps, 1)
            for layer, (wt, src, dst, ready) in enumerate((("x1_w1", feats, bank, f_ready), ("x1_w2", h1, bank, h_ready))):
                for n in range(parts):
                    pe.wait_ge(ready, parts if ready is f_ready else n + 1)
                    nc.tensor.matmul(dst[n][0:H, 0:COLS], c.w[wt][:, :], src[:, cols(n)], start=True, stop=True).then_inc(h_ps, 1)
            for n in range(parts):
                pe.wait_ge(h_ready, parts + n + 1)
                nc.tensor.matmul(last[n][:, 0:COLS], c.w["x1_w3"][:, :], h2[:, cols(n)], start=True, stop=True).then_inc(t_ps, 1)

        @block.scalar
        def _(act):
            for n in range(parts):
                act.wait_ge(f_ps, n + 1)
                nc.scalar.activation(feats[:, cols(n)], bank[n][0:3, 0:COLS], ACT.Copy).then_inc(f_ready, 1)
            for layer, (dst, col) in enumerate(((h1, 0), (h2, 1))):
                for n in range(parts):
                    act.wait_ge(h_ps, layer * parts + n + 1)
                    nc.scalar.activation(dst[:, cols(n)], bank[n][0:H, 0:COLS], ACT.Gelu,
                                         bias=c.w["x1_mlp_b"][:, col:col + 1]).then_inc(h_ready, 1)
            act.wait_ge(lt_ready, 1)
            nc.scalar.activation(t[:, :], lt[:, :], ACT.Exp).then_inc(t_ready, 1)


def tempered_pass(c, final):
    nc, B = c.nc, c.B
    K = c.keys
    ctx, sb, ps, sem = stage_scope(c)
    with ctx:
        cx = sb("cx", [P, UNROLL, K])
        xn = sb("xn", [P, 2, D])
        xT = sb("xT", [P, 2, P])
        qT, kT = sb("qT", [P, 2, P]), sb("kT", [P, 2, K])
        k_bd = sb("k_bd", [P, 2, GROUP, K])
        nmax = sb("nmax", [P, HEADS])
        d = sb("d", [P, 2, HEADS, K])
        e = sb("e", [P, 2, HEADS, K])
        sq = sb("sq", [P, 2, HEADS, K])
        if final:
            v_bd = sb("v_bd", [K, UNROLL, GROUPS, GROUP, STRIP])
            z, rz = sb("z", [P, HEADS]), sb("rz", [P, HEADS])
            pT = sb("pT", [K, 2, HEADS, P])
            oT = sb("oT", [P, 2, P])
        ps_x, ps_qk = ps("ps_x"), ps("ps_qk")
        ps_n = [ps(f"ps_n{i}") for i in range(2)]
        if final:
            ps_t = [ps(f"ps_t{i}") for i in range(2)]
            ps_o, ps_y = ps("ps_o"), ps("ps_y")
        names = ("xn_ready", "xT_ps", "xT_ready", "qk_ps", "qk_ready", "k_bd_ready", "made", "s_ps", "max_done", "d_ready",
                 "exp_done", "z_done", "rz_done", "sq_ready", "sq_done", "pT_ps", "pT_ready", "o_ps", "oT_ready", "y_ps",
                 "x_done", "cx_ready", "sums_done")
        (xn_ready, xT_ps, xT_ready, qk_ps, qk_ready, k_bd_ready, made, s_ps, max_done, d_ready,
         exp_done, z_done, rz_done, sq_ready, sq_done, pT_ps, pT_ready, o_ps, oT_ready, y_ps,
         x_done, cx_ready, sums_done) = (sem(n) for n in names)
        block = ctx.enter_context(nc.Block())
        EVAC = 3 if final else 2

        def strip(g):
            return slice(STRIP * g, STRIP * g + STRIP)

        def four(t, g):
            return t[:, 4 * g:4 * g + 4]

        def bank_heads(bank, rows=P, cols=K):
            return bank[0:rows, 0:4 * cols].rearrange("p (h k) -> p h k", h=4)

        TURN, PROJECT, SCORE, WEIGH, SPREAD, VALUE, LAST = 1, 2, 3, 4, 5, 6, 7
        LAG = LAST if final else SPREAD

        @block.tensor
        def _(pe):
            def scores(at, g):
                s, u = at
                if g == 0:
                    pe.wait_ge(k_bd_ready, s + 1)
                wait(pe, d_ready, 4 * s + g - 1)
                nc.tensor.matmul(ps_n[g % 2][:, 0:4 * K], qT[strip(g), u % 2, :], k_bd[strip(g), u % 2, :, :],
                                 start=True, stop=True).then_inc(s_ps, 1)

            def transposes(at, g):
                s, u = at
                if g == 0:
                    pe.wait_ge(sq_ready, s + 1)
                wait(pe, pT_ready, 4 * s + g - 1)
                for n in range(4):
                    ins = nc.tensor.transpose(ps_t[g % 2][0:K, n * P:n * P + P], sq[:, u % 2, 4 * g + n, :], c.ident[:, :])
                ins.then_inc(pT_ps, 1)

            def slot(sl):
                scored, spread = sl.step(SCORE), sl.step(SPREAD) if final else None
                if scored:
                    scores(scored, 0)
                    scores(scored, 1)
                if at := sl.step(PROJECT):
                    s, u = at
                    pe.wait_ge(cx_ready, s + 1)
                    pe.wait_ge(xT_ready, s + 1)
                    wait(pe, qk_ready, EVAC * s)
                    nc.tensor.matmul(ps_qk[:, 0:P], c.w["x1_q"][:, :], xT[:, u % 2, :], start=True, stop=True)
                    ins = nc.tensor.matmul(ps_qk[:, P:P + K], c.w["x1_k"][:, :], cx[:, u, :], start=True, stop=True)
                    if final:
                        nc.tensor.matmul(ps_qk[0:K, 3 * P:4 * P], c.ones_row[0:1, 0:K], c.w["x1_bv"][0:1, :], start=True, stop=False)
                        ins = nc.tensor.matmul(ps_qk[0:K, 3 * P:4 * P], cx[:, u, :], c.w["x1_v"][:, :], start=False, stop=True)
                    ins.then_inc(qk_ps, 1)
                if final and (at := sl.step(VALUE)):
                    s, u = at
                    pe.wait_ge(pT_ready, 4 * (s + 1))
                    pe.wait_ge(qk_ready, EVAC * (s + 1))
                    wait(pe, oT_ready, s)
                    for j in range(GROUP):
                        for g in range(GROUPS):
                            ins = nc.tensor.matmul(ps_o[strip(g), 0:P], v_bd[:, u, g, j, :], pT[:, u % 2, GROUP * g + j, :],
                                                   start=j == 0, stop=j == GROUP - 1)
                    ins.then_inc(o_ps, 1)
                if at := sl.step(TURN):
                    s, u = at
                    pe.wait_ge(xn_ready, s + 1)
                    wait(pe, xT_ready, s)
                    nc.tensor.transpose(ps_x[:, 0:P], xn[:, u % 2, :], c.ident[:, :]).then_inc(xT_ps, 1)
                if scored:
                    scores(scored, 2)
                if spread:
                    transposes(spread, 0)
                    transposes(spread, 1)
                if scored:
                    scores(scored, 3)
                if spread:
                    transposes(spread, 2)
                    transposes(spread, 3)
                if final and (at := sl.step(LAST)):
                    s, u = at
                    pe.wait_ge(oT_ready, s + 1)
                    wait(pe, x_done, s)
                    nc.tensor.matmul(ps_y[:, 0:D], c.ones_row[0:1, 0:P], c.w["x1_bo"][0:1, :], start=True, stop=False)
                    nc.tensor.matmul(ps_y[:, 0:D], oT[:, u % 2, :], c.w["x1_o"][:, :], start=False, stop=True).then_inc(y_ps, 1)

            run_slots(pe, slot, B, LAG)

        @block.scalar
        def _(act):
            if final:
                act.wait_ge(made, 1)

            def slot(sl):
                if at := sl.step(PROJECT):
                    s, u = at
                    act.wait_ge(qk_ps, s + 1)
                    wait(act, k_bd_ready, s - 1)
                    wait(act, s_ps, 4 * (s - 1))
                    if not final:
                        wait(act, sums_done, s - 1)
                    q_bias, q_scale = c.w["x1_bias"][:, 0:1], 1.0
                    if final:
                        q_bias, q_scale = c.t_qb[:, bass.ds(s, 1)], c.t_g[:, bass.ds(s, 1)]
                    nc.scalar.activation(qT[:, u % 2, :], ps_qk[:, 0:P], ACT.Identity, scale=q_scale, bias=q_bias).then_inc(qk_ready, 1)
                    nc.scalar.activation(kT[:, u % 2, :], ps_qk[:, P:P + K], ACT.Identity,
                                         bias=c.w["x1_bias"][:, 1:2]).then_inc(qk_ready, 1)
                    if final:
                        wait(act, o_ps, s - 3)
                        for j in range(GROUP):
                            at_j = slice(HD * j, HD * j + HD)
                            ins = nc.scalar.activation(v_bd[:, u, :, j, at_j],
                                                       ps_qk[0:K, 3 * P:4 * P].rearrange("p (g r) -> p g r", g=GROUPS)[:, :, at_j], ACT.Copy)
                        ins.then_inc(qk_ready, 1)
                if final and (at := sl.step(VALUE)):
                    s, u = at
                    act.wait_ge(o_ps, s + 1)
                    wait(act, y_ps, s - 1)
                    nc.scalar.activation(oT[:, u % 2, :], ps_o[:, 0:P], ACT.Copy).then_inc(oT_ready, 1)
                if at := sl.step(TURN):
                    s, u = at
                    act.wait_ge(xT_ps, s + 1)
                    wait(act, qk_ps, s - 1)
                    nc.scalar.activation(xT[:, u % 2, :], ps_x[:, 0:P], ACT.Copy).then_inc(xT_ready, 1)
                spread = sl.step(SPREAD) if final else None

                def transposed(groups):
                    s, u = spread
                    for g in groups:
                        act.wait_ge(pT_ps, 4 * s + g + 1)
                        nc.scalar.activation(four(pT[:, u % 2], g), bank_heads(ps_t[g % 2], K, P), ACT.Copy).then_inc(pT_ready, 1)

                if spread:
                    transposed(range(4))
                if at := sl.step(SCORE):
                    s, u = at
                    act.wait_ge(d_ready, 4 * (s + 1))
                    wait(act, sq_ready, s - 1)
                    nc.scalar.activation(e[:, u % 2, :, :], d[:, u % 2, :, :], ACT.Exp,
                                         scale=1.0 if final else HD ** -0.5).then_inc(exp_done, 1)

            run_slots(act, slot, B, LAG)

        @block.gpsimd
        def _(pool):
            if final:
                nc.gpsimd.memset(v_bd[:, :, :, :, :], 0.0).then_inc(made, 1)

            def slot(sl):
                if at := sl.step(PROJECT):
                    s, u = at
                    pool.wait_ge(qk_ready, EVAC * (s + 1))
                    wait(pool, s_ps, 4 * (s - 1))
                    nc.gpsimd.tensor_tensor(k_bd[:, u % 2, :, :], kT[:, u % 2, :].unsqueeze(1).broadcast_to([P, GROUP, K]),
                                            c.block[:, 0:GROUP].unsqueeze(2).broadcast_to([P, GROUP, K]),
                                            ALU.mult).then_inc(k_bd_ready, 1)
                if at := sl.step(0):
                    s, u = at
                    wait(pool, qk_ps, s - 3)
                    nc.gpsimd.tensor_copy(cx[:, u, :], c.ctx[:, s, :]).then_inc(cx_ready, 1)
                if at := sl.step(WEIGH):
                    s, u = at
                    pool.wait_ge(rz_done if final else exp_done, s + 1)
                    wait(pool, pT_ps if final else sq_done, 4 * (s - 1) if final else s - 1)
                    other = rz[:, :].unsqueeze(2).broadcast_to([P, HEADS, K]) if final else e[:, u % 2, :, :]
                    nc.gpsimd.tensor_tensor(sq[:, u % 2, :, :], e[:, u % 2, :, :], other, ALU.mult).then_inc(sq_ready, 1)

            run_slots(pool, slot, B, LAG)

        @block.vector
        def _(dve):
            def slot(sl):
                if at := sl.step(0):
                    s, u = at
                    wait(dve, xT_ps, s - 1)
                    nc.vector.tensor_scalar(xn[:, u % 2, :], c.x[:, s, :], c.mean[:, bass.ds(s, 1)], c.rstd[:, bass.ds(s, 1)],
                                            ALU.subtract, ALU.mult).then_inc(xn_ready, 1)
                scored = sl.step(SCORE)

                def differences(groups):
                    s, u = scored
                    top = nmax[:, :] if final else c.t_max[:, s, :]
                    for g in groups:
                        dve.wait_ge(s_ps, 4 * s + g + 1)
                        nc.vector.tensor_reduce(four(top, g), bank_heads(ps_n[g % 2]), AX.X, ALU.max).then_inc(max_done, 1)
                        dve.wait_ge(max_done, 4 * s + g + 1)
                        nc.vector.tensor_tensor(four(d[:, u % 2], g), bank_heads(ps_n[g % 2]),
                                                four(top, g).unsqueeze(2).broadcast_to([P, 4, K]),
                                                ALU.subtract).then_inc(d_ready, 1)

                if scored:
                    wait(dve, exp_done, scored[0] - 1)
                    differences((0, 1))
                if at := sl.step(WEIGH):
                    s, u = at
                    dve.wait_ge(exp_done, s + 1)
                    if final:
                        wait(dve, sq_ready, s)
                    nc.vector.tensor_reduce(z[:, :] if final else c.t_z[:, s, :], e[:, u % 2, :, :], AX.X, ALU.add).then_inc(z_done, 1)
                    if final:
                        dve.wait_ge(z_done, s + 1)
                        nc.vector.reciprocal(rz[:, :], z[:, :]).then_inc(rz_done, 1)
                if scored:
                    differences((2, 3))
                if final and (at := sl.step(LAST)):
                    s, u = at
                    dve.wait_ge(y_ps, s + 1)
                    nc.vector.tensor_tensor(c.x[:, s, :], c.x[:, s, :], ps_y[:, 0:D], ALU.add).then_inc(x_done, 1)
                    dve.wait_ge(x_done, s + 1)
                    nc.vector.bn_stats(c.stats[:, s, :], c.x[:, s, :])
                if not final and (at := sl.step(SPREAD)):
                    s, u = at
                    dve.wait_ge(sq_ready, s + 1)
                    nc.vector.tensor_reduce(c.t_sq[:, s, :], sq[:, u % 2, :, :], AX.X, ALU.add).then_inc(sq_done, 1)
                if not final and (at := sl.step(SCORE)):
                    s, u = at
                    dve.wait_ge(qk_ready, 2 * (s + 1))
                    nc.vector.tensor_reduce(c.t_q[:, bass.ds(s, 1)], qT[:, u % 2, :], AX.X, ALU.add)
                    nc.vector.tensor_reduce(c.t_k[:, bass.ds(s, 1)], kT[:, u % 2, :], AX.X, ALU.add).then_inc(sums_done, 1)

            run_slots(dve, slot, B, LAG)


T6 = 4


def mixed_experts(c):
    nc, B = c.nc, c.B
    c.stage = "f1"
    ctx, sb, ps, sem = stage_scope(c)
    with ctx:
        c.f1_xT = sb("xT", [D, B, P])
        c.f1_wt = sb("wt", [P, B, 4])
        c.f1 = {}
        late = [n for n in c.inp if n.startswith("late_f1_")]
        for name in late:
            c.f1[name[8:]] = sb(name, list(c.inp[name].shape))
        c.f1_me, c.f1_me_b = sb("me", [D, 2, D]), sb("me_b", [P, 2])
        c.f1_ce, c.f1_ce_b = sb("ce", [D, D]), sb("ce_b", [1, D])
        arrived = sem("arrived")
        with nc.Block() as block:
            @block.sync
            def _(sp):
                for name in late:
                    tile = c.f1[name[8:]]
                    sp.dma_start(tile[(slice(None),) * len(c.inp[name].shape)], c.inp[name]).then_inc(arrived, 16)
                sp.wait_ge(arrived, 16 * len(late))
        c.stage = "f1w"
        chain_weights(c)
        c.stage = "f1r"
        route(c)
        f = c.f1
        c.stage = "f1a"
        hidden_expert(c, 0, ACT.Silu, f["sw_1"][:, :, :], f["sw_3"], None, f["sw_2"], None)
        c.stage = "f1b"
        hidden_expert(c, 1, ACT.Gelu, c.f1_me[:, :, :], None, c.f1_me_b, f["c2"], f["c2b"])
        c.stage = "f1d"
        hidden_expert(c, 3, ACT.Gelu, f["ml_1"][:, :, :], None, f["ml_b1"], f["ml_2"], f["ml_b2"])
        c.stage = "f1c"
        normed_expert(c, 2)


def chain_weights(c):
    nc, f = c.nc, c.f1
    ctx, sb, ps, sem = stage_scope(c)
    with ctx:
        m1, m2, mo = sb("m1", [D, 2 * D]), sb("m2", [D, 2 * D]), sb("mo", [D, D])
        col1, col2 = sb("col1", [P, 1]), sb("col2", [P, 1])
        pm, pv, po, pb = ps("pm"), ps("pv"), ps("po"), ps("pb")
        m_ps, m_done, v_ps, v_done, o_ps, o_done, b_ps, b_done = (
            sem(n) for n in ("m_ps", "m_done", "v_ps", "v_done", "o_ps", "o_done", "b_ps", "b_done"))
        block = ctx.enter_context(nc.Block())
        c1 = f["c1"][:, :, :].rearrange("p n d -> p (n d)")
        me = c.f1_me[:, :, :].rearrange("p n d -> p (n d)")

        @block.tensor
        def _(pe):
            for n, (left, right) in enumerate((("me_oT", c1), ("me_vT", m1[:, :]), ("me_eqT", m2[:, :]))):
                wait(pe, m_done, n)
                nc.tensor.matmul(pm[:, 0:2 * D], f[left][:, :], right, start=True, stop=True).then_inc(m_ps, 1)
            for n, (left, right) in enumerate((("me_v", f["cols"][:, 0:1]), ("me_o", col1[:, :]))):
                wait(pe, v_done, n)
                nc.tensor.matmul(pv[:, n:n + 1], f[left][:, :], right, start=True, stop=True).then_inc(v_ps, 1)
            pe.wait_ge(v_done, 2)
            for n in range(2):
                nc.tensor.matmul(pv[:, 2 + n:3 + n], f["c1"][:, n, :], col2[:, :], start=True, stop=True).then_inc(v_ps, 1)
            nc.tensor.matmul(po[:, 0:D], f["ce_vT"][:, :], f["ce_o"][:, :], start=True, stop=True).then_inc(o_ps, 1)
            pe.wait_ge(o_done, 1)
            nc.tensor.matmul(po[:, 0:D], f["ce_synT"][:, :], mo[:, :], start=True, stop=True).then_inc(o_ps, 1)
            nc.tensor.matmul(pb[0:1, 0:D], f["cols"][:, 3:4], mo[:, :], start=True, stop=False)
            nc.tensor.matmul(pb[0:1, 0:D], f["cols"][:, 4:5], f["ce_o"][:, :], start=False, stop=False)
            nc.tensor.matmul(pb[0:1, 0:D], c.ones_row[0:1, 0:1], f["ce_bo"][0:1, :], start=False, stop=True).then_inc(b_ps, 1)

        @block.scalar
        def _(act):
            for n, out in enumerate((m1[:, :], m2[:, :], me)):
                act.wait_ge(m_ps, n + 1)
                nc.scalar.activation(out, pm[:, 0:2 * D], ACT.Copy).then_inc(m_done, 1)

        @block.vector
        def _(dve):
            for n, out in enumerate((col1, col2)):
                dve.wait_ge(v_ps, n + 1)
                nc.vector.tensor_tensor(out[:, :], pv[:, n:n + 1], f["cols"][:, 1 + n:2 + n], ALU.add).then_inc(v_done, 1)
            dve.wait_ge(v_ps, 4)
            nc.vector.tensor_tensor(c.f1_me_b[:, :], pv[:, 2:4], f["c1b"][:, :], ALU.add).then_inc(v_done, 1)
            dve.wait_ge(o_ps, 1)
            nc.vector.tensor_tensor(mo[:, :], po[:, 0:D], c.ident[:, :], ALU.add).then_inc(o_done, 1)
            dve.wait_ge(o_ps, 2)
            nc.vector.tensor_copy(c.f1_ce[:, :], po[:, 0:D]).then_inc(o_done, 1)
            dve.wait_ge(b_ps, 1)
            nc.vector.tensor_copy(c.f1_ce_b[:, :], pb[0:1, 0:D]).then_inc(b_done, 1)


def tiled(c, t):
    return t[:, :, :].rearrange("p (s i) d -> p s i d", i=T6)


def route(c):
    nc = c.nc
    T, E = T6, 4
    steps = c.B // T
    ctx, sb, ps, sem = stage_scope(c)
    with ctx:
        xn = sb("xn", [P, 2, T, D])
        xT = sb("xT", [D, 2, T, P])
        sc, top, dif, e = (sb(n, [P, T, k]) for n, k in (("sc", E), ("top", 1), ("dif", E), ("e", E)))
        rank, best, z, rz = (sb(n, [P, T, k]) for n, k in (("rank", E), ("best", E), ("z", 1), ("rz", 1)))
        gt, ge = sb("gt", [P, T, E, E]), sb("ge", [P, T, E, E])
        ps_x, ps_r = ps("ps_x"), ps("ps_r")
        xn_ready, xT_ps, xT_ready, copy_done, r_ps, dif_ready, exp_done, own, w_done = (
            sem(n) for n in ("xn_ready", "xT_ps", "xT_ready", "copy_done", "r_ps", "dif_ready", "exp_done", "own", "w_done"))
        block = ctx.enter_context(nc.Block())
        LAG = 3
        x4, xT4, wt4 = tiled(c, c.x), tiled(c, c.f1_xT), tiled(c, c.f1_wt)
        mean4, rstd4 = (t[:, :].rearrange("p (s i) -> p s i", i=T) for t in (c.mean, c.rstd))
        OWN = 11

        @block.tensor
        def _(pe):
            def slot(sl):
                if at := sl.step(1):
                    s, u = at
                    pe.wait_ge(xn_ready, s + 1)
                    wait(pe, xT_ready, s)
                    for i in range(T):
                        ins = nc.tensor.transpose(ps_x[:, i * P:i * P + P], xn[:, u % 2, i, :], c.ident[:, :])
                    ins.then_inc(xT_ps, 1)
                if at := sl.step(2):
                    s, u = at
                    pe.wait_ge(xT_ready, s + 1)
                    wait(pe, own, OWN * (s - 1) + 1)
                    for i in range(T):
                        ins = nc.tensor.matmul(ps_r[:, i * E:i * E + E], xT[:, u % 2, i, :], c.f1["router"][:, :], start=True, stop=True)
                    ins.then_inc(r_ps, 1)

            run_slots(pe, slot, steps, LAG)

        @block.scalar
        def _(act):
            def slot(sl):
                if at := sl.step(1):
                    s, u = at
                    act.wait_ge(xT_ps, s + 1)
                    wait(act, copy_done, s - 1)
                    wait(act, r_ps, s - 1)
                    nc.scalar.activation(xT[:, u % 2, :, :], ps_x[:, :].rearrange("p (i t) -> p i t", i=T), ACT.Copy).then_inc(xT_ready, 1)
                if at := sl.step(2):
                    s, u = at
                    act.wait_ge(dif_ready, s + 1)
                    nc.scalar.activation(e[:, :, :], dif[:, :, :], ACT.Exp).then_inc(exp_done, 1)

            run_slots(act, slot, steps, LAG)

        @block.gpsimd
        def _(pool):
            def slot(sl):
                if at := sl.step(1):
                    s, u = at
                    pool.wait_ge(xT_ready, s + 1)
                    nc.gpsimd.tensor_copy(xT4[:, s, :, :], xT[:, u % 2, :, :]).then_inc(copy_done, 1)

            run_slots(pool, slot, steps, LAG)

        @block.vector
        def _(dve):
            def slot(sl):
                if at := sl.step(0):
                    s, u = at
                    wait(dve, xT_ps, s - 1)
                    for i in range(T):
                        ins = nc.vector.tensor_scalar(xn[:, u % 2, i, :], x4[:, s, i, :], mean4[:, s, i:i + 1], rstd4[:, s, i:i + 1],
                                                      ALU.subtract, ALU.mult)
                    ins.then_inc(xn_ready, 1)
                if at := sl.step(2):
                    s, u = at
                    base = OWN * s

                    def after(ins, k):
                        ins.then_inc(own, 1)
                        dve.wait_ge(own, base + k)

                    def per_token(t):
                        return t[:, :, :].broadcast_to([P, T, E])

                    dve.wait_ge(r_ps, s + 1)
                    bias = [c.f1["router_b"][:, n, :].unsqueeze(1).broadcast_to([P, T, E]) for n in range(2)]
                    after(nc.vector.tensor_tensor(dif[:, :, :], ps_r[:, 0:T * E].rearrange("p (i e) -> p i e", i=T), bias[0], ALU.add), 1)
                    after(nc.vector.tensor_tensor(sc[:, :, :], dif[:, :, :], bias[1], ALU.add), 2)
                    after(nc.vector.tensor_reduce(top[:, :, 0], sc[:, :, :], AX.X, ALU.max), 3)
                    nc.vector.tensor_tensor(dif[:, :, :], sc[:, :, :], per_token(top), ALU.subtract).then_inc(dif_ready, 1)
                    dve.wait_ge(exp_done, s + 1)
                    after(top_two(c, dve, own, base + 3, sc[:, :, :], e[:, :, :], gt[:, :, :, :], ge[:, :, :, :], rank[:, :, :],
                                  c.w["tri4"][:, :, :, :], best[:, :, :]), 8)
                    after(nc.vector.tensor_reduce(z[:, :, 0], best[:, :, :], AX.X, ALU.add), 9)
                    after(nc.vector.reciprocal(rz[:, :, :], z[:, :, :]), 10)
                    after(nc.vector.tensor_tensor(wt4[:, s, :, :], best[:, :, :], per_token(rz), ALU.mult), 11)

            run_slots(dve, slot, steps, LAG)


def hidden_expert(c, expert, func, w1, w_gated, bias1, w2, bias2):
    nc = c.nc
    T, N = T6, T6 * P
    steps = c.B // T
    C = w1.shape[1]
    ctx, sb, ps, sem = stage_scope(c)
    with ctx:
        hid = sb("hid", [P, 2, C, N])
        sg = sb("sg", [P, 2, N]) if w_gated is not None else None
        ps_g = [ps(f"ps_g{i}") for i in range(2)]
        ps_u = [ps(f"ps_u{i}") for i in range(2)]
        ps_y = [ps(f"ps_y{i}") for i in range(2)]
        g_ps, u_ps, g_done, h_ready, y_ps, y_done = (sem(n) for n in ("g_ps", "u_ps", "g_done", "h_ready", "y_ps", "y_done"))
        block = ctx.enter_context(nc.Block())
        LAG = 1
        g_freed = h_ready if w_gated is None else g_done
        x4, wt4 = tiled(c, c.x), tiled(c, c.f1_wt)
        xT4 = tiled(c, c.f1_xT)

        @block.tensor
        def _(pe):
            def slot(sl):
                if at := sl.step(0):
                    s, u = at
                    for n in range(C):
                        wait(pe, g_freed, C * s + n - 1)
                        nc.tensor.matmul(ps_g[n % 2][:, :], w1[:, n, :], xT4[:, s, :, :], start=True, stop=True).then_inc(g_ps, 1)
                        if w_gated is not None:
                            wait(pe, h_ready, C * s + n - 1)
                            nc.tensor.matmul(ps_u[n % 2][:, :], w_gated[:, n, :], xT4[:, s, :, :], start=True, stop=True).then_inc(u_ps, 1)
                if at := sl.step(1):
                    s, u = at
                    pe.wait_ge(h_ready, C * (s + 1))
                    wait(pe, y_done, s - 1)
                    for i in range(T):
                        part = ps_y[u % 2][:, i * P:i * P + P]
                        if bias2 is not None:
                            nc.tensor.matmul(part, c.ones_row[0:1, 0:P], bias2[0:1, :], start=True, stop=False)
                        for n in range(C):
                            ins = nc.tensor.matmul(part, hid[:, u % 2, n, i * P:i * P + P], w2[:, n, :],
                                                   start=n == 0 and bias2 is None, stop=n == C - 1)
                    ins.then_inc(y_ps, 1)

            run_slots(pe, slot, steps, LAG)

        @block.scalar
        def _(act):
            def slot(sl):
                if at := sl.step(0):
                    s, u = at
                    for n in range(C):
                        act.wait_ge(g_ps, C * s + n + 1)
                        if w_gated is not None:
                            wait(act, h_ready, C * s + n - 1)
                            nc.scalar.activation(sg[:, n % 2, :], ps_g[n % 2][:, :], func).then_inc(g_done, 1)
                        else:
                            wait(act, y_ps, s - 1)
                            nc.scalar.activation(hid[:, u % 2, n, :], ps_g[n % 2][:, :], func, bias=bias1[:, n:n + 1]).then_inc(h_ready, 1)

            run_slots(act, slot, steps, LAG)

        @block.vector
        def _(dve):
            def slot(sl):
                if w_gated is not None and (at := sl.step(0)):
                    s, u = at
                    for n in range(C):
                        dve.wait_ge(g_done, C * s + n + 1)
                        dve.wait_ge(u_ps, C * s + n + 1)
                        wait(dve, y_ps, s - 1)
                        nc.vector.tensor_tensor(hid[:, u % 2, n, :], sg[:, n % 2, :], ps_u[n % 2][:, :], ALU.mult).then_inc(h_ready, 1)
                if at := sl.step(1):
                    s, u = at
                    dve.wait_ge(y_ps, s + 1)
                    for i in range(T):
                        ins = nc.vector.scalar_tensor_tensor(out=x4[:, s, i, :], in0=ps_y[u % 2][:, i * P:i * P + P],
                                                             scalar=wt4[:, s, i, expert:expert + 1], in1=x4[:, s, i, :],
                                                             op0=ALU.mult, op1=ALU.add)
                    ins.then_inc(y_done, 1)

            run_slots(dve, slot, steps, LAG)


def normed_expert(c, expert):
    nc, f = c.nc, c.f1
    T, N = T6, T6 * P
    steps = c.B // T
    ctx, sb, ps, sem = stage_scope(c)
    with ctx:
        xr = sb("xr", [D, 2, T, P])
        st = sb("st", [P, 2, T, 6])
        both, dif, dif2, sq, mean, var, vpe, root, rstd = (
            sb(n, [P, 2, T]) for n in ("both", "dif", "dif2", "sq", "mean", "var", "vpe", "root", "rstd"))
        rows = [sb(f"rows{k}", [P, 2, T, D]) for k in range(2)]
        hT = [sb(f"hT{k}", [D, 2, N]) for k in range(2)]
        ff = sb("ff", [P, 2, 2, N])
        pre = [ps(f"pre{k}") for k in range(2)]
        ps_h = [ps(f"ps_h{k}") for k in range(2)]
        ps_g = [ps(f"ps_g{k}") for k in range(2)]
        ps_y = ps("ps_y")
        xr_ready, f_ps, f_ready, y_ps, y_done = (sem(n) for n in ("xr_ready", "f_ps", "f_ready", "y_ps", "y_done"))
        pre_ps, st_done, ag_done, var_ready, root_ready, rstd_done, rows_ready, h_ps, h_ready = (
            [sem(f"{n}{k}") for k in range(2)] for n in ("pre_ps", "st_done", "ag_done", "var_ready", "root_ready", "rstd_done",
                                                         "rows_ready", "h_ps", "h_ready"))
        block = ctx.enter_context(nc.Block())
        LAG = 4
        x4, wt4, xT4 = tiled(c, c.x), tiled(c, c.f1_wt), tiled(c, c.f1_xT)

        @block.tensor
        def _(pe):
            def transposes(at, k):
                s, u = at
                pe.wait_ge(rows_ready[k], s + 1)
                wait(pe, h_ready[k], s)
                for i in range(T):
                    ins = nc.tensor.transpose(ps_h[k][:, i * P:i * P + P], rows[k][:, u % 2, i, :], c.ident[:, :])
                ins.then_inc(h_ps[k], 1)

            def slot(sl):
                if at := sl.step(2):
                    transposes(at, 0)
                if at := sl.step(4):
                    transposes(at, 1)
                if at := sl.step(1):
                    s, u = at
                    pe.wait_ge(xr_ready, s + 1)
                    wait(pe, rows_ready[0], s)
                    for i in range(T):
                        part = pre[0][:, i * P:i * P + P]
                        nc.tensor.matmul(part, c.ones_row[0:1, 0:P], c.f1_ce_b[0:1, :], start=True, stop=False)
                        ins = nc.tensor.matmul(part, xr[:, u % 2, i, :], c.f1_ce[:, :], start=False, stop=True)
                    ins.then_inc(pre_ps[0], 1)
                if at := sl.step(3):
                    s, u = at
                    pe.wait_ge(f_ready, 2 * (s + 1))
                    wait(pe, rows_ready[1], s)
                    for i in range(T):
                        part = pre[1][:, i * P:i * P + P]
                        cols = slice(i * P, i * P + P)
                        nc.tensor.matmul(part, c.ones_row[0:1, 0:P], f["f2b"][0:1, :], start=True, stop=False)
                        nc.tensor.matmul(part, hT[0][:, u % 2, cols], c.ident[:, :], start=False, stop=False)
                        for n in range(2):
                            ins = nc.tensor.matmul(part, ff[:, u % 2, n, cols], f["f2"][:, n, :], start=False, stop=n == 1)
                    ins.then_inc(pre_ps[1], 1)
                if at := sl.step(2):
                    s, u = at
                    pe.wait_ge(h_ready[0], s + 1)
                    for n in range(2):
                        wait(pe, f_ready, 2 * s - 1 + n)
                        nc.tensor.matmul(ps_g[n][:, :], f["f1"][:, n, :], hT[0][:, u % 2, :], start=True, stop=True).then_inc(f_ps, 1)
                if at := sl.step(4):
                    s, u = at
                    pe.wait_ge(h_ready[1], s + 1)
                    wait(pe, y_done, s)
                    for i in range(T):
                        part = ps_y[:, i * P:i * P + P]
                        nc.tensor.matmul(part, c.ones_row[0:1, 0:P], f["genb"][0:1, :], start=True, stop=False)
                        ins = nc.tensor.matmul(part, hT[1][:, u % 2, i * P:i * P + P], f["gen"][:, :], start=False, stop=True)
                    ins.then_inc(y_ps, 1)

            run_slots(pe, slot, steps, LAG)

        @block.scalar
        def _(act):
            def shifted(at, k):
                s, u = at
                act.wait_ge(h_ps[k], s + 1)
                if k == 0:
                    wait(act, pre_ps[1], s - 1)
                else:
                    wait(act, y_ps, s - 1)
                nc.scalar.activation(hT[k][:, u % 2, :], ps_h[k][:, :], ACT.Identity, scale=f["norms"][:, 2 * k:2 * k + 1],
                                     bias=f["norms"][:, 2 * k + 1:2 * k + 2]).then_inc(h_ready[k], 1)

            def roots(at, k):
                s, u = at
                act.wait_ge(var_ready[k], s + 1)
                nc.scalar.activation(root[:, k, :], vpe[:, k, :], ACT.Sqrt).then_inc(root_ready[k], 1)

            def slot(sl):
                if at := sl.step(2):
                    shifted(at, 0)
                if at := sl.step(4):
                    shifted(at, 1)
                if at := sl.step(1):
                    roots(at, 0)
                if at := sl.step(3):
                    roots(at, 1)
                if at := sl.step(2):
                    s, u = at
                    for n in range(2):
                        act.wait_ge(f_ps, 2 * s + n + 1)
                        nc.scalar.activation(ff[:, u % 2, n, :], ps_g[n][:, :], ACT.Relu, bias=f["f1b"][:, n:n + 1]).then_inc(f_ready, 1)

            run_slots(act, slot, steps, LAG)

        @block.gpsimd
        def _(pool):
            def slot(sl):
                if at := sl.step(0):
                    s, u = at
                    wait(pool, pre_ps[0], s - 1)
                    nc.gpsimd.tensor_copy(xr[:, u % 2, :, :], xT4[:, s, :, :]).then_inc(xr_ready, 1)

            run_slots(pool, slot, steps, LAG)

        @block.vector
        def _(dve):
            def statistics(at, k):
                s, u = at
                dve.wait_ge(pre_ps[k], s + 1)
                for i in range(T):
                    ins = nc.vector.bn_stats(st[:, k, i, :], pre[k][:, i * P:i * P + P])
                ins.then_inc(st_done[k], 1)
                me, mo, ve, vo = (st[:, k, :, n] for n in (1, 4, 2, 5))
                dve.wait_ge(st_done[k], s + 1)
                nc.vector.tensor_tensor(both[:, k, :], me, mo, ALU.add)
                nc.vector.tensor_tensor(dif[:, k, :], me, mo, ALU.subtract)
                nc.vector.tensor_tensor(sq[:, k, :], ve, vo, ALU.add).then_inc(ag_done[k], 1)
                dve.wait_ge(ag_done[k], 3 * s + 1)
                nc.vector.tensor_scalar(mean[:, k, :], both[:, k, :], 0.5, None, ALU.mult)
                nc.vector.tensor_tensor(dif2[:, k, :], dif[:, k, :], dif[:, k, :], ALU.mult).then_inc(ag_done[k], 1)
                dve.wait_ge(ag_done[k], 3 * s + 2)
                nc.vector.scalar_tensor_tensor(out=var[:, k, :], in0=dif2[:, k, :], scalar=D / 4, in1=sq[:, k, :],
                                               op0=ALU.mult, op1=ALU.add).then_inc(ag_done[k], 1)
                dve.wait_ge(ag_done[k], 3 * s + 3)
                nc.vector.tensor_scalar(vpe[:, k, :], var[:, k, :], 1.0 / D, EPS, ALU.mult, ALU.add).then_inc(var_ready[k], 1)

            def normalised(at, k):
                s, u = at
                dve.wait_ge(root_ready[k], s + 1)
                nc.vector.reciprocal(rstd[:, k, :], root[:, k, :]).then_inc(rstd_done[k], 1)
                dve.wait_ge(rstd_done[k], s + 1)
                wait(dve, h_ps[k], s - 1)
                for i in range(T):
                    ins = nc.vector.tensor_scalar(rows[k][:, u % 2, i, :], pre[k][:, i * P:i * P + P], mean[:, k, i:i + 1],
                                                  rstd[:, k, i:i + 1], ALU.subtract, ALU.mult)
                ins.then_inc(rows_ready[k], 1)

            def slot(sl):
                first, second = sl.step(1), sl.step(3)
                if first:
                    statistics(first, 0)
                if second:
                    statistics(second, 1)
                if first:
                    normalised(first, 0)
                if second:
                    normalised(second, 1)
                if at := sl.step(4):
                    s, u = at
                    dve.wait_ge(y_ps, s + 1)
                    for i in range(T):
                        ins = nc.vector.scalar_tensor_tensor(out=x4[:, s, i, :], in0=ps_y[:, i * P:i * P + P],
                                                             scalar=wt4[:, s, i, expert:expert + 1], in1=x4[:, s, i, :],
                                                             op0=ALU.mult, op1=ALU.add)
                    ins.then_inc(y_done, 1)

            run_slots(dve, slot, steps, LAG)


def latent_weights(c):
    nc = c.nc
    ctx, sb, ps, sem = stage_scope(c)
    with ctx:
        pq = [ps(f"p{n}") for n in range(3)]
        ready, copied = sem("ready"), sem("copied")
        block = ctx.enter_context(nc.Block())
        parts = ((c.w["a0_dq"], c.w["a0_uq"], c.a0_q), (c.w["a0_dkv"], c.w["a0_uk"], c.a0_k), (c.w["a0_dkv"], c.w["a0_uv"], c.a0_v))

        @block.tensor
        def _(pe):
            for n, (down, up, out) in enumerate(parts):
                nc.tensor.matmul(pq[n][:, 0:out.shape[1]], down[:, :], up[:, :], start=True, stop=True).then_inc(ready, 1)

        @block.scalar
        def _(act):
            for n, (down, up, out) in enumerate(parts):
                act.wait_ge(ready, n + 1)
                nc.scalar.activation(out[:, :], pq[n][:, 0:out.shape[1]], ACT.Copy).then_inc(copied, 1)
            act.wait_ge(copied, len(parts))


def store_output(c):
    nc = c.nc
    ctx, sb, ps, sem = stage_scope(c)
    with ctx:
        stored = sem("stored")
        block = ctx.enter_context(nc.Block())

        @block.sync
        def _(sp):
            sp.dma_start(c.out.rearrange("b p d -> p b d"), c.x[:, :, :]).then_inc(stored, 16)
            sp.wait_ge(stored, 16)


def decoder(nc, inp, out, batches, layers=6):
    c = Core(nc, inp, out, batches)
    B = batches
    ctx = ExitStack()
    with ctx:
        def sb(name, shape, dt=F32):
            return ctx.enter_context(nc.sbuf_tensor(name, shape, dt))

        c.x = sb("x", [P, B, D])
        c.stats = sb("stats", [P, B, 6])
        c.mean, c.rstd = sb("mean", [P, B]), sb("rstd", [P, B])
        c.w = {}
        keep = []
        for name in inp:
            if name == "x" or name.startswith("late_"):
                continue
            shape = list(inp[name].shape)
            c.w[name] = sb("w_" + name, shape, inp[name].dtype)
            keep.append((name, c.w[name][(slice(None),) * len(shape)]))
        c.ident, c.ident16, c.ones_row = c.w["ident"], c.w["ident16"], c.w["ones_row"]
        c.mask_q, c.mask_k = c.w["mask_q"], c.w["mask_k"]
        c.block, c.ones16 = c.w["block"], c.w["ones16"]
        c.a0_q, c.a0_k, c.a0_v = (sb(n, [P, D]) for n in ("a0_q", "a0_k", "a0_v"))

        c.keys = inp["ctx"].shape[2]
        c.ctx = c.w["ctx"]
        c.x0_a, c.x0_o, c.x0_b = sb("x0_a", [P, HEADS, D]), sb("x0_o", [P, HEADS // 2, D]), sb("x0_b", [1, D])

        c.stage = "load"
        load_inputs(c, keep)
        if layers >= 1:
            c.stage = "n0"
            norm_scalars(c, False)
            c.stage = "lat"
            latent_weights(c)
            c.stage = "a0"
            self_attention(c, (c.a0_q[:, :], c.a0_k[:, :], c.a0_v[:, :], c.w["a0_o"][:, :]), HD ** -0.5)
        if layers >= 2:
            c.stage = "n1"
            norm_scalars(c, True)
            c.stage = "x0"
            wide_weights(c)
            cross_attention_wide(c)
        if layers >= 3:
            c.stage = "n2"
            norm_scalars(c, False)
            c.stage = "f0"
            scored_experts(c)
        if layers >= 4:
            c.stage = "n3"
            norm_scalars(c, False)
            c.stage = "a1"
            attention_over_heads(c)
        if layers >= 5:
            c.stage = "n4"
            norm_scalars(c, False)
            cross_attention_tempered(c)
        if layers >= 6:
            c.stage = "n5"
            norm_scalars(c, False)
            mixed_experts(c)
        c.stage = "out"
        store_output(c)



def triangles(experts):
    behind = np.triu(np.ones((experts, experts), np.float32), 1)
    return np.broadcast_to(np.stack([behind, behind.T]), (P, 2, experts, experts))


def constants():
    bf = mybir.dt.np(BF16)
    r = np.arange(P)
    strip = r % STRIP
    block = np.zeros((P, 2 * GROUP), np.float32)
    block[:, 0:GROUP] = strip[:, None] // HD == np.arange(GROUP)
    block[:, GROUP:] = (strip[:, None] % GROUP == np.arange(GROUP)) & (strip[:, None] < 3 * GROUP)
    later = np.where(r[None, :] > r[:, None], MASKED, 0.0)
    return {
        "ident": np.eye(P, dtype=np.float32), "ident16": np.eye(P).astype(bf),
        "mask_q": later.astype(bf), "mask_k": later.T.astype(bf),
        "tri8": triangles(8), "tri4": triangles(4),
        "block": block,
        "ones_row": np.ones((1, 512), np.float32), "ones16": np.ones((P, P), bf),
    }


def layouts(inputs, layers=6):
    a = {k: np.asarray(v) for k, v in inputs.items()}
    t = {"x": a["x"]}
    t.update(constants())
    t["a0_dq"], t["a0_uq"] = a["L0_attn_W_dq"].T, a["L0_attn_W_uq"]
    t["a0_dkv"], t["a0_uk"] = a["L0_attn_W_dkv"].T, a["L0_attn_W_uk"]
    t["a0_uv"], t["a0_o"] = a["L0_attn_W_uv"], a["L0_attn_W_o"]
    t["a1_qkv"] = np.concatenate([a["L1_attn_W" + n].T for n in "qkv"], axis=1)
    t["a1_o"] = np.tile(a["L1_attn_Wo"].T.reshape(HEADS, HD, D), (P // HEADS, 1, 1))
    t["a1_b"] = a["L1_attn_bo"][None]
    t["a1_rows"] = (np.arange(P)[:, None] // HEADS == np.arange(P // HEADS)).astype(np.float32)
    t["ctx"] = a["ctx_1024"].transpose(2, 0, 1)
    inner = a["L0_xattn_w_q"].shape[1]
    per_head = lambda w: w.T.reshape(HEADS, inner // HEADS, D).transpose(1, 0, 2)
    t["x0_q"], t["x0_k"] = per_head(a["L0_xattn_w_q"]), per_head(a["L0_xattn_w_kv"][:, :inner])
    t["x0_v"] = a["L0_xattn_w_kv"][:, inner:]
    t["x0_out"] = a["L0_xattn_w_out"].reshape(HEADS // 2, P, D).transpose(1, 0, 2)
    t["x0_bias"] = a["L0_xattn_b_out"][None]
    t["x0_gate"] = np.broadcast_to(a["L0_xattn_gate"][None], (P, 1))
    E, H = a["L0_ffn_W1"].shape[:2]
    t["f0_router"] = a["L0_ffn_Wg"].T
    t["late_f0_1"], t["late_f0_2"] = (a["L0_ffn_W" + n].reshape(E * H, D).T for n in "12")
    down = np.zeros((E, 3 * P, D), np.float32)
    down[:, :H] = a["L0_ffn_W3"].transpose(0, 2, 1)
    t["late_f0_3"] = down.reshape(E, 3, P, D).transpose(2, 0, 1, 3)
    t["x1_q"], t["x1_k"], t["x1_v"], t["x1_o"] = (a["L1_xattn_W" + n].T for n in "qkvo")
    t["x1_bias"] = np.stack([a["L1_xattn_bq"], a["L1_xattn_bk"]], axis=1)
    t["x1_bv"], t["x1_bo"] = a["L1_xattn_bv"][None], a["L1_xattn_bo"][None]
    t["x1_w1"], t["x1_w2"] = a["L1_xattn_w1"].T, a["L1_xattn_w2"].T
    t["x1_w3"] = np.broadcast_to(a["L1_xattn_w3"].T, (a["L1_xattn_w3"].shape[1], P))
    t["x1_mlp_b"] = np.stack([a["L1_xattn_b1"], a["L1_xattn_b2"]], axis=1)
    t["x1_b3"] = np.broadcast_to(a["L1_xattn_b3"][None], (P, 1))
    t["x1_heads"] = np.arange(P)[:, None] // HD == np.arange(HEADS)
    t["x1_heads"] = t["x1_heads"].astype(np.float32)
    keys = a["ctx_1024"].shape[1]
    pick = np.zeros((P, 3, 3), np.float32)
    pick[:, 0, 0] = HD ** -0.5 / (P * keys)
    pick[:, 1, 1] = HD ** -0.5 / P
    pick[:, 2, 2] = 1.0 / (P * (keys - 1))
    t["x1_pick"] = pick.reshape(P, 9)
    t["x1_less"] = np.array([[0.0, 0.0, -1.0 / (keys * (keys - 1))]], np.float32)
    place = np.arange(STRIP)[None] // HD == np.arange(GROUP)[:, None]
    t["x1_place"] = np.broadcast_to(place.astype(np.float32), (P, GROUP, STRIP))
    f = lambda n: a["L1_ffn_" + n]
    units = lambda w: w.reshape(D, -1, P)
    down = lambda w: w.reshape(-1, P, w.shape[1]).transpose(1, 0, 2)
    col = lambda b: b.reshape(-1, P).T
    late = {
        "router": f("router_w"),
        "router_b": np.broadcast_to(np.stack([f("router_b"), f("load_balancer")]), (P, 2, 4)),
        "sw_1": units(f("sw_w1")), "sw_3": units(f("sw_w3")), "sw_2": down(f("sw_w2")),
        "me_eqT": f("me_eq_w").T, "me_vT": f("me_wv").T, "me_oT": f("me_wo").T, "me_v": f("me_wv"), "me_o": f("me_wo"),
        "c1": units(f("me_c1w")), "c1b": col(f("me_c1b")), "c2": down(f("me_c2w")), "c2b": f("me_c2b")[None],
        "cols": np.stack([f(n) for n in ("me_eq_b", "me_bv", "me_bo", "ce_syn_b", "ce_bv")], axis=1),
        "ce_vT": f("ce_wv").T, "ce_o": f("ce_wo"), "ce_synT": f("ce_syn_w").T, "ce_bo": f("ce_bo")[None],
        "norms": np.stack([f(n) for n in ("ce_n1g", "ce_n1b", "ce_n2g", "ce_n2b")], axis=1),
        "f1": units(f("ce_f1w")), "f1b": col(f("ce_f1b")), "f2": down(f("ce_f2w")), "f2b": f("ce_f2b")[None],
        "gen": f("ce_gen_w"), "genb": f("ce_gen_b")[None],
        "ml_1": units(f("ml_w1")), "ml_b1": col(f("ml_b1")), "ml_2": down(f("ml_w2")), "ml_b2": f("ml_b2")[None],
    }
    t.update({"late_f1_" + n: v for n, v in late.items()})
    t["x0_ln"] = np.stack([a["L0_xattn_ln_gamma"], a["L0_xattn_ln_beta"]], axis=1)
    return {k: np.ascontiguousarray(v) for k, v in t.items()}


def kernel(**inputs):
    import concourse.bacc as bacc
    from concourse.bass_utils import run_bass_kernel_spmd

    nc = bacc.Bacc("TRN2", target_bir_lowering=False, num_devices=1)
    arrays = layouts(inputs)
    B = arrays["x"].shape[0]
    aps = {k: nc.dram_tensor("in_" + k, v.shape, mybir.dt.from_np(v.dtype), kind="ExternalInput").ap() for k, v in arrays.items()}
    out = nc.dram_tensor("out", (B, P, D), F32, kind="ExternalOutput").ap()
    decoder(nc, aps, out, B)
    r = run_bass_kernel_spmd(nc, [{"in_" + k: v for k, v in arrays.items()}], core_ids=[0])
    return r.results[0]["out"]
```

```python
from contextlib import ExitStack

import numpy as np

import concourse.bass as bass
import concourse.mybir as mybir

F32 = mybir.dt.float32
F32R = mybir.dt.float32r
BF16 = mybir.dt.bfloat16
ALU = mybir.AluOpType
ACT = mybir.ActivationFunctionType
AX = mybir.AxisListType

P = 128
D = 128
HEADS = 16
HD = 8
GROUPS = 4
GROUP = 4
STRIP = 32
EPS = 1e-5
MASKED = -1e30
UNROLL = 4


class Slot:

    def __init__(self, t, odd, steps, fixed, ring):
        self.t, self.odd, self.steps, self.fixed, self.ring = t, odd, steps, fixed, ring

    def step(self, lag):
        if self.fixed and not 0 <= self.t - lag < self.steps:
            return None
        return self.t - lag, (self.odd - lag) % self.ring


def run_slots(eng, slot, steps, lag, unroll=UNROLL):
    ring = max(unroll, UNROLL)
    first = min(-(-(lag + 2) // unroll) * unroll, steps)
    last = steps - (steps - first) % unroll
    for t in range(first):
        slot(Slot(t, t % ring, steps, True, ring))
    if last > first:
        with eng.Fori(first // unroll, last // unroll) as i:
            for k in range(unroll):
                slot(Slot(i * unroll + k, k, steps, False, ring))
    for t in range(last, steps + lag):
        slot(Slot(t, t % ring, steps, True, ring))


def wait(eng, sem, value):
    if not (isinstance(value, int) and value <= 0):
        eng.wait_ge(sem, value)


class Core:

    def __init__(self, nc, inputs, out, batches):
        self.nc, self.inp, self.out, self.B = nc, inputs, out, batches


def stage_scope(c):
    ctx = ExitStack()

    def sb(name, shape, dt=F32):
        return ctx.enter_context(c.nc.sbuf_tensor(f"{stage}_{name}", shape, dt))

    def ps(name, shape=(P, 512), dt=F32):
        return ctx.enter_context(c.nc.psum_tensor(f"{stage}_{name}", list(shape), dt))

    sems = []

    def sem(name):
        sems.append(c.nc.alloc_semaphore(name=f"{stage}_{name}"))
        return sems[-1]

    stage = c.stage

    def clear():
        c.nc.clear_and_free_semaphores(sems)
        c.nc.all_engine_barrier()

    ctx.callback(clear)
    return ctx, sb, ps, sem


def norm_scalars(c, second):
    nc = c.nc
    ctx, sb, ps, sem = stage_scope(c)
    with ctx:
        dif, var, vpe, root, rec, t1, t2 = (sb(n, [P, c.B]) for n in ("dif", "var", "vpe", "root", "rec", "t1", "t2"))
        dv = sem("dv")
        var_ready, root_ready = sem("var_ready"), sem("root_ready")
        block = ctx.enter_context(nc.Block())
        me, mo, ve, vo = (c.stats[:, :, k] for k in (1, 4, 2, 5))

        @block.vector
        def _(dve):
            n = [0]

            def own(ins):
                n[0] += 1
                ins.then_inc(dv, 1)
                dve.wait_ge(dv, n[0])

            def rsqrt(out, x, k):
                nc.vector.tensor_copy(vpe[:, :], x).then_inc(var_ready, 1)
                dve.wait_ge(root_ready, k)
                own(nc.vector.reciprocal(rec[:, :], root[:, :]))
                own(nc.vector.tensor_tensor(t1[:, :], rec[:, :], rec[:, :], ALU.mult))
                own(nc.vector.tensor_tensor(t2[:, :], t1[:, :], vpe[:, :], ALU.mult))
                own(nc.vector.tensor_scalar(t1[:, :], t2[:, :], -0.5, 1.5, ALU.mult, ALU.add))
                own(nc.vector.tensor_tensor(out, t1[:, :], rec[:, :], ALU.mult))

            own(nc.vector.tensor_tensor(t1[:, :], me, mo, ALU.add))
            own(nc.vector.tensor_scalar(c.mean[:, :], t1[:, :], 0.5, None, ALU.mult))
            own(nc.vector.tensor_tensor(dif[:, :], me, mo, ALU.subtract))
            own(nc.vector.tensor_tensor(t1[:, :], dif[:, :], dif[:, :], ALU.mult))
            own(nc.vector.tensor_tensor(t2[:, :], ve, vo, ALU.add))
            own(nc.vector.scalar_tensor_tensor(out=dif[:, :], in0=t1[:, :], scalar=D / 4, in1=t2[:, :],
                                               op0=ALU.mult, op1=ALU.add))
            own(nc.vector.tensor_scalar(var[:, :], dif[:, :], 1.0 / D, None, ALU.mult))
            own(nc.vector.tensor_scalar(t1[:, :], var[:, :], EPS, None, ALU.add))
            rsqrt(c.rstd[:, :], t1[:, :], 1)
            if second:
                own(nc.vector.tensor_tensor(t1[:, :], c.rstd[:, :], c.rstd[:, :], ALU.mult))
                own(nc.vector.tensor_tensor(t2[:, :], t1[:, :], var[:, :], ALU.mult))
                own(nc.vector.tensor_scalar(t1[:, :], t2[:, :], EPS, None, ALU.add))
                rsqrt(dif[:, :], t1[:, :], 2)
                own(nc.vector.tensor_tensor(t1[:, :], c.rstd[:, :], dif[:, :], ALU.mult))
                own(nc.vector.tensor_copy(c.rstd[:, :], t1[:, :]))

        @block.scalar
        def _(act):
            for k in range(2 if second else 1):
                act.wait_ge(var_ready, k + 1)
                nc.scalar.activation(root[:, :], vpe[:, :], ACT.Sqrt).then_inc(root_ready, 1)


def load_inputs(c, keep):
    nc = c.nc
    ctx, sb, ps, sem = stage_scope(c)
    with ctx:
        parts = max(1, c.B // 16)
        per = c.B // parts
        x_in = [sem(f"x_in{n}") for n in range(parts)]
        w_in, made = sem("w_in"), sem("made")
        block = ctx.enter_context(nc.Block())
        xs = c.inp["x"].rearrange("b p d -> p b d")

        @block.sync
        def _(sp):
            for n in range(parts):
                sp.dma_start(c.x[:, n * per:(n + 1) * per, :], xs[:, n * per:(n + 1) * per, :]).then_inc(x_in[n], 16)
            for name, tile in keep:
                sp.dma_start(tile, c.inp[name]).then_inc(w_in, 16)
            sp.wait_ge(w_in, 16 * len(keep))

        @block.vector
        def _(dve):
            for n in range(parts):
                dve.wait_ge(x_in[n], 16)
                for s in range(n * per, (n + 1) * per):
                    ins = nc.vector.bn_stats(c.stats[:, s, :], c.x[:, s, :])
            ins.then_inc(made, 1)
            dve.wait_ge(made, 1)


def self_attention(c, weights, scale):
    nc, B = c.nc, c.B
    ctx, sb, ps, sem = stage_scope(c)
    with ctx:
        wq, wk, wv, wo = weights
        xn = sb("xn", [P, 2, D])
        xT = sb("xT", [P, P])
        qkv = sb("qkv", [P, 2, 3, P])
        q_bd, k_bd = sb("q_bd", [P, 2, GROUP, P]), sb("k_bd", [P, 2, GROUP, P])
        v1 = sb("v1", [P, UNROLL, HEADS, STRIP])
        nmax = sb("nmax", [P, HEADS])
        rest = sb("rest", [P, 2, HEADS])
        part = sb("part", [P, 2, HEADS], BF16)
        pad = sb("pad", [P, P])
        fold = sb("fold", [P, 2, GROUP, P], BF16)
        e = sb("e", [P, 2, HEADS, P])
        oz = sb("oz", [P, 512])
        rz = sb("rz", [P, HEADS])
        o = sb("o", [P, 2, D])
        oT = sb("oT", [D, P])

        ps_misc, ps_qkv, ps_o, ps_z = ps("ps_misc"), ps("ps_qkv"), ps("ps_o"), ps("ps_z")
        ps_x, ps_f, ps_oT, ps_y = (ps_misc[:, n * P:n * P + P] for n in range(4))
        ps_n = [ps(f"ps_n{i}") for i in range(2)]
        ps_t = [ps(f"ps_t{i}") for i in range(2)]

        made = sem("made")
        xn_ready, xT_ps, xT_ready, qkv_ps, qkv_ready = (sem(n) for n in ("xn_ready", "xT_ps", "xT_ready", "qkv_ps", "qkv_ready"))
        k_bd_ready, q_bd_ready, v_ready = sem("k_bd_ready"), sem("q_bd_ready"), sem("v_ready")
        nat_ps, max_done, own, pad_ready, pad_ps, fold_ready = (
            sem(n) for n in ("nat_ps", "max_done", "own", "pad_ready", "pad_ps", "fold_ready"))
        sT_ps, exp_done = sem("sT_ps"), sem("exp_done")
        o_ps, oz_ready, z_ps, rz_ready, o_ready, oT_ps, oT_ready, y_ps, x_done = (
            sem(n) for n in ("o_ps", "oz_ready", "z_ps", "rz_ready", "o_ready", "oT_ps", "oT_ready", "y_ps", "x_done"))
        block = ctx.enter_context(nc.Block())
        LAG = 5

        def strip(g):
            return slice(STRIP * g, STRIP * g + STRIP)

        @block.tensor
        def _(pe):
            def slot(sl):
                if at := sl.step(4):
                    s, u = at
                    pe.wait_ge(exp_done, (s + 1) * GROUPS)
                    pe.wait_ge(v_ready, s + 1)
                    for n in range(HEADS):
                        j, g = divmod(n, GROUPS)
                        h = GROUP * g + j
                        ins = nc.tensor.matmul(ps_o[strip(g), j * P:j * P + P], v1[:, u, h, :], e[:, u % 2, h, :],
                                               start=True, stop=True)
                    ins.then_inc(o_ps, 1)
                if at := sl.step(1):
                    s, u = at
                    pe.wait_ge(xn_ready, s + 1)
                    wait(pe, fold_ready, s - 1)
                    wait(pe, x_done, s - 4)
                    nc.tensor.transpose(ps_x, xn[:, u % 2, :], c.ident[:, :]).then_inc(xT_ps, 1)
                if at := sl.step(2):
                    s, u = at
                    pe.wait_ge(k_bd_ready, s + 1)
                    for g in range(GROUPS):
                        wait(pe, max_done, s * GROUPS + g - 1)
                        nc.tensor.matmul(ps_n[g % 2][:, :], qkv[strip(g), u % 2, 0, :],
                                               k_bd[strip(g), u % 2, :, :], start=True, stop=False)
                        nc.tensor.matmul(ps_n[g % 2][:, :].rearrange("p (t k) -> p t k", t=GROUP), c.ident16[:, :],
                                         c.mask_q[:, :].unsqueeze(1).broadcast_to([P, GROUP, P]),
                                         start=False, stop=True).then_inc(nat_ps, 1)
                if at := sl.step(4):
                    s, u = at
                    pe.wait_ge(oz_ready, s + 1)
                    wait(pe, o_ready, s)
                    for j in range(GROUP):
                        ins = nc.tensor.transpose(ps_z[:, j * P:j * P + P], oz[:, j * P:j * P + P], c.ident[:, :])
                    ins.then_inc(z_ps, 1)
                if at := sl.step(5):
                    s, u = at
                    pe.wait_ge(o_ready, s + 1)
                    wait(pe, xT_ready, min(s + 5, B) if sl.fixed else s + 5)
                    wait(pe, x_done, s)
                    nc.tensor.transpose(ps_oT, o[:, u % 2, :], c.ident[:, :]).then_inc(oT_ps, 1)
                if at := sl.step(3):
                    s, u = at
                    pe.wait_ge(q_bd_ready, s + 1)
                    pe.wait_ge(fold_ready, s + 1)
                    for g in range(GROUPS):
                        wait(pe, exp_done, s * GROUPS + g - 1)
                        nc.tensor.matmul(ps_t[g % 2][:, :], qkv[strip(g), u % 2, 1, :], q_bd[strip(g), u % 2, :, :],
                                         start=True, stop=False)
                        nc.tensor.matmul(ps_t[g % 2][:, :].rearrange("p (t k) -> p t k", t=GROUP), c.ident16[:, :],
                                         c.mask_k[:, :].unsqueeze(1).broadcast_to([P, GROUP, P]),
                                         start=False, stop=False)
                        nc.tensor.matmul(ps_t[g % 2][:, :], c.ones16[strip(g), :], fold[strip(g), u % 2, :, :],
                                         start=False, stop=True).then_inc(sT_ps, 1)
                if at := sl.step(2):
                    s, u = at
                    pe.wait_ge(pad_ready, s + 1)
                    wait(pe, xT_ready, min(s + 2, B) if sl.fixed else s + 2)
                    wait(pe, oT_ready, s - 2)
                    nc.tensor.transpose(ps_f, pad[:, :], c.ident[:, :]).then_inc(pad_ps, 1)
                if at := sl.step(1):
                    s, u = at
                    pe.wait_ge(xT_ready, s + 1)
                    wait(pe, qkv_ready, s)
                    nc.tensor.matmul(ps_qkv[:, 0:P], wq, xT[:, :], start=True, stop=True)
                    nc.tensor.matmul(ps_qkv[:, P:2 * P], wk, xT[:, :], start=True, stop=True)
                    nc.tensor.matmul(ps_qkv[:, 2 * P:3 * P], xT[:, :], wv, start=True, stop=True).then_inc(qkv_ps, 1)
                if at := sl.step(5):
                    s, u = at
                    pe.wait_ge(oT_ready, s + 1)
                    wait(pe, fold_ready, min(s + 4, B) if sl.fixed else s + 4)
                    nc.tensor.matmul(ps_y, oT[:, :], wo, start=True, stop=True).then_inc(y_ps, 1)

            run_slots(pe, slot, B, LAG)

        @block.scalar
        def _(act):
            def slot(sl):
                if at := sl.step(4):
                    s, u = at
                    act.wait_ge(o_ps, s + 1)
                    wait(act, z_ps, s)
                    nc.scalar.activation(oz[:, :], ps_o[:, :], ACT.Copy).then_inc(oz_ready, 1)
                if at := sl.step(1):
                    s, u = at
                    act.wait_ge(xT_ps, s + 1)
                    nc.scalar.activation(xT[:, :], ps_x, ACT.Copy).then_inc(xT_ready, 1)
                if at := sl.step(5):
                    s, u = at
                    act.wait_ge(oT_ps, s + 1)
                    nc.scalar.activation(oT[:, :], ps_oT, ACT.Copy).then_inc(oT_ready, 1)
                if at := sl.step(3):
                    s, u = at
                    for g in range(GROUPS):
                        act.wait_ge(sT_ps, s * GROUPS + g + 1)
                        nc.scalar.activation(e[:, u % 2, GROUP * g:GROUP * g + GROUP, :],
                                             ps_t[g % 2][:, :].rearrange("p (t q) -> p t q", t=GROUP),
                                             ACT.Exp, scale=scale).then_inc(exp_done, 1)
                if at := sl.step(1):
                    s, u = at
                    act.wait_ge(qkv_ps, s + 1)
                    wait(act, v_ready, s - 1)
                    nc.scalar.activation(qkv[:, u % 2, :, :], ps_qkv[:, 0:3 * P].rearrange("p (n k) -> p n k", n=3),
                                         ACT.Copy).then_inc(qkv_ready, 1)

            run_slots(act, slot, B, LAG)

        @block.gpsimd
        def _(pool):
            nc.gpsimd.memset(v1[:, :, :, :], 1.0).then_inc(made, 1)
            pool.wait_ge(made, 1)

            def slot(sl):
                if at := sl.step(1):
                    s, u = at
                    pool.wait_ge(qkv_ready, s + 1)
                    for n, bd, ready in ((1, k_bd, k_bd_ready), (0, q_bd, q_bd_ready)):
                        nc.gpsimd.tensor_tensor(bd[:, u % 2, :, :], qkv[:, u % 2, n, :].unsqueeze(1).broadcast_to([P, GROUP, P]),
                                                c.block[:, 0:GROUP].unsqueeze(2).broadcast_to([P, GROUP, P]),
                                                ALU.mult).then_inc(ready, 1)
                    nc.gpsimd.tensor_copy(v1[:, u, :, 0:HD], qkv[:, u % 2, 2, :].rearrange("p (h d) -> p h d", d=HD)).then_inc(v_ready, 1)

            run_slots(pool, slot, B, LAG)

        @block.vector
        def _(dve):
            nc.vector.memset(pad[:, :], 0.0)
            rows = pad[:, :].rearrange("p (g r) -> p g r", g=GROUPS)

            def heads(t):
                return t.rearrange("p (g j) -> p g j", g=GROUPS)

            def slot(sl):
                if at := sl.step(0):
                    s, u = at
                    wait(dve, xT_ps, s - 1)
                    nc.vector.tensor_scalar(xn[:, u % 2, :], c.x[:, s, :], c.mean[:, bass.ds(s, 1)], c.rstd[:, bass.ds(s, 1)],
                                            ALU.subtract, ALU.mult).then_inc(xn_ready, 1)
                if at := sl.step(2):
                    s, u = at
                    for g in range(GROUPS):
                        dve.wait_ge(nat_ps, s * GROUPS + g + 1)
                        nc.vector.tensor_reduce(nmax[:, GROUP * g:GROUP * g + GROUP],
                                                ps_n[g % 2][:, :].rearrange("p (t k) -> p t k", t=GROUP),
                                                AX.X, ALU.max, negate=True).then_inc(max_done, 1)
                    dve.wait_ge(max_done, (s + 1) * GROUPS)
                    left = nmax[:, :]
                    for n in range(2):
                        nc.vector.tensor_copy(part[:, n, :], left).then_inc(own, 1)
                        dve.wait_ge(own, 4 * s + 2 * n + 1)
                        nc.vector.tensor_copy(rows[:, :, GROUP * n:GROUP * n + GROUP], heads(part[:, n, :]))
                        nc.vector.tensor_tensor(rest[:, n, :], left, part[:, n, :], ALU.subtract).then_inc(own, 1)
                        left = rest[:, n, :]
                        dve.wait_ge(own, 4 * s + 2 * n + 2)
                    nc.vector.tensor_copy(rows[:, :, 2 * GROUP:3 * GROUP], heads(left)).then_inc(pad_ready, 1)
                if at := sl.step(4):
                    s, u = at
                    dve.wait_ge(z_ps, s + 1)
                    z = ps_z[:, :].rearrange("p (j g r) -> p g j r", j=GROUP, g=GROUPS)
                    nc.vector.reciprocal(heads(rz[:, :]), z[:, :, :, HD]).then_inc(rz_ready, 1)
                    dve.wait_ge(rz_ready, s + 1)
                    nc.vector.tensor_tensor(o[:, u % 2, :].rearrange("p (g j d) -> p g j d", g=GROUPS, j=GROUP), z[:, :, :, 0:HD],
                                            heads(rz[:, :]).unsqueeze(3).broadcast_to([P, GROUPS, GROUP, HD]),
                                            ALU.mult).then_inc(o_ready, 1)
                if at := sl.step(2):
                    s, u = at
                    dve.wait_ge(pad_ps, s + 1)
                    nc.vector.tensor_tensor(fold[:, u % 2, :, :], ps_f.unsqueeze(1).broadcast_to([P, GROUP, P]),
                                            c.block[:, GROUP:2 * GROUP].unsqueeze(2).broadcast_to([P, GROUP, P]),
                                            ALU.mult).then_inc(fold_ready, 1)
                if at := sl.step(5):
                    s, u = at
                    dve.wait_ge(y_ps, s + 1)
                    nc.vector.tensor_tensor(c.x[:, s, :], c.x[:, s, :], ps_y, ALU.add).then_inc(x_done, 1)
                    dve.wait_ge(x_done, s + 1)
                    nc.vector.bn_stats(c.stats[:, s, :], c.x[:, s, :])

            run_slots(dve, slot, B, LAG)


def wide_weights(c):
    nc = c.nc
    ctx, sb, ps, sem = stage_scope(c)
    with ctx:
        bank = [ps(f"bank{n}") for n in range(4)]
        tg = sb("tg", [P, 1])
        ready, copied, gated, done = sem("ready"), sem("copied"), sem("gated"), sem("done")
        block = ctx.enter_context(nc.Block())

        @block.tensor
        def _(pe):
            for h in range(HEADS):
                ins = nc.tensor.matmul(bank[h // 4][:, (h % 4) * P:(h % 4) * P + P], c.w["x0_k"][:, h, :], c.w["x0_q"][:, h, :],
                                       start=True, stop=True)
                if h % 4 == 3:
                    ins.then_inc(ready, 1)

        @block.scalar
        def _(act):
            nc.scalar.activation(tg[:, :], c.w["x0_gate"][:, :], ACT.Tanh).then_inc(gated, 1)
            for n in range(4):
                act.wait_ge(ready, n + 1)
                nc.scalar.activation(c.x0_a[:, 4 * n:4 * n + 4, :], bank[n][:, :].rearrange("p (h d) -> p h d", h=4),
                                     ACT.Copy).then_inc(copied, 1)

        @block.vector
        def _(dve):
            dve.wait_ge(gated, 1)
            nc.vector.tensor_scalar(c.x0_o[:, :, :], c.w["x0_out"][:, :, :], tg[:, 0:1], None, ALU.mult).then_inc(done, 1)
            nc.vector.tensor_scalar(c.x0_b[:, :], c.w["x0_bias"][:, :], tg[0:1, 0:1], None, ALU.mult).then_inc(done, 1)


def cross_attention_wide(c):
    nc, B = c.nc, c.B
    K = c.keys
    DH = 64
    PAIRS = HEADS // 2
    BATCHES = 4
    ctx, sb, ps, sem = stage_scope(c)
    with ctx:
        cx = sb("cx", [P, 2, K])
        xn = sb("xn", [P, 2, D])
        xT = sb("xT", [P, 2, P])
        uu = sb("uu", [P, 2, HEADS, BATCHES, K])
        v = sb("v", [K, 2, HEADS * DH])
        top = sb("top", [P, HEADS])
        z, rz = sb("z", [P, HEADS]), sb("rz", [P, HEADS])
        p = sb("p", [P, 4, HEADS, K])
        pT = sb("pT", [K, 2, HEADS, P])
        oT = sb("oT", [P, 2, PAIRS, P])

        ps_misc, ps_o = ps("ps_misc"), ps("ps_o")
        ps_x, ps_y = ps_misc[:, 0:P], ps_misc[:, P:2 * P]
        ps_u = [ps(f"ps_u{i}") for i in range(2)]
        ps_n = [ps(f"ps_n{i}") for i in range(2)]
        ps_t = [ps(f"ps_t{i}") for i in range(2)]

        names = ("xn_ready", "xT_ps", "xT_ready", "u_ps", "u_ready", "v_ps", "v_ready", "s_ps", "max_done", "d_ready",
                 "exp_done", "z_done", "rz_done", "p_ready", "pT_ps", "pT_ready", "o_ps", "oT_ready", "y_ps", "x_done", "cx_ready")
        (xn_ready, xT_ps, xT_ready, u_ps, u_ready, v_ps, v_ready, s_ps, max_done, d_ready,
         exp_done, z_done, rz_done, p_ready, pT_ps, pT_ready, o_ps, oT_ready, y_ps, x_done, cx_ready) = (sem(n) for n in names)
        block = ctx.enter_context(nc.Block())
        NORM, TURN, SCORE, WEIGH, SPREAD, VALUE, LAST = 2, 3, 4, 5, 6, 7, 8
        LAG, BODY = LAST, 2 * BATCHES

        def four(t, g):
            return t[:, 4 * g:4 * g + 4]

        def bank_heads(bank, rows=P, cols=K):
            return bank[0:rows, 0:4 * cols].rearrange("p (h k) -> p h k", h=4)

        @block.tensor
        def _(pe):
            def scores(at, g):
                s, u = at
                if g == 0:
                    pe.wait_ge(xT_ready, s + 1)
                    pe.wait_ge(u_ready, 4 * (s - u % 4 + 4))
                wait(pe, d_ready, 4 * s + g - 1)
                nc.tensor.matmul(ps_n[g % 2][:, 0:4 * K], xT[:, u % 2, :], four(uu[:, u // 4], g)[:, :, u % 4, :],
                                 start=True, stop=True).then_inc(s_ps, 1)

            def outputs(at, half):
                s, u = at
                if half == 0:
                    pe.wait_ge(pT_ready, (s + 1) * 4)
                    pe.wait_ge(v_ready, 2 * (s + 1))
                wait(pe, oT_ready, 2 * s + half)
                for n in range(PAIRS // 2):
                    for odd in range(2):
                        h = half * PAIRS + 2 * n + odd
                        ins = nc.tensor.matmul(ps_o[DH * odd:DH * odd + DH, n * P:n * P + P], v[:, u % 2, h * DH:h * DH + DH],
                                               pT[:, u % 2, h, :], start=True, stop=True)
                ins.then_inc(o_ps, 1)

            def transposes(at, g):
                s, u = at
                if g == 0:
                    pe.wait_ge(p_ready, s + 1)
                wait(pe, pT_ready, 4 * s + g - 1)
                for n in range(4):
                    ins = nc.tensor.transpose(ps_t[g % 2][0:K, n * P:n * P + P], p[:, u % 4, 4 * g + n, :], c.ident[:, :])
                ins.then_inc(pT_ps, 1)

            def slot(sl):
                scored, spread, valued = sl.step(SCORE), sl.step(SPREAD), sl.step(VALUE)
                if scored:
                    scores(scored, 0)
                    scores(scored, 1)
                if valued:
                    outputs(valued, 0)
                if at := sl.step(TURN):
                    s, u = at
                    pe.wait_ge(xn_ready, s + 1)
                    wait(pe, x_done, s + TURN - LAST)
                    nc.tensor.transpose(ps_x, xn[:, u % 2, :], c.ident[:, :]).then_inc(xT_ps, 1)
                if scored:
                    scores(scored, 2)
                if spread:
                    transposes(spread, 0)
                    transposes(spread, 1)
                if valued:
                    outputs(valued, 1)
                if scored:
                    scores(scored, 3)
                if spread:
                    transposes(spread, 2)
                    transposes(spread, 3)
                if at := sl.step(0):
                    s, u = at
                    for n in range(4):
                        if n < 2 and not (sl.fixed and s <= SPREAD):
                            pe.wait_ge(v_ready, 2 * (s - SPREAD - 1) + n + 1)
                        else:
                            wait(pe, u_ready, 4 * s + n - 1)
                        nc.tensor.matmul(ps_u[n % 2][:, 0:BATCHES * K], c.x0_a[:, 4 * (u % 4) + n, :],
                                         c.ctx[:, bass.ds(s - u % 4, BATCHES), :], start=True, stop=True).then_inc(u_ps, 1)
                if spread:
                    s, u = spread
                    pe.wait_ge(cx_ready, s + 1)
                    for half in range(2):
                        done = 4 * (s + SPREAD + 1) - 1 + half
                        pe.wait_ge(u_ready, min(done, 4 * B) if sl.fixed else done)
                        wait(pe, v_ready, 2 * (s - 1) + half + 1)
                        nc.tensor.matmul(ps_u[half][0:K, :], cx[:, u % 2, :], c.w["x0_v"][:, half * 512:half * 512 + 512],
                                         start=True, stop=True).then_inc(v_ps, 1)
                if at := sl.step(LAST):
                    s, u = at
                    pe.wait_ge(oT_ready, 2 * (s + 1))
                    turned = s + LAST - TURN + 1
                    wait(pe, xT_ready, min(turned, B) if sl.fixed else turned)
                    wait(pe, x_done, s)
                    nc.tensor.matmul(ps_y, c.ones_row[0:1, 0:P], c.x0_b[0:1, :], start=True, stop=False)
                    for n in range(PAIRS):
                        ins = nc.tensor.matmul(ps_y, oT[:, u % 2, n, :], c.x0_o[:, n, :], start=False, stop=n == PAIRS - 1)
                    ins.then_inc(y_ps, 1)

            run_slots(pe, slot, B, LAG, BODY)

        @block.scalar
        def _(act):
            def outputs(at, half):
                s, u = at
                act.wait_ge(o_ps, 2 * s + half + 1)
                if half == 0:
                    wait(act, y_ps, s - 1)
                nc.scalar.activation(oT[:, u % 2, 4 * half:4 * half + 4, :], ps_o[:, :].rearrange("p (n q) -> p n q", n=4),
                                     ACT.Copy).then_inc(oT_ready, 1)

            def transposed(at, groups):
                s, u = at
                for g in groups:
                    act.wait_ge(pT_ps, 4 * s + g + 1)
                    if g == 0:
                        wait(act, o_ps, 2 * (s - 1))
                    nc.scalar.activation(four(pT[:, u % 2], g), bank_heads(ps_t[g % 2], K, P), ACT.Copy).then_inc(pT_ready, 1)

            def slot(sl):
                spread, valued = sl.step(SPREAD), sl.step(VALUE)
                if valued:
                    outputs(valued, 0)
                if at := sl.step(TURN):
                    s, u = at
                    act.wait_ge(xT_ps, s + 1)
                    wait(act, s_ps, 4 * (s - 1))
                    nc.scalar.activation(xT[:, u % 2, :], ps_x, ACT.Identity, scale=c.w["x0_ln"][:, 0:1],
                                         bias=c.w["x0_ln"][:, 1:2]).then_inc(xT_ready, 1)
                if spread:
                    transposed(spread, (0, 1))
                if valued:
                    outputs(valued, 1)
                if spread:
                    transposed(spread, (2, 3))
                    s, u = spread
                    for half in range(2):
                        act.wait_ge(v_ps, 2 * s + half + 1)
                        wait(act, o_ps, 2 * (s - 1))
                        nc.scalar.activation(v[:, u % 2, half * 512:half * 512 + 512], ps_u[half][0:K, :], ACT.Copy).then_inc(v_ready, 1)
                if at := sl.step(SCORE):
                    s, u = at
                    act.wait_ge(d_ready, 4 * (s + 1))
                    nc.scalar.activation(p[:, u % 4, :, :], p[:, u % 4, :, :], ACT.Exp, scale=DH ** -0.5).then_inc(exp_done, 1)

            run_slots(act, slot, B, LAG, BODY)

        @block.gpsimd
        def _(pool):
            def slot(sl):
                if at := sl.step(WEIGH):
                    s, u = at
                    wait(pool, v_ps, 2 * (s - 1))
                    nc.gpsimd.tensor_copy(cx[:, u % 2, :], c.ctx[:, s, :]).then_inc(cx_ready, 1)
                    pool.wait_ge(rz_done, s + 1)
                    nc.gpsimd.tensor_tensor(p[:, u % 4, :, :], p[:, u % 4, :, :], rz[:, :].unsqueeze(2).broadcast_to([P, HEADS, K]),
                                            ALU.mult).then_inc(p_ready, 1)

            run_slots(pool, slot, B, LAG, BODY)

        @block.vector
        def _(dve):
            def differences(at, groups):
                s, u = at
                for g in groups:
                    dve.wait_ge(s_ps, 4 * s + g + 1)
                    if g == 0:
                        wait(dve, pT_ps, 4 * (s - 3))
                    nc.vector.tensor_reduce(four(top, g), bank_heads(ps_n[g % 2]), AX.X, ALU.max).then_inc(max_done, 1)
                    dve.wait_ge(max_done, 4 * s + g + 1)
                    nc.vector.tensor_tensor(four(p[:, u % 4], g), bank_heads(ps_n[g % 2]),
                                            four(top, g).unsqueeze(2).broadcast_to([P, 4, K]), ALU.subtract).then_inc(d_ready, 1)

            def slot(sl):
                scored = sl.step(SCORE)
                if scored:
                    differences(scored, (0, 1))
                if at := sl.step(WEIGH):
                    s, u = at
                    dve.wait_ge(exp_done, s + 1)
                    wait(dve, p_ready, s)
                    nc.vector.tensor_reduce(z[:, :], p[:, u % 4, :, :], AX.X, ALU.add).then_inc(z_done, 1)
                    dve.wait_ge(z_done, s + 1)
                    nc.vector.reciprocal(rz[:, :], z[:, :]).then_inc(rz_done, 1)
                if scored:
                    differences(scored, (2, 3))
                if at := sl.step(NORM):
                    s, u = at
                    wait(dve, xT_ps, s - 1)
                    nc.vector.tensor_scalar(xn[:, u % 2, :], c.x[:, s, :], c.mean[:, bass.ds(s, 1)], c.rstd[:, bass.ds(s, 1)],
                                            ALU.subtract, ALU.mult).then_inc(xn_ready, 1)
                if at := sl.step(0):
                    s, u = at
                    wait(dve, s_ps, 4 * (s - u % 4 - 4))
                    for n in range(4):
                        dve.wait_ge(u_ps, 4 * s + n + 1)
                        nc.vector.tensor_copy(uu[:, u // 4, 4 * (u % 4) + n, :, :],
                                              ps_u[n % 2][:, 0:BATCHES * K].rearrange("p (b k) -> p b k", b=BATCHES)).then_inc(u_ready, 1)
                if at := sl.step(LAST):
                    s, u = at
                    dve.wait_ge(y_ps, s + 1)
                    nc.vector.tensor_tensor(c.x[:, s, :], c.x[:, s, :], ps_y, ALU.add).then_inc(x_done, 1)
                    dve.wait_ge(x_done, s + 1)
                    nc.vector.bn_stats(c.stats[:, s, :], c.x[:, s, :])

            run_slots(dve, slot, B, LAG, BODY)


def top_two(c, dve, own, base, score, sel, gt, ge, rank, tri, out):
    nc = c.nc
    T, E = score.shape[1], score.shape[2]
    other = score.unsqueeze(2).broadcast_to([P, T, E, E])
    mine = score.unsqueeze(3).broadcast_to([P, T, E, E])
    behind, ahead = (tri[:, n, :, :].unsqueeze(1).broadcast_to([P, T, E, E]) for n in range(2))
    nc.vector.tensor_tensor(gt, other, mine, ALU.is_gt)
    nc.vector.tensor_tensor(ge, other, mine, ALU.is_ge).then_inc(own, 1)
    dve.wait_ge(own, base + 1)
    nc.vector.tensor_tensor(gt, gt, behind, ALU.mult)
    nc.vector.tensor_tensor(ge, ge, ahead, ALU.mult).then_inc(own, 1)
    dve.wait_ge(own, base + 2)
    nc.vector.tensor_tensor(gt, gt, ge, ALU.add).then_inc(own, 1)
    dve.wait_ge(own, base + 3)
    nc.vector.tensor_reduce(rank, gt, AX.X, ALU.add).then_inc(own, 1)
    dve.wait_ge(own, base + 4)
    return nc.vector.scalar_tensor_tensor(out=out, in0=rank, scalar=2.0, in1=sel, op0=ALU.is_lt, op1=ALU.mult)


def scored_experts(c):
    nc = c.nc
    T = 4
    N = T * P
    steps = c.B // T
    E, H = 8, 352
    CH = [P, P, H - 2 * P]
    ctx, sb, ps, sem = stage_scope(c)
    with ctx:
        w_hi = [sb(f"w{n}_hi", [D, E * H], F32R) for n in range(2)]
        w_lo = [sb(f"w{n}_lo", [D, E * H], F32R) for n in range(2)]
        w3 = sb("w3", [P, E, 3, D])
        raw_in, w3_in, split_hi, split_lo = sem("raw_in0"), sem("w3_in"), sem("split_hi"), sem("split_lo")
        raw_in2 = sem("raw_in1")
        with nc.sbuf_tensor("f0_raw", [D, 2, E * H], F32) as raw, nc.Block() as block:
            @block.sync
            def _(sp):
                for n, (name, arrived) in enumerate((("late_f0_1", raw_in), ("late_f0_2", raw_in2))):
                    sp.dma_start(raw[:, n, :], c.inp[name]).then_inc(arrived, 16)
                sp.dma_start(w3[:, :, :, :], c.inp["late_f0_3"]).then_inc(w3_in, 16)
                sp.wait_ge(w3_in, 16)

            @block.scalar
            def _(act):
                for n, arrived in enumerate((raw_in, raw_in2)):
                    act.wait_ge(arrived, 16)
                    nc.scalar.activation(w_hi[n][:, :], raw[:, n, :], ACT.Copy).then_inc(split_hi, 1)

            @block.vector
            def _(dve):
                for n in range(2):
                    dve.wait_ge(split_hi, n + 1)
                    nc.vector.tensor_tensor(w_lo[n][:, :], raw[:, n, :], w_hi[n][:, :].bitcast(F32), ALU.subtract).then_inc(split_lo, 1)
                dve.wait_ge(split_lo, 2)

        xn = sb("xn", [P, 2, T, D])
        xT = sb("xT", [D, N])
        x_hi, x_lo = sb("x_hi", [D, 2, N], F32R), sb("x_lo", [D, 2, N], F32R)
        sg = sb("sg", [P, 2, N])
        act_in = sb("act", [P, 2, 3, N])
        sc, rank, wt = sb("sc", [P, T, E]), sb("rank", [P, T, E]), sb("wt", [P, 2, T, E])
        gt, ge = sb("gt", [P, T, E, E]), sb("ge", [P, T, E, E])

        ps_g, ps_u, ps_y = ([ps(f"ps_{n}{i}") for i in range(2)] for n in "guy")
        ps_x, ps_r = ps("ps_x"), ps("ps_r")
        names = ("xn_ready", "xT_ps", "xT_ready", "hi_ready", "lo_ready", "r_ps", "sc_ready", "own", "w_ready",
                 "g_ps", "u_ps", "sg_ready", "act_ready", "y_ps", "y_taken", "stats_done")
        (xn_ready, xT_ps, xT_ready, hi_ready, lo_ready, r_ps, sc_ready, own, w_ready,
         g_ps, u_ps, sg_ready, act_ready, y_ps, y_taken, stats_done) = (sem(n) for n in names)
        block = ctx.enter_context(nc.Block())
        LAG, TURN = 2, 4
        NCH = 3 * E
        x4 = c.x[:, :, :].rearrange("p (s i) d -> p s i d", i=T)
        st4 = c.stats[:, :, :].rearrange("p (s i) k -> p s i k", i=T)
        mean4 = c.mean[:, :].rearrange("p (s i) -> p s i", i=T)
        rstd4 = c.rstd[:, :].rearrange("p (s i) -> p s i", i=T)

        @block.tensor
        def _(pe):
            def hidden(at, e):
                s, u = at
                if e == 0:
                    pe.wait_ge(hi_ready, s + 1)
                    pe.wait_ge(lo_ready, s + 1)
                for k, m in enumerate(CH):
                    n = 3 * e + k
                    cols = slice(e * H + k * P, e * H + k * P + m)
                    for w, bank, taken, ready in ((0, ps_g, sg_ready, g_ps), (1, ps_u, act_ready, u_ps)):
                        wait(pe, taken, s * NCH + n - 1)
                        out = bank[n % 2][0:m, :]
                        nc.tensor.matmul(out, w_hi[w][:, cols], x_hi[:, u % 2, :], start=True, stop=False)
                        nc.tensor.matmul(out, w_hi[w][:, cols], x_lo[:, u % 2, :], start=False, stop=False)
                        nc.tensor.matmul(out, w_lo[w][:, cols], x_hi[:, u % 2, :], start=False, stop=True).then_inc(ready, 1)

            def down(at, e):
                s, u = at
                pe.wait_ge(act_ready, s * NCH + 3 * e + 3)
                wait(pe, y_taken, s * E + e - 1)
                for i in range(T):
                    for k, m in enumerate(CH):
                        ins = nc.tensor.matmul(ps_y[e % 2][:, i * P:i * P + P], act_in[0:m, e % 2, k, i * P:i * P + P],
                                               w3[0:m, e, k, :], start=k == 0, stop=k == 2)
                ins.then_inc(y_ps, 1)

            def transposes(at):
                s, u = at
                pe.wait_ge(xn_ready, s + 1)
                wait(pe, lo_ready, s)
                for i in range(T):
                    ins = nc.tensor.transpose(ps_x[:, i * P:i * P + P], xn[:, u % 2, i, :], c.ident[:, :])
                ins.then_inc(xT_ps, 1)

            def router(at):
                s, u = at
                pe.wait_ge(xT_ready, s + 1)
                wait(pe, sc_ready, s)
                for i in range(T):
                    ins = nc.tensor.matmul(ps_r[:, i * E:i * E + E], xT[:, i * P:i * P + P], c.w["f0_router"][:, :],
                                           start=True, stop=True)
                ins.then_inc(r_ps, 1)

            def slot(sl):
                main, ahead = sl.step(2), sl.step(1)
                for e in range(E):
                    if main:
                        hidden(main, e)
                        if e:
                            down(main, e - 1)
                    if ahead and e == TURN:
                        transposes(ahead)
                    if ahead and e == TURN + 2:
                        router(ahead)
                if main:
                    down(main, E - 1)

            run_slots(pe, slot, steps, LAG, 2)

        @block.scalar
        def _(act):
            def slot(sl):
                main, ahead = sl.step(2), sl.step(1)
                for e in range(E):
                    if main:
                        s, u = main
                        for k, m in enumerate(CH):
                            n = 3 * e + k
                            act.wait_ge(g_ps, s * NCH + n + 1)
                            wait(act, act_ready, s * NCH + n - 1)
                            nc.scalar.activation(sg[0:m, n % 2, :], ps_g[n % 2][0:m, :], ACT.Silu).then_inc(sg_ready, 1)
                    if ahead and e == TURN:
                        s, u = ahead
                        act.wait_ge(xT_ps, s + 1)
                        wait(act, r_ps, s)
                        nc.scalar.activation(xT[:, :], ps_x[:, :], ACT.Copy).then_inc(xT_ready, 1)
                        nc.scalar.activation(x_hi[:, u % 2, :], ps_x[:, :], ACT.Copy).then_inc(hi_ready, 1)

            run_slots(act, slot, steps, LAG, 2)

        @block.vector
        def _(dve):
            def add(at, e):
                s, u = at
                dve.wait_ge(y_ps, s * E + e + 1)
                wait(dve, y_taken, s * E + e)
                for i in range(T):
                    ins = nc.vector.scalar_tensor_tensor(out=x4[:, s, i, :], in0=ps_y[e % 2][:, i * P:i * P + P],
                                                         scalar=wt[:, u % 2, i, e:e + 1], in1=x4[:, s, i, :],
                                                         op0=ALU.mult, op1=ALU.add)
                ins.then_inc(y_taken, 1)

            def slot(sl):
                if at := sl.step(0):
                    s, u = at
                    wait(dve, xT_ps, s - 1)
                    for i in range(T):
                        ins = nc.vector.tensor_scalar(xn[:, u % 2, i, :], x4[:, s, i, :], mean4[:, s, i:i + 1], rstd4[:, s, i:i + 1],
                                                      ALU.subtract, ALU.mult)
                    ins.then_inc(xn_ready, 1)
                main, ahead = sl.step(2), sl.step(1)
                for e in range(E):
                    if main:
                        s, u = main
                        if e == 0:
                            dve.wait_ge(w_ready, s + 1)
                        for k, m in enumerate(CH):
                            n = 3 * e + k
                            dve.wait_ge(sg_ready, s * NCH + n + 1)
                            dve.wait_ge(u_ps, s * NCH + n + 1)
                            if k == 0:
                                wait(dve, y_ps, s * E + e - 1)
                            nc.vector.tensor_tensor(act_in[0:m, e % 2, k, :], sg[0:m, n % 2, :], ps_u[n % 2][0:m, :],
                                                    ALU.mult).then_inc(act_ready, 1)
                        if e:
                            add(main, e - 1)
                    if ahead and e == TURN:
                        s, u = ahead
                        dve.wait_ge(hi_ready, s + 1)
                        nc.vector.tensor_tensor(x_lo[:, u % 2, :], ps_x[:, :], x_hi[:, u % 2, :].bitcast(F32),
                                                ALU.subtract).then_inc(lo_ready, 1)
                    if ahead and e == TURN + 2:
                        s, u = ahead
                        dve.wait_ge(r_ps, s + 1)
                        nc.vector.tensor_copy(sc[:, :, :], ps_r[:, 0:T * E].rearrange("p (i e) -> p i e", i=T)).then_inc(sc_ready, 1)
                        dve.wait_ge(sc_ready, s + 1)
                        top_two(c, dve, own, 4 * s, sc[:, :, :], sc[:, :, :], gt[:, :, :, :], ge[:, :, :, :], rank[:, :, :],
                                c.w["tri8"][:, :, :, :], wt[:, u % 2, :, :]).then_inc(w_ready, 1)
                if main:
                    add(main, E - 1)
                    s, u = main
                    dve.wait_ge(y_taken, (s + 1) * E)
                    for i in range(T):
                        nc.vector.bn_stats(st4[:, s, i, :], x4[:, s, i, :])

            run_slots(dve, slot, steps, LAG, 2)


def attention_over_heads(c):
    nc, B = c.nc, c.B
    A = P // HEADS
    ctx, sb, ps, sem = stage_scope(c)
    with ctx:
        xn, xT = sb("xn", [P, 2, D]), sb("xT", [P, 2, P])
        qkv = sb("qkv", [P, UNROLL, 3, HEADS, HD])
        qk = sb("qk", [P, 2, HD, HEADS, HEADS])
        top, dif = sb("top", [P, HEADS]), sb("dif", [P, 2, HEADS, HEADS])
        e = sb("e", [P, 2, HEADS, HEADS])
        z, rz = sb("z", [P, HEADS]), sb("rz", [P, HEADS])
        ev = sb("ev", [P, HEADS, HD, HEADS])
        sums, o = sb("sums", [P, HEADS, HD]), sb("o", [P, 2, HEADS, HD])
        r = sb("r", [P, 2, HD, HEADS, A])
        ps_x, ps_qkv, ps_y = ps("ps_x"), ps("ps_qkv"), ps("ps_y")
        ps_s = [ps(f"ps_s{i}") for i in range(2)]
        names = ("xn_ready", "xT_ps", "xT_ready", "qkv_ps", "qkv_ready", "qk_ready", "s_ps", "top_done", "dif_ready", "exp_done",
                 "z_done", "rz_done", "ev_low", "ev_done", "sums_done", "o_ready", "r_ready", "y_ps", "x_done")
        (xn_ready, xT_ps, xT_ready, qkv_ps, qkv_ready, qk_ready, s_ps, top_done, dif_ready, exp_done,
         z_done, rz_done, ev_low, ev_done, sums_done, o_ready, r_ready, y_ps, x_done) = (sem(n) for n in names)
        block = ctx.enter_context(nc.Block())
        TURN, PROJECT, MULTIPLY, SCORE, WEIGH, SPREAD, LAST = 1, 2, 3, 4, 5, 6, 7
        LAG = LAST
        full = [P, HD, HEADS, HEADS]
        LOW = 4

        def weighted(eng, u, first, last):
            n = [P, last - first, HD, HEADS]
            return eng.tensor_tensor(ev[:, first:last, :, :], e[:, u % 2, first:last, :].unsqueeze(2).broadcast_to(n),
                                     qkv[:, u, 2, :, :].rearrange("p h d -> p d h").unsqueeze(1).broadcast_to(n), ALU.mult)

        @block.tensor
        def _(pe):
            def slot(sl):
                if at := sl.step(SCORE):
                    s, u = at
                    pe.wait_ge(qk_ready, s + 1)
                    wait(pe, dif_ready, s - 1)
                    for k in range(HD):
                        ins = nc.tensor.matmul(ps_s[u % 2][:, 0:HEADS * HEADS], c.ident[:, :], qk[:, u % 2, k, :, :],
                                               start=k == 0, stop=k == HD - 1)
                    ins.then_inc(s_ps, 1)
                if at := sl.step(TURN):
                    s, u = at
                    pe.wait_ge(xn_ready, s + 1)
                    wait(pe, xT_ready, s)
                    nc.tensor.transpose(ps_x[:, 0:P], xn[:, u % 2, :], c.ident[:, :]).then_inc(xT_ps, 1)
                if at := sl.step(PROJECT):
                    s, u = at
                    pe.wait_ge(xT_ready, s + 1)
                    wait(pe, qkv_ready, s)
                    nc.tensor.matmul(ps_qkv[:, 0:3 * D], xT[:, u % 2, :], c.w["a1_qkv"][:, :], start=True, stop=True).then_inc(qkv_ps, 1)
                if at := sl.step(LAST):
                    s, u = at
                    pe.wait_ge(r_ready, s + 1)
                    wait(pe, x_done, s)
                    nc.tensor.matmul(ps_y[:, 0:D], c.ones_row[0:1, 0:P], c.w["a1_b"][0:1, :], start=True, stop=False)
                    for k in range(HD):
                        ins = nc.tensor.matmul(ps_y[:, 0:D], r[:, u % 2, k, :, :], c.w["a1_o"][:, k, :], start=False, stop=k == HD - 1)
                    ins.then_inc(y_ps, 1)

            run_slots(pe, slot, B, LAG)

        @block.scalar
        def _(act):
            def slot(sl):
                if at := sl.step(TURN):
                    s, u = at
                    act.wait_ge(xT_ps, s + 1)
                    wait(act, qkv_ps, s - 1)
                    nc.scalar.activation(xT[:, u % 2, :], ps_x[:, 0:P], ACT.Copy).then_inc(xT_ready, 1)
                if at := sl.step(PROJECT):
                    s, u = at
                    act.wait_ge(qkv_ps, s + 1)
                    wait(act, ev_done, s - 3)
                    wait(act, ev_low, s - 3)
                    nc.scalar.activation(qkv[:, u, :, :, :], ps_qkv[:, 0:3 * D].rearrange("p (n h d) -> p n h d", n=3, h=HEADS),
                                         ACT.Copy).then_inc(qkv_ready, 1)
                if at := sl.step(SPREAD):
                    s, u = at
                    act.wait_ge(o_ready, s + 1)
                    wait(act, y_ps, s - 1)
                    for a in range(A):
                        ins = nc.scalar.activation(r[:, u % 2, :, :, a], o[:, u % 2, :, :].rearrange("p h d -> p d h"), ACT.Copy,
                                                   scale=c.w["a1_rows"][:, a:a + 1])
                    ins.then_inc(r_ready, 1)
                if at := sl.step(SCORE):
                    s, u = at
                    act.wait_ge(dif_ready, s + 1)
                    wait(act, ev_done, s - 1)
                    wait(act, ev_low, s - 1)
                    nc.scalar.activation(e[:, u % 2, :, :], dif[:, u % 2, :, :], ACT.Exp, scale=HD ** -0.5).then_inc(exp_done, 1)

            run_slots(act, slot, B, LAG)

        @block.gpsimd
        def _(pool):
            def slot(sl):
                if at := sl.step(WEIGH):
                    s, u = at
                    pool.wait_ge(exp_done, s + 1)
                    wait(pool, sums_done, s)
                    weighted(nc.gpsimd, u, 0, LOW).then_inc(ev_low, 1)
                if at := sl.step(MULTIPLY):
                    s, u = at
                    pool.wait_ge(qkv_ready, s + 1)
                    wait(pool, s_ps, s - 1)
                    nc.gpsimd.tensor_tensor(qk[:, u % 2, :, :, :], qkv[:, u, 0, :, :].rearrange("p h d -> p d h").unsqueeze(3).broadcast_to(full),
                                            qkv[:, u, 1, :, :].rearrange("p h d -> p d h").unsqueeze(2).broadcast_to(full), ALU.mult).then_inc(qk_ready, 1)

            run_slots(pool, slot, B, LAG)

        @block.vector
        def _(dve):
            def slot(sl):
                if at := sl.step(0):
                    s, u = at
                    wait(dve, xT_ps, s - 1)
                    nc.vector.tensor_scalar(xn[:, u % 2, :], c.x[:, s, :], c.mean[:, bass.ds(s, 1)], c.rstd[:, bass.ds(s, 1)],
                                            ALU.subtract, ALU.mult).then_inc(xn_ready, 1)
                if at := sl.step(WEIGH):
                    s, u = at
                    dve.wait_ge(exp_done, s + 1)
                    wait(dve, o_ready, s)
                    nc.vector.tensor_reduce(z[:, :], e[:, u % 2, :, :], AX.X, ALU.add).then_inc(z_done, 1)
                    weighted(nc.vector, u, LOW, HEADS).then_inc(ev_done, 1)
                    dve.wait_ge(z_done, s + 1)
                    nc.vector.reciprocal(rz[:, :], z[:, :]).then_inc(rz_done, 1)
                    dve.wait_ge(ev_done, s + 1)
                    dve.wait_ge(ev_low, s + 1)
                    nc.vector.tensor_reduce(sums[:, :, :], ev[:, :, :, :], AX.X, ALU.add).then_inc(sums_done, 1)
                    dve.wait_ge(rz_done, s + 1)
                    dve.wait_ge(sums_done, s + 1)
                    wait(dve, r_ready, s - 1)
                    nc.vector.tensor_tensor(o[:, u % 2, :, :], sums[:, :, :], rz[:, :].unsqueeze(2).broadcast_to([P, HEADS, HD]),
                                            ALU.mult).then_inc(o_ready, 1)
                if at := sl.step(SCORE):
                    s, u = at
                    dve.wait_ge(s_ps, s + 1)
                    score = ps_s[u % 2][:, 0:HEADS * HEADS].rearrange("p (i j) -> p i j", i=HEADS)
                    nc.vector.tensor_reduce(top[:, :], score, AX.X, ALU.max).then_inc(top_done, 1)
                    dve.wait_ge(top_done, s + 1)
                    wait(dve, exp_done, s - 1)
                    nc.vector.tensor_tensor(dif[:, u % 2, :, :], score, top[:, :].unsqueeze(2).broadcast_to([P, HEADS, HEADS]),
                                            ALU.subtract).then_inc(dif_ready, 1)
                if at := sl.step(LAST):
                    s, u = at
                    dve.wait_ge(y_ps, s + 1)
                    nc.vector.tensor_tensor(c.x[:, s, :], c.x[:, s, :], ps_y[:, 0:D], ALU.add).then_inc(x_done, 1)
                    dve.wait_ge(x_done, s + 1)
                    nc.vector.bn_stats(c.stats[:, s, :], c.x[:, s, :])

            run_slots(dve, slot, B, LAG)


def cross_attention_tempered(c):
    B = c.B
    c.stage = "x1"
    ctx, sb, ps, sem = stage_scope(c)
    with ctx:
        c.t_max, c.t_z, c.t_sq = (sb(n, [P, B, HEADS]) for n in ("t_max", "t_z", "t_sq"))
        c.t_q, c.t_k = sb("t_q", [P, B]), sb("t_k", [P, B])
        c.t_g, c.t_qb = sb("t_g", [P, B]), sb("t_qb", [P, B])
        c.stage = "x1s"
        tempered_pass(c, False)
        c.stage = "x1t"
        temperatures(c)
        c.stage = "x1a"
        tempered_pass(c, True)


def temperatures(c):
    nc, B = c.nc, c.B
    N = B * HEADS
    COLS = min(N, 512)
    parts = N // COLS
    H = c.w["x1_w2"].shape[0]
    ctx, sb, ps, sem = stage_scope(c)
    with ctx:
        z2, rec, ent, prod = sb("z2", [P, N]), sb("rec", [P, N]), sb("ent", [P, N]), sb("prod", [P, B])
        sims = sb("sims", [P, B, HEADS])
        feats = sb("feats", [3, N])
        h1, h2 = sb("h1", [H, N]), sb("h2", [H, N])
        own_t = sb("own_t", [P, B, HEADS])
        lt, t = sb("lt", [P, B]), sb("t", [P, B])
        bank = [ps(f"bank{n}") for n in range(parts)]
        last = [ps(f"last{n}") for n in range(parts)]
        dv, in_ready, f_ps, f_ready, h_ps, h_ready, t_ps, lt_ready, t_ready = (
            sem(n) for n in ("dv", "in_ready", "f_ps", "f_ready", "h_ps", "h_ready", "t_ps", "lt_ready", "t_ready"))
        block = ctx.enter_context(nc.Block())
        flat = lambda tile: tile[:, :, :].rearrange("p b h -> p (b h)")
        head_mask = c.w["x1_heads"][:, :].unsqueeze(1).broadcast_to([P, B, HEADS])
        cols = lambda n: slice(n * COLS, n * COLS + COLS)

        @block.vector
        def _(dve):
            n_own = [0]

            def own(ins):
                n_own[0] += 1
                ins.then_inc(dv, 1)
                dve.wait_ge(dv, n_own[0])

            own(nc.vector.tensor_tensor(prod[:, :], c.t_q[:, :], c.t_k[:, :], ALU.mult))
            own(nc.vector.tensor_tensor(sims[:, :, :], prod[:, :].unsqueeze(2).broadcast_to([P, B, HEADS]), head_mask, ALU.mult))
            own(nc.vector.tensor_tensor(z2[:, :], flat(c.t_z), flat(c.t_z), ALU.mult))
            own(nc.vector.reciprocal(rec[:, :], z2[:, :]))
            nc.vector.tensor_tensor(ent[:, :], rec[:, :], flat(c.t_sq), ALU.mult).then_inc(in_ready, 1)
            for n in range(parts):
                dve.wait_ge(t_ps, n + 1)
                b = COLS // HEADS
                own(nc.vector.tensor_tensor(own_t[:, n * b:n * b + b, :], last[n][:, 0:COLS].rearrange("p (b h) -> p b h", h=HEADS),
                                            c.w["x1_heads"][:, :].unsqueeze(1).broadcast_to([P, b, HEADS]), ALU.mult))
            own(nc.vector.tensor_reduce(lt[:, :], own_t[:, :, :], AX.X, ALU.add))
            own(nc.vector.tensor_scalar(t[:, :], lt[:, :], c.w["x1_b3"][:, 0:1], float(np.log(0.1)), ALU.add, ALU.max))
            nc.vector.tensor_scalar(lt[:, :], t[:, :], float(np.log(10.0)), None, ALU.min).then_inc(lt_ready, 1)
            dve.wait_ge(t_ready, 1)
            own(nc.vector.tensor_scalar(lt[:, :], t[:, :], 2.0, None, ALU.mult))
            own(nc.vector.reciprocal(c.t_g[:, :], lt[:, :]))
            own(nc.vector.tensor_scalar(c.t_qb[:, :], c.t_g[:, :], c.w["x1_bias"][:, 0:1], None, ALU.mult))

        @block.tensor
        def _(pe):
            pe.wait_ge(in_ready, 1)
            for n in range(parts):
                for k, data in enumerate((flat(sims), flat(c.t_max), ent[:, :])):
                    nc.tensor.matmul(bank[n][0:3, 0:COLS], c.w["x1_pick"][:, 3 * k:3 * k + 3], data[:, cols(n)],
                                     start=k == 0, stop=False)
                nc.tensor.matmul(bank[n][0:3, 0:COLS], c.w["x1_less"][0:1, :], c.ones_row[0:1, 0:COLS],
                                 start=False, stop=True).then_inc(f_ps, 1)
            for layer, (wt, src, dst, ready) in enumerate((("x1_w1", feats, bank, f_ready), ("x1_w2", h1, bank, h_ready))):
                for n in range(parts):
                    pe.wait_ge(ready, parts if ready is f_ready else n + 1)
                    nc.tensor.matmul(dst[n][0:H, 0:COLS], c.w[wt][:, :], src[:, cols(n)], start=True, stop=True).then_inc(h_ps, 1)
            for n in range(parts):
                pe.wait_ge(h_ready, parts + n + 1)
                nc.tensor.matmul(last[n][:, 0:COLS], c.w["x1_w3"][:, :], h2[:, cols(n)], start=True, stop=True).then_inc(t_ps, 1)

        @block.scalar
        def _(act):
            for n in range(parts):
                act.wait_ge(f_ps, n + 1)
                nc.scalar.activation(feats[:, cols(n)], bank[n][0:3, 0:COLS], ACT.Copy).then_inc(f_ready, 1)
            for layer, (dst, col) in enumerate(((h1, 0), (h2, 1))):
                for n in range(parts):
                    act.wait_ge(h_ps, layer * parts + n + 1)
                    nc.scalar.activation(dst[:, cols(n)], bank[n][0:H, 0:COLS], ACT.Gelu,
                                         bias=c.w["x1_mlp_b"][:, col:col + 1]).then_inc(h_ready, 1)
            act.wait_ge(lt_ready, 1)
            nc.scalar.activation(t[:, :], lt[:, :], ACT.Exp).then_inc(t_ready, 1)


def tempered_pass(c, final):
    nc, B = c.nc, c.B
    K = c.keys
    ctx, sb, ps, sem = stage_scope(c)
    with ctx:
        cx = sb("cx", [P, UNROLL, K])
        xn = sb("xn", [P, 2, D])
        xT = sb("xT", [P, 2, P])
        qT, kT = sb("qT", [P, 2, P]), sb("kT", [P, 2, K])
        k_bd = sb("k_bd", [P, 2, GROUP, K])
        nmax = sb("nmax", [P, HEADS])
        d = sb("d", [P, 2, HEADS, K])
        e = sb("e", [P, 2, HEADS, K])
        sq = sb("sq", [P, 2, HEADS, K])
        if final:
            v_bd = sb("v_bd", [K, UNROLL, GROUPS, GROUP, STRIP])
            z, rz = sb("z", [P, HEADS]), sb("rz", [P, HEADS])
            pT = sb("pT", [K, 2, HEADS, P])
            oT = sb("oT", [P, 2, P])
        ps_x, ps_qk = ps("ps_x"), ps("ps_qk")
        ps_n = [ps(f"ps_n{i}") for i in range(2)]
        if final:
            ps_t = [ps(f"ps_t{i}") for i in range(2)]
            ps_o, ps_y = ps("ps_o"), ps("ps_y")
        names = ("xn_ready", "xT_ps", "xT_ready", "qk_ps", "qk_ready", "k_bd_ready", "made", "s_ps", "max_done", "d_ready",
                 "exp_done", "z_done", "rz_done", "sq_ready", "sq_done", "pT_ps", "pT_ready", "o_ps", "oT_ready", "y_ps",
                 "x_done", "cx_ready", "sums_done")
        (xn_ready, xT_ps, xT_ready, qk_ps, qk_ready, k_bd_ready, made, s_ps, max_done, d_ready,
         exp_done, z_done, rz_done, sq_ready, sq_done, pT_ps, pT_ready, o_ps, oT_ready, y_ps,
         x_done, cx_ready, sums_done) = (sem(n) for n in names)
        block = ctx.enter_context(nc.Block())
        EVAC = 3 if final else 2

        def strip(g):
            return slice(STRIP * g, STRIP * g + STRIP)

        def four(t, g):
            return t[:, 4 * g:4 * g + 4]

        def bank_heads(bank, rows=P, cols=K):
            return bank[0:rows, 0:4 * cols].rearrange("p (h k) -> p h k", h=4)

        TURN, PROJECT, SCORE, WEIGH, SPREAD, VALUE, LAST = 1, 2, 3, 4, 5, 6, 7
        LAG = LAST if final else SPREAD

        @block.tensor
        def _(pe):
            def scores(at, g):
                s, u = at
                if g == 0:
                    pe.wait_ge(k_bd_ready, s + 1)
                wait(pe, d_ready, 4 * s + g - 1)
                nc.tensor.matmul(ps_n[g % 2][:, 0:4 * K], qT[strip(g), u % 2, :], k_bd[strip(g), u % 2, :, :],
                                 start=True, stop=True).then_inc(s_ps, 1)

            def transposes(at, g):
                s, u = at
                if g == 0:
                    pe.wait_ge(sq_ready, s + 1)
                wait(pe, pT_ready, 4 * s + g - 1)
                for n in range(4):
                    ins = nc.tensor.transpose(ps_t[g % 2][0:K, n * P:n * P + P], sq[:, u % 2, 4 * g + n, :], c.ident[:, :])
                ins.then_inc(pT_ps, 1)

            def slot(sl):
                scored, spread = sl.step(SCORE), sl.step(SPREAD) if final else None
                if scored:
                    scores(scored, 0)
                    scores(scored, 1)
                if at := sl.step(PROJECT):
                    s, u = at
                    pe.wait_ge(cx_ready, s + 1)
                    pe.wait_ge(xT_ready, s + 1)
                    wait(pe, qk_ready, EVAC * s)
                    nc.tensor.matmul(ps_qk[:, 0:P], c.w["x1_q"][:, :], xT[:, u % 2, :], start=True, stop=True)
                    ins = nc.tensor.matmul(ps_qk[:, P:P + K], c.w["x1_k"][:, :], cx[:, u, :], start=True, stop=True)
                    if final:
                        nc.tensor.matmul(ps_qk[0:K, 3 * P:4 * P], c.ones_row[0:1, 0:K], c.w["x1_bv"][0:1, :], start=True, stop=False)
                        ins = nc.tensor.matmul(ps_qk[0:K, 3 * P:4 * P], cx[:, u, :], c.w["x1_v"][:, :], start=False, stop=True)
                    ins.then_inc(qk_ps, 1)
                if final and (at := sl.step(VALUE)):
                    s, u = at
                    pe.wait_ge(pT_ready, 4 * (s + 1))
                    pe.wait_ge(qk_ready, EVAC * (s + 1))
                    wait(pe, oT_ready, s)
                    for j in range(GROUP):
                        for g in range(GROUPS):
                            ins = nc.tensor.matmul(ps_o[strip(g), 0:P], v_bd[:, u, g, j, :], pT[:, u % 2, GROUP * g + j, :],
                                                   start=j == 0, stop=j == GROUP - 1)
                    ins.then_inc(o_ps, 1)
                if at := sl.step(TURN):
                    s, u = at
                    pe.wait_ge(xn_ready, s + 1)
                    wait(pe, xT_ready, s)
                    nc.tensor.transpose(ps_x[:, 0:P], xn[:, u % 2, :], c.ident[:, :]).then_inc(xT_ps, 1)
                if scored:
                    scores(scored, 2)
                if spread:
                    transposes(spread, 0)
                    transposes(spread, 1)
                if scored:
                    scores(scored, 3)
                if spread:
                    transposes(spread, 2)
                    transposes(spread, 3)
                if final and (at := sl.step(LAST)):
                    s, u = at
                    pe.wait_ge(oT_ready, s + 1)
                    wait(pe, x_done, s)
                    nc.tensor.matmul(ps_y[:, 0:D], c.ones_row[0:1, 0:P], c.w["x1_bo"][0:1, :], start=True, stop=False)
                    nc.tensor.matmul(ps_y[:, 0:D], oT[:, u % 2, :], c.w["x1_o"][:, :], start=False, stop=True).then_inc(y_ps, 1)

            run_slots(pe, slot, B, LAG)

        @block.scalar
        def _(act):
            if final:
                act.wait_ge(made, 1)

            def slot(sl):
                if at := sl.step(PROJECT):
                    s, u = at
                    act.wait_ge(qk_ps, s + 1)
                    wait(act, k_bd_ready, s - 1)
                    wait(act, s_ps, 4 * (s - 1))
                    if not final:
                        wait(act, sums_done, s - 1)
                    q_bias, q_scale = c.w["x1_bias"][:, 0:1], 1.0
                    if final:
                        q_bias, q_scale = c.t_qb[:, bass.ds(s, 1)], c.t_g[:, bass.ds(s, 1)]
                    nc.scalar.activation(qT[:, u % 2, :], ps_qk[:, 0:P], ACT.Identity, scale=q_scale, bias=q_bias).then_inc(qk_ready, 1)
                    nc.scalar.activation(kT[:, u % 2, :], ps_qk[:, P:P + K], ACT.Identity,
                                         bias=c.w["x1_bias"][:, 1:2]).then_inc(qk_ready, 1)
                    if final:
                        wait(act, o_ps, s - 3)
                        for j in range(GROUP):
                            at_j = slice(HD * j, HD * j + HD)
                            ins = nc.scalar.activation(v_bd[:, u, :, j, at_j],
                                                       ps_qk[0:K, 3 * P:4 * P].rearrange("p (g r) -> p g r", g=GROUPS)[:, :, at_j], ACT.Copy)
                        ins.then_inc(qk_ready, 1)
                if final and (at := sl.step(VALUE)):
                    s, u = at
                    act.wait_ge(o_ps, s + 1)
                    wait(act, y_ps, s - 1)
                    nc.scalar.activation(oT[:, u % 2, :], ps_o[:, 0:P], ACT.Copy).then_inc(oT_ready, 1)
                if at := sl.step(TURN):
                    s, u = at
                    act.wait_ge(xT_ps, s + 1)
                    wait(act, qk_ps, s - 1)
                    nc.scalar.activation(xT[:, u % 2, :], ps_x[:, 0:P], ACT.Copy).then_inc(xT_ready, 1)
                spread = sl.step(SPREAD) if final else None

                def transposed(groups):
                    s, u = spread
                    for g in groups:
                        act.wait_ge(pT_ps, 4 * s + g + 1)
                        nc.scalar.activation(four(pT[:, u % 2], g), bank_heads(ps_t[g % 2], K, P), ACT.Copy).then_inc(pT_ready, 1)

                if spread:
                    transposed(range(4))
                if at := sl.step(SCORE):
                    s, u = at
                    act.wait_ge(d_ready, 4 * (s + 1))
                    wait(act, sq_ready, s - 1)
                    nc.scalar.activation(e[:, u % 2, :, :], d[:, u % 2, :, :], ACT.Exp,
                                         scale=1.0 if final else HD ** -0.5).then_inc(exp_done, 1)

            run_slots(act, slot, B, LAG)

        @block.gpsimd
        def _(pool):
            if final:
                nc.gpsimd.memset(v_bd[:, :, :, :, :], 0.0).then_inc(made, 1)

            def slot(sl):
                if at := sl.step(PROJECT):
                    s, u = at
                    pool.wait_ge(qk_ready, EVAC * (s + 1))
                    wait(pool, s_ps, 4 * (s - 1))
                    nc.gpsimd.tensor_tensor(k_bd[:, u % 2, :, :], kT[:, u % 2, :].unsqueeze(1).broadcast_to([P, GROUP, K]),
                                            c.block[:, 0:GROUP].unsqueeze(2).broadcast_to([P, GROUP, K]),
                                            ALU.mult).then_inc(k_bd_ready, 1)
                if at := sl.step(0):
                    s, u = at
                    wait(pool, qk_ps, s - 3)
                    nc.gpsimd.tensor_copy(cx[:, u, :], c.ctx[:, s, :]).then_inc(cx_ready, 1)
                if at := sl.step(WEIGH):
                    s, u = at
                    pool.wait_ge(rz_done if final else exp_done, s + 1)
                    wait(pool, pT_ps if final else sq_done, 4 * (s - 1) if final else s - 1)
                    other = rz[:, :].unsqueeze(2).broadcast_to([P, HEADS, K]) if final else e[:, u % 2, :, :]
                    nc.gpsimd.tensor_tensor(sq[:, u % 2, :, :], e[:, u % 2, :, :], other, ALU.mult).then_inc(sq_ready, 1)

            run_slots(pool, slot, B, LAG)

        @block.vector
        def _(dve):
            def slot(sl):
                if at := sl.step(0):
                    s, u = at
                    wait(dve, xT_ps, s - 1)
                    nc.vector.tensor_scalar(xn[:, u % 2, :], c.x[:, s, :], c.mean[:, bass.ds(s, 1)], c.rstd[:, bass.ds(s, 1)],
                                            ALU.subtract, ALU.mult).then_inc(xn_ready, 1)
                scored = sl.step(SCORE)

                def differences(groups):
                    s, u = scored
                    top = nmax[:, :] if final else c.t_max[:, s, :]
                    for g in groups:
                        dve.wait_ge(s_ps, 4 * s + g + 1)
                        nc.vector.tensor_reduce(four(top, g), bank_heads(ps_n[g % 2]), AX.X, ALU.max).then_inc(max_done, 1)
                        dve.wait_ge(max_done, 4 * s + g + 1)
                        nc.vector.tensor_tensor(four(d[:, u % 2], g), bank_heads(ps_n[g % 2]),
                                                four(top, g).unsqueeze(2).broadcast_to([P, 4, K]),
                                                ALU.subtract).then_inc(d_ready, 1)

                if scored:
                    wait(dve, exp_done, scored[0] - 1)
                    differences((0, 1))
                if at := sl.step(WEIGH):
                    s, u = at
                    dve.wait_ge(exp_done, s + 1)
                    if final:
                        wait(dve, sq_ready, s)
                    nc.vector.tensor_reduce(z[:, :] if final else c.t_z[:, s, :], e[:, u % 2, :, :], AX.X, ALU.add).then_inc(z_done, 1)
                    if final:
                        dve.wait_ge(z_done, s + 1)
                        nc.vector.reciprocal(rz[:, :], z[:, :]).then_inc(rz_done, 1)
                if scored:
                    differences((2, 3))
                if final and (at := sl.step(LAST)):
                    s, u = at
                    dve.wait_ge(y_ps, s + 1)
                    nc.vector.tensor_tensor(c.x[:, s, :], c.x[:, s, :], ps_y[:, 0:D], ALU.add).then_inc(x_done, 1)
                    dve.wait_ge(x_done, s + 1)
                    nc.vector.bn_stats(c.stats[:, s, :], c.x[:, s, :])
                if not final and (at := sl.step(SPREAD)):
                    s, u = at
                    dve.wait_ge(sq_ready, s + 1)
                    nc.vector.tensor_reduce(c.t_sq[:, s, :], sq[:, u % 2, :, :], AX.X, ALU.add).then_inc(sq_done, 1)
                if not final and (at := sl.step(SCORE)):
                    s, u = at
                    dve.wait_ge(qk_ready, 2 * (s + 1))
                    nc.vector.tensor_reduce(c.t_q[:, bass.ds(s, 1)], qT[:, u % 2, :], AX.X, ALU.add)
                    nc.vector.tensor_reduce(c.t_k[:, bass.ds(s, 1)], kT[:, u % 2, :], AX.X, ALU.add).then_inc(sums_done, 1)

            run_slots(dve, slot, B, LAG)


T6 = 4


def mixed_experts(c):
    nc, B = c.nc, c.B
    c.stage = "f1"
    ctx, sb, ps, sem = stage_scope(c)
    with ctx:
        c.f1_hi, c.f1_lo = sb("hi", [D, B, P], F32R), sb("lo", [D, B, P], F32R)
        c.f1_wt = sb("wt", [P, B, 4])
        c.f1 = {}
        late = [n for n in c.inp if n.startswith("late_f1_")]
        for name in late:
            c.f1[name[8:]] = sb(name, list(c.inp[name].shape))
        c.f1_me, c.f1_me_b = sb("me", [D, 2, D]), sb("me_b", [P, 2])
        c.f1_rows = {name: sb("row_" + name, [P, D]) for name in ("ce", "f2b", "genb", "c2b", "ml_b2")}
        c.f1_parts = {name: [sb(f"{name}_{part}", [D, n, P], F32R) for part in ("hi", "lo")]
                      for name, n in (("sw_1", 4), ("sw_3", 4), ("me", 2), ("ml_1", 4))}
        c.f1_ce, c.f1_ce_b = sb("ce", [D, D]), sb("ce_b", [1, D])
        arrived = sem("arrived")
        with nc.Block() as block:
            @block.sync
            def _(sp):
                for name in late:
                    tile = c.f1[name[8:]]
                    sp.dma_start(tile[(slice(None),) * len(c.inp[name].shape)], c.inp[name]).then_inc(arrived, 16)
                sp.wait_ge(arrived, 16 * len(late))
        c.stage = "f1w"
        chain_weights(c)
        c.stage = "f1r"
        route(c)
        f = c.f1
        c.stage = "f1a"
        hidden_expert(c, 0, ACT.Silu, "sw_1", "sw_3", None, f["sw_2"], None)
        c.stage = "f1b"
        hidden_expert(c, 1, ACT.Gelu, "me", None, c.f1_me_b, f["c2"], c.f1_rows["c2b"])
        c.stage = "f1d"
        hidden_expert(c, 3, ACT.Gelu, "ml_1", None, f["ml_b1"], f["ml_2"], c.f1_rows["ml_b2"])
        c.stage = "f1c"
        normed_expert(c, 2)


def chain_weights(c):
    nc, f = c.nc, c.f1
    ctx, sb, ps, sem = stage_scope(c)
    with ctx:
        m1, m2, mo = sb("m1", [D, 2 * D]), sb("m2", [D, 2 * D]), sb("mo", [D, D])
        col1, col2 = sb("col1", [P, 1]), sb("col2", [P, 1])
        pm, pv, po, pb = ps("pm"), ps("pv"), ps("po"), ps("pb")
        pr = [ps(f"pr{n}") for n in range(2)]
        m_ps, m_done, v_ps, v_done, o_ps, o_done, b_ps, b_done, r_ps, r_done, hi_done, lo_done = (
            sem(n) for n in ("m_ps", "m_done", "v_ps", "v_done", "o_ps", "o_done", "b_ps", "b_done", "r_ps", "r_done",
                             "hi_done", "lo_done"))
        row_of = (("f2b", f["f2b"]), ("genb", f["genb"]), ("c2b", f["c2b"]), ("ml_b2", f["ml_b2"]), ("ce", c.f1_ce_b))
        split = (("sw_1", f["sw_1"]), ("sw_3", f["sw_3"]), ("ml_1", f["ml_1"]), ("me", c.f1_me))
        block = ctx.enter_context(nc.Block())
        c1 = f["c1"][:, :, :].rearrange("p n d -> p (n d)")
        me = c.f1_me[:, :, :].rearrange("p n d -> p (n d)")

        @block.tensor
        def _(pe):
            for n, (left, right) in enumerate((("me_oT", c1), ("me_vT", m1[:, :]), ("me_eqT", m2[:, :]))):
                wait(pe, m_done, n)
                nc.tensor.matmul(pm[:, 0:2 * D], f[left][:, :], right, start=True, stop=True).then_inc(m_ps, 1)
            for n, (left, right) in enumerate((("me_v", f["cols"][:, 0:1]), ("me_o", col1[:, :]))):
                wait(pe, v_done, n)
                nc.tensor.matmul(pv[:, n:n + 1], f[left][:, :], right, start=True, stop=True).then_inc(v_ps, 1)
            pe.wait_ge(v_done, 2)
            for n in range(2):
                nc.tensor.matmul(pv[:, 2 + n:3 + n], f["c1"][:, n, :], col2[:, :], start=True, stop=True).then_inc(v_ps, 1)
            nc.tensor.matmul(po[:, 0:D], f["ce_vT"][:, :], f["ce_o"][:, :], start=True, stop=True).then_inc(o_ps, 1)
            pe.wait_ge(o_done, 1)
            nc.tensor.matmul(po[:, 0:D], f["ce_synT"][:, :], mo[:, :], start=True, stop=True).then_inc(o_ps, 1)
            nc.tensor.matmul(pb[0:1, 0:D], f["cols"][:, 3:4], mo[:, :], start=True, stop=False)
            nc.tensor.matmul(pb[0:1, 0:D], f["cols"][:, 4:5], f["ce_o"][:, :], start=False, stop=False)
            nc.tensor.matmul(pb[0:1, 0:D], c.ones_row[0:1, 0:1], f["ce_bo"][0:1, :], start=False, stop=True).then_inc(b_ps, 1)
            pe.wait_ge(b_done, 1)
            for n, (name, row) in enumerate(row_of):
                nc.tensor.matmul(pr[n // 4][:, (n % 4) * D:(n % 4) * D + D], c.ones_row[0:1, 0:P], row[0:1, :],
                                 start=True, stop=True).then_inc(r_ps, 1)

        @block.scalar
        def _(act):
            for n, out in enumerate((m1[:, :], m2[:, :], me)):
                act.wait_ge(m_ps, n + 1)
                nc.scalar.activation(out, pm[:, 0:2 * D], ACT.Copy).then_inc(m_done, 1)
            act.wait_ge(m_done, 3)
            for name, w in split:
                nc.scalar.activation(c.f1_parts[name][0][:, :, :], w[:, :, :], ACT.Copy).then_inc(hi_done, 1)

        @block.vector
        def _(dve):
            for n, out in enumerate((col1, col2)):
                dve.wait_ge(v_ps, n + 1)
                nc.vector.tensor_tensor(out[:, :], pv[:, n:n + 1], f["cols"][:, 1 + n:2 + n], ALU.add).then_inc(v_done, 1)
            dve.wait_ge(v_ps, 4)
            nc.vector.tensor_tensor(c.f1_me_b[:, :], pv[:, 2:4], f["c1b"][:, :], ALU.add).then_inc(v_done, 1)
            dve.wait_ge(o_ps, 1)
            nc.vector.tensor_tensor(mo[:, :], po[:, 0:D], c.ident[:, :], ALU.add).then_inc(o_done, 1)
            dve.wait_ge(o_ps, 2)
            nc.vector.tensor_copy(c.f1_ce[:, :], po[:, 0:D]).then_inc(o_done, 1)
            dve.wait_ge(b_ps, 1)
            nc.vector.tensor_copy(c.f1_ce_b[:, :], pb[0:1, 0:D]).then_inc(b_done, 1)
            dve.wait_ge(r_ps, len(row_of))
            for n, (name, row) in enumerate(row_of):
                nc.vector.tensor_copy(c.f1_rows[name][:, :], pr[n // 4][:, (n % 4) * D:(n % 4) * D + D]).then_inc(r_done, 1)
            for n, (name, w) in enumerate(split):
                dve.wait_ge(hi_done, n + 1)
                hi, lo = c.f1_parts[name]
                nc.vector.tensor_tensor(lo[:, :, :], w[:, :, :], hi[:, :, :].bitcast(F32), ALU.subtract).then_inc(lo_done, 1)


def tiled(c, t):
    return t[:, :, :].rearrange("p (s i) d -> p s i d", i=T6)


def route(c):
    nc = c.nc
    T, E = T6, 4
    steps = c.B // T
    ctx, sb, ps, sem = stage_scope(c)
    with ctx:
        xn = sb("xn", [P, 2, T, D])
        xT = sb("xT", [D, 2, T, P])
        sc, top, dif, e = (sb(n, [P, T, k]) for n, k in (("sc", E), ("top", 1), ("dif", E), ("e", E)))
        rank, best, z, rz = (sb(n, [P, T, k]) for n, k in (("rank", E), ("best", E), ("z", 1), ("rz", 1)))
        gt, ge = sb("gt", [P, T, E, E]), sb("ge", [P, T, E, E])
        ps_x, ps_r = ps("ps_x"), ps("ps_r")
        xn_ready, xT_ps, xT_ready, hi_ready, lo_done, r_ps, dif_ready, exp_done, own = (
            sem(n) for n in ("xn_ready", "xT_ps", "xT_ready", "hi_ready", "lo_done", "r_ps", "dif_ready", "exp_done", "own"))
        block = ctx.enter_context(nc.Block())
        LAG = 3
        x4, wt4, hi4, lo4 = (tiled(c, t) for t in (c.x, c.f1_wt, c.f1_hi, c.f1_lo))
        mean4, rstd4 = (t[:, :].rearrange("p (s i) -> p s i", i=T) for t in (c.mean, c.rstd))
        OWN = 11

        @block.tensor
        def _(pe):
            def slot(sl):
                if at := sl.step(1):
                    s, u = at
                    pe.wait_ge(xn_ready, s + 1)
                    wait(pe, xT_ready, s)
                    for i in range(T):
                        ins = nc.tensor.transpose(ps_x[:, i * P:i * P + P], xn[:, u % 2, i, :], c.ident[:, :])
                    ins.then_inc(xT_ps, 1)
                if at := sl.step(2):
                    s, u = at
                    pe.wait_ge(xT_ready, s + 1)
                    wait(pe, own, OWN * (s - 1) + 1)
                    for i in range(T):
                        ins = nc.tensor.matmul(ps_r[:, i * E:i * E + E], xT[:, u % 2, i, :], c.f1["router"][:, :], start=True, stop=True)
                    ins.then_inc(r_ps, 1)

            run_slots(pe, slot, steps, LAG)

        @block.scalar
        def _(act):
            def slot(sl):
                if at := sl.step(1):
                    s, u = at
                    act.wait_ge(xT_ps, s + 1)
                    wait(act, r_ps, s - 1)
                    wait(act, lo_done, s - 1)
                    wide = ps_x[:, :].rearrange("p (i t) -> p i t", i=T)
                    nc.scalar.activation(hi4[:, s, :, :], wide, ACT.Copy).then_inc(hi_ready, 1)
                    nc.scalar.activation(xT[:, u % 2, :, :], wide, ACT.Copy).then_inc(xT_ready, 1)
                if at := sl.step(2):
                    s, u = at
                    act.wait_ge(dif_ready, s + 1)
                    nc.scalar.activation(e[:, :, :], dif[:, :, :], ACT.Exp).then_inc(exp_done, 1)

            run_slots(act, slot, steps, LAG)

        @block.vector
        def _(dve):
            def slot(sl):
                if at := sl.step(0):
                    s, u = at
                    wait(dve, xT_ps, s - 1)
                    for i in range(T):
                        ins = nc.vector.tensor_scalar(xn[:, u % 2, i, :], x4[:, s, i, :], mean4[:, s, i:i + 1], rstd4[:, s, i:i + 1],
                                                      ALU.subtract, ALU.mult)
                    ins.then_inc(xn_ready, 1)
                if at := sl.step(2):
                    s, u = at
                    base = OWN * s

                    def after(ins, k):
                        ins.then_inc(own, 1)
                        dve.wait_ge(own, base + k)

                    def per_token(t):
                        return t[:, :, :].broadcast_to([P, T, E])

                    dve.wait_ge(r_ps, s + 1)
                    bias = [c.f1["router_b"][:, n, :].unsqueeze(1).broadcast_to([P, T, E]) for n in range(2)]
                    after(nc.vector.tensor_tensor(dif[:, :, :], ps_r[:, 0:T * E].rearrange("p (i e) -> p i e", i=T), bias[0], ALU.add), 1)
                    after(nc.vector.tensor_tensor(sc[:, :, :], dif[:, :, :], bias[1], ALU.add), 2)
                    after(nc.vector.tensor_reduce(top[:, :, 0], sc[:, :, :], AX.X, ALU.max), 3)
                    nc.vector.tensor_tensor(dif[:, :, :], sc[:, :, :], per_token(top), ALU.subtract).then_inc(dif_ready, 1)
                    dve.wait_ge(exp_done, s + 1)
                    after(top_two(c, dve, own, base + 3, sc[:, :, :], e[:, :, :], gt[:, :, :, :], ge[:, :, :, :], rank[:, :, :],
                                  c.w["tri4"][:, :, :, :], best[:, :, :]), 8)
                    after(nc.vector.tensor_reduce(z[:, :, 0], best[:, :, :], AX.X, ALU.add), 9)
                    after(nc.vector.reciprocal(rz[:, :, :], z[:, :, :]), 10)
                    after(nc.vector.tensor_tensor(wt4[:, s, :, :], best[:, :, :], per_token(rz), ALU.mult), 11)

                if at := sl.step(2):
                    s, u = at
                    dve.wait_ge(xT_ready, s + 1)
                    dve.wait_ge(hi_ready, s + 1)
                    nc.vector.tensor_tensor(lo4[:, s, :, :], xT[:, u % 2, :, :], hi4[:, s, :, :].bitcast(F32), ALU.subtract).then_inc(lo_done, 1)

            run_slots(dve, slot, steps, LAG)


def hidden_expert(c, expert, func, w1, w_gated, bias1, w2, bias2):
    nc = c.nc
    T, N = T6, T6 * P
    steps = c.B // T
    C = c.f1_parts[w1][0].shape[1]
    ctx, sb, ps, sem = stage_scope(c)
    with ctx:
        hid = sb("hid", [P, 2, C, N])
        sg = sb("sg", [P, 2, N]) if w_gated is not None else None
        yb = sb("yb", [P, T, D])
        ps_g = [ps(f"ps_g{i}") for i in range(2)]
        ps_u = [ps(f"ps_u{i}") for i in range(2)]
        ps_y = [ps(f"ps_y{i}") for i in range(2)]
        g_ps, u_ps, g_done, h_ready, y_ps, y_done, biased = (
            sem(n) for n in ("g_ps", "u_ps", "g_done", "h_ready", "y_ps", "y_done", "biased"))
        block = ctx.enter_context(nc.Block())
        LAG = 1
        g_freed = h_ready if w_gated is None else g_done
        x4, wt4 = tiled(c, c.x), tiled(c, c.f1_wt)
        hi4, lo4 = tiled(c, c.f1_hi), tiled(c, c.f1_lo)

        @block.tensor
        def _(pe):
            def product(out, name, n, s):
                w_hi, w_lo = c.f1_parts[name]
                nc.tensor.matmul(out, w_hi[:, n, :], hi4[:, s, :, :], start=True, stop=False)
                nc.tensor.matmul(out, w_hi[:, n, :], lo4[:, s, :, :], start=False, stop=False)
                return nc.tensor.matmul(out, w_lo[:, n, :], hi4[:, s, :, :], start=False, stop=True)

            def slot(sl):
                if at := sl.step(0):
                    s, u = at
                    for n in range(C):
                        wait(pe, g_freed, C * s + n - 1)
                        product(ps_g[n % 2][:, :], w1, n, s).then_inc(g_ps, 1)
                        if w_gated is not None:
                            wait(pe, h_ready, C * s + n - 1)
                            product(ps_u[n % 2][:, :], w_gated, n, s).then_inc(u_ps, 1)
                if at := sl.step(1):
                    s, u = at
                    pe.wait_ge(h_ready, C * (s + 1))
                    wait(pe, y_done, s - 1)
                    for i in range(T):
                        part = ps_y[u % 2][:, i * P:i * P + P]
                        for n in range(C):
                            ins = nc.tensor.matmul(part, hid[:, u % 2, n, i * P:i * P + P], w2[:, n, :],
                                                   start=n == 0, stop=n == C - 1)
                    ins.then_inc(y_ps, 1)

            run_slots(pe, slot, steps, LAG)

        @block.scalar
        def _(act):
            def slot(sl):
                if at := sl.step(0):
                    s, u = at
                    for n in range(C):
                        act.wait_ge(g_ps, C * s + n + 1)
                        if w_gated is not None:
                            wait(act, h_ready, C * s + n - 1)
                            nc.scalar.activation(sg[:, n % 2, :], ps_g[n % 2][:, :], func).then_inc(g_done, 1)
                        else:
                            wait(act, y_ps, s - 1)
                            nc.scalar.activation(hid[:, u % 2, n, :], ps_g[n % 2][:, :], func, bias=bias1[:, n:n + 1]).then_inc(h_ready, 1)

            run_slots(act, slot, steps, LAG)

        @block.vector
        def _(dve):
            def slot(sl):
                if w_gated is not None and (at := sl.step(0)):
                    s, u = at
                    for n in range(C):
                        dve.wait_ge(g_done, C * s + n + 1)
                        dve.wait_ge(u_ps, C * s + n + 1)
                        wait(dve, y_ps, s - 1)
                        nc.vector.tensor_tensor(hid[:, u % 2, n, :], sg[:, n % 2, :], ps_u[n % 2][:, :], ALU.mult).then_inc(h_ready, 1)
                if at := sl.step(1):
                    s, u = at
                    dve.wait_ge(y_ps, s + 1)
                    wait(dve, y_done, s)
                    y = ps_y[u % 2][:, :].rearrange("p (i d) -> p i d", i=T)
                    if bias2 is not None:
                        nc.vector.tensor_tensor(yb[:, :, :], y, bias2[:, :].unsqueeze(1).broadcast_to([P, T, D]), ALU.add).then_inc(biased, 1)
                        dve.wait_ge(biased, s + 1)
                        y = yb
                    for i in range(T):
                        ins = nc.vector.scalar_tensor_tensor(out=x4[:, s, i, :], in0=y[:, i, :],
                                                             scalar=wt4[:, s, i, expert:expert + 1], in1=x4[:, s, i, :],
                                                             op0=ALU.mult, op1=ALU.add)
                    ins.then_inc(y_done, 1)

            run_slots(dve, slot, steps, LAG)


def normed_expert(c, expert):
    nc, f = c.nc, c.f1
    T, N = T6, T6 * P
    steps = c.B // T
    ctx, sb, ps, sem = stage_scope(c)
    with ctx:
        xr = sb("xr", [D, 2, T, P])
        full = sb("full", [P, 2, T, D])
        yb = sb("yb", [P, T, D])
        st = sb("st", [P, 2, T, 6])
        both, dif, dif2, sq, mean, var, vpe, root, rstd = (
            sb(n, [P, 2, T]) for n in ("both", "dif", "dif2", "sq", "mean", "var", "vpe", "root", "rstd"))
        rows = [sb(f"rows{k}", [P, 2, T, D]) for k in range(2)]
        hT = [sb(f"hT{k}", [D, 2, N]) for k in range(2)]
        ff = sb("ff", [P, 2, 2, N])
        pre = [ps(f"pre{k}") for k in range(2)]
        ps_h = [ps(f"ps_h{k}") for k in range(2)]
        ps_g = [ps(f"ps_g{k}") for k in range(2)]
        ps_y = ps("ps_y")
        xr_ready, f_ps, f_ready, y_ps, y_done = (sem(n) for n in ("xr_ready", "f_ps", "f_ready", "y_ps", "y_done"))
        full_ready = [sem(f"full_ready{k}") for k in range(2)]
        biased = sem("biased")
        pre_ps, st_done, ag_done, var_ready, root_ready, rstd_done, rows_ready, h_ps, h_ready = (
            [sem(f"{n}{k}") for k in range(2)] for n in ("pre_ps", "st_done", "ag_done", "var_ready", "root_ready", "rstd_done",
                                                         "rows_ready", "h_ps", "h_ready"))
        block = ctx.enter_context(nc.Block())
        LAG = 4
        x4, wt4, hi4, lo4 = (tiled(c, t) for t in (c.x, c.f1_wt, c.f1_hi, c.f1_lo))

        @block.tensor
        def _(pe):
            def transposes(at, k):
                s, u = at
                pe.wait_ge(rows_ready[k], s + 1)
                wait(pe, h_ready[k], s)
                for i in range(T):
                    ins = nc.tensor.transpose(ps_h[k][:, i * P:i * P + P], rows[k][:, u % 2, i, :], c.ident[:, :])
                ins.then_inc(h_ps[k], 1)

            def slot(sl):
                if at := sl.step(2):
                    transposes(at, 0)
                if at := sl.step(4):
                    transposes(at, 1)
                if at := sl.step(1):
                    s, u = at
                    pe.wait_ge(xr_ready, s + 1)
                    wait(pe, full_ready[0], s)
                    for i in range(T):
                        part = pre[0][:, i * P:i * P + P]
                        ins = nc.tensor.matmul(part, xr[:, u % 2, i, :], c.f1_ce[:, :], start=True, stop=True)
                    ins.then_inc(pre_ps[0], 1)
                if at := sl.step(3):
                    s, u = at
                    pe.wait_ge(f_ready, 2 * (s + 1))
                    wait(pe, full_ready[1], s)
                    for i in range(T):
                        part = pre[1][:, i * P:i * P + P]
                        cols = slice(i * P, i * P + P)
                        nc.tensor.matmul(part, hT[0][:, u % 2, cols], c.ident[:, :], start=True, stop=False)
                        for n in range(2):
                            ins = nc.tensor.matmul(part, ff[:, u % 2, n, cols], f["f2"][:, n, :], start=False, stop=n == 1)
                    ins.then_inc(pre_ps[1], 1)
                if at := sl.step(2):
                    s, u = at
                    pe.wait_ge(h_ready[0], s + 1)
                    for n in range(2):
                        wait(pe, f_ready, 2 * s - 1 + n)
                        nc.tensor.matmul(ps_g[n][:, :], f["f1"][:, n, :], hT[0][:, u % 2, :], start=True, stop=True).then_inc(f_ps, 1)
                if at := sl.step(4):
                    s, u = at
                    pe.wait_ge(h_ready[1], s + 1)
                    wait(pe, y_done, s)
                    for i in range(T):
                        part = ps_y[:, i * P:i * P + P]
                        ins = nc.tensor.matmul(part, hT[1][:, u % 2, i * P:i * P + P], f["gen"][:, :], start=True, stop=True)
                    ins.then_inc(y_ps, 1)

            run_slots(pe, slot, steps, LAG)

        @block.scalar
        def _(act):
            def shifted(at, k):
                s, u = at
                act.wait_ge(h_ps[k], s + 1)
                if k == 0:
                    wait(act, pre_ps[1], s - 1)
                else:
                    wait(act, y_ps, s - 1)
                nc.scalar.activation(hT[k][:, u % 2, :], ps_h[k][:, :], ACT.Identity, scale=f["norms"][:, 2 * k:2 * k + 1],
                                     bias=f["norms"][:, 2 * k + 1:2 * k + 2]).then_inc(h_ready[k], 1)

            def roots(at, k):
                s, u = at
                act.wait_ge(var_ready[k], s + 1)
                nc.scalar.activation(root[:, k, :], vpe[:, k, :], ACT.Sqrt).then_inc(root_ready[k], 1)

            def slot(sl):
                if at := sl.step(2):
                    shifted(at, 0)
                if at := sl.step(4):
                    shifted(at, 1)
                if at := sl.step(1):
                    roots(at, 0)
                if at := sl.step(3):
                    roots(at, 1)
                if at := sl.step(2):
                    s, u = at
                    for n in range(2):
                        act.wait_ge(f_ps, 2 * s + n + 1)
                        nc.scalar.activation(ff[:, u % 2, n, :], ps_g[n][:, :], ACT.Relu, bias=f["f1b"][:, n:n + 1]).then_inc(f_ready, 1)

            run_slots(act, slot, steps, LAG)

        @block.gpsimd
        def _(pool):
            def slot(sl):
                if at := sl.step(0):
                    s, u = at
                    wait(pool, pre_ps[0], s - 1)
                    nc.gpsimd.tensor_tensor(xr[:, u % 2, :, :], hi4[:, s, :, :].bitcast(F32), lo4[:, s, :, :].bitcast(F32), ALU.add).then_inc(xr_ready, 1)

            run_slots(pool, slot, steps, LAG)

        @block.vector
        def _(dve):
            def statistics(at, k):
                s, u = at
                dve.wait_ge(pre_ps[k], s + 1)
                wait(dve, rows_ready[k], s)
                bias = c.f1_rows[("ce", "f2b")[k]][:, :].unsqueeze(1).broadcast_to([P, T, D])
                nc.vector.tensor_tensor(full[:, k, :, :], pre[k][:, :].rearrange("p (i d) -> p i d", i=T), bias, ALU.add).then_inc(full_ready[k], 1)
                dve.wait_ge(full_ready[k], s + 1)
                for i in range(T):
                    ins = nc.vector.bn_stats(st[:, k, i, :], full[:, k, i, :])
                ins.then_inc(st_done[k], 1)
                me, mo, ve, vo = (st[:, k, :, n] for n in (1, 4, 2, 5))
                dve.wait_ge(st_done[k], s + 1)
                nc.vector.tensor_tensor(both[:, k, :], me, mo, ALU.add)
                nc.vector.tensor_tensor(dif[:, k, :], me, mo, ALU.subtract)
                nc.vector.tensor_tensor(sq[:, k, :], ve, vo, ALU.add).then_inc(ag_done[k], 1)
                dve.wait_ge(ag_done[k], 3 * s + 1)
                nc.vector.tensor_scalar(mean[:, k, :], both[:, k, :], 0.5, None, ALU.mult)
                nc.vector.tensor_tensor(dif2[:, k, :], dif[:, k, :], dif[:, k, :], ALU.mult).then_inc(ag_done[k], 1)
                dve.wait_ge(ag_done[k], 3 * s + 2)
                nc.vector.scalar_tensor_tensor(out=var[:, k, :], in0=dif2[:, k, :], scalar=D / 4, in1=sq[:, k, :],
                                               op0=ALU.mult, op1=ALU.add).then_inc(ag_done[k], 1)
                dve.wait_ge(ag_done[k], 3 * s + 3)
                nc.vector.tensor_scalar(vpe[:, k, :], var[:, k, :], 1.0 / D, EPS, ALU.mult, ALU.add).then_inc(var_ready[k], 1)

            def normalised(at, k):
                s, u = at
                dve.wait_ge(root_ready[k], s + 1)
                nc.vector.reciprocal(rstd[:, k, :], root[:, k, :]).then_inc(rstd_done[k], 1)
                dve.wait_ge(rstd_done[k], s + 1)
                wait(dve, h_ps[k], s - 1)
                for i in range(T):
                    ins = nc.vector.tensor_scalar(rows[k][:, u % 2, i, :], full[:, k, i, :], mean[:, k, i:i + 1],
                                                  rstd[:, k, i:i + 1], ALU.subtract, ALU.mult)
                ins.then_inc(rows_ready[k], 1)

            def slot(sl):
                first, second = sl.step(1), sl.step(3)
                if first:
                    statistics(first, 0)
                if second:
                    statistics(second, 1)
                if first:
                    normalised(first, 0)
                if second:
                    normalised(second, 1)
                if at := sl.step(4):
                    s, u = at
                    dve.wait_ge(y_ps, s + 1)
                    wait(dve, y_done, s)
                    nc.vector.tensor_tensor(yb[:, :, :], ps_y[:, :].rearrange("p (i d) -> p i d", i=T),
                                            c.f1_rows["genb"][:, :].unsqueeze(1).broadcast_to([P, T, D]), ALU.add).then_inc(biased, 1)
                    dve.wait_ge(biased, s + 1)
                    for i in range(T):
                        ins = nc.vector.scalar_tensor_tensor(out=x4[:, s, i, :], in0=yb[:, i, :],
                                                             scalar=wt4[:, s, i, expert:expert + 1], in1=x4[:, s, i, :],
                                                             op0=ALU.mult, op1=ALU.add)
                    ins.then_inc(y_done, 1)

            run_slots(dve, slot, steps, LAG)


def latent_weights(c):
    nc = c.nc
    ctx, sb, ps, sem = stage_scope(c)
    with ctx:
        pq = [ps(f"p{n}") for n in range(3)]
        ready, copied = sem("ready"), sem("copied")
        block = ctx.enter_context(nc.Block())
        parts = ((c.w["a0_dq"], c.w["a0_uq"], c.a0_q), (c.w["a0_dkv"], c.w["a0_uk"], c.a0_k), (c.w["a0_dkv"], c.w["a0_uv"], c.a0_v))

        @block.tensor
        def _(pe):
            for n, (down, up, out) in enumerate(parts):
                nc.tensor.matmul(pq[n][:, 0:out.shape[1]], down[:, :], up[:, :], start=True, stop=True).then_inc(ready, 1)

        @block.scalar
        def _(act):
            for n, (down, up, out) in enumerate(parts):
                act.wait_ge(ready, n + 1)
                nc.scalar.activation(out[:, :], pq[n][:, 0:out.shape[1]], ACT.Copy).then_inc(copied, 1)
            act.wait_ge(copied, len(parts))


def store_output(c):
    nc = c.nc
    ctx, sb, ps, sem = stage_scope(c)
    with ctx:
        stored = sem("stored")
        block = ctx.enter_context(nc.Block())

        @block.sync
        def _(sp):
            sp.dma_start(c.out.rearrange("b p d -> p b d"), c.x[:, :, :]).then_inc(stored, 16)
            sp.wait_ge(stored, 16)


def decoder(nc, inp, out, batches, layers=6):
    c = Core(nc, inp, out, batches)
    B = batches
    whole, most, first = ExitStack(), ExitStack(), ExitStack()
    with whole, most, first:
        def sb(name, shape, dt=F32, life=whole):
            return life.enter_context(nc.sbuf_tensor(name, shape, dt))

        c.x = sb("x", [P, B, D])
        c.stats = sb("stats", [P, B, 6])
        c.mean, c.rstd = sb("mean", [P, B]), sb("rstd", [P, B])
        c.w = {}
        tiles = {}
        for life, prefixes in ((whole, None), (most, ("ctx", "a1_", "x1_")), (first, ("a0_", "x0_"))):
            for name in inp:
                if name == "x" or name.startswith("late_"):
                    continue
                if prefixes is None and name.startswith(("ctx", "a1_", "x1_", "a0_", "x0_")):
                    continue
                if prefixes is not None and not name.startswith(prefixes):
                    continue
                shape = list(inp[name].shape)
                c.w[name] = sb("w_" + name, shape, inp[name].dtype, life)
                tiles[name] = c.w[name][(slice(None),) * len(shape)]
        keep = [(name, tiles[name]) for name in inp if name in tiles]
        c.ident, c.ident16, c.ones_row = c.w["ident"], c.w["ident16"], c.w["ones_row"]
        c.mask_q, c.mask_k = c.w["mask_q"], c.w["mask_k"]
        c.block, c.ones16 = c.w["block"], c.w["ones16"]
        c.keys = inp["ctx"].shape[2]
        c.ctx = c.w["ctx"]
        c.a0_q, c.a0_k, c.a0_v = (sb(n, [P, D], life=first) for n in ("a0_q", "a0_k", "a0_v"))
        c.x0_a, c.x0_o = sb("x0_a", [P, HEADS, D], life=first), sb("x0_o", [P, HEADS // 2, D], life=first)
        c.x0_b = sb("x0_b", [1, D], life=first)

        c.stage = "load"
        load_inputs(c, keep)
        if layers >= 1:
            c.stage = "n0"
            norm_scalars(c, False)
            c.stage = "lat"
            latent_weights(c)
            c.stage = "a0"
            self_attention(c, (c.a0_q[:, :], c.a0_k[:, :], c.a0_v[:, :], c.w["a0_o"][:, :]), HD ** -0.5)
        if layers >= 2:
            c.stage = "n1"
            norm_scalars(c, True)
            c.stage = "x0"
            wide_weights(c)
            cross_attention_wide(c)
        first.close()
        if layers >= 3:
            c.stage = "n2"
            norm_scalars(c, False)
            c.stage = "f0"
            scored_experts(c)
        if layers >= 4:
            c.stage = "n3"
            norm_scalars(c, False)
            c.stage = "a1"
            attention_over_heads(c)
        if layers >= 5:
            c.stage = "n4"
            norm_scalars(c, False)
            cross_attention_tempered(c)
        most.close()
        if layers >= 6:
            c.stage = "n5"
            norm_scalars(c, False)
            mixed_experts(c)
        c.stage = "out"
        store_output(c)



def triangles(experts):
    behind = np.triu(np.ones((experts, experts), np.float32), 1)
    return np.broadcast_to(np.stack([behind, behind.T]), (P, 2, experts, experts))


def constants():
    bf = mybir.dt.np(BF16)
    r = np.arange(P)
    strip = r % STRIP
    block = np.zeros((P, 2 * GROUP), np.float32)
    block[:, 0:GROUP] = strip[:, None] // HD == np.arange(GROUP)
    block[:, GROUP:] = (strip[:, None] % GROUP == np.arange(GROUP)) & (strip[:, None] < 3 * GROUP)
    later = np.where(r[None, :] > r[:, None], MASKED, 0.0)
    return {
        "ident": np.eye(P, dtype=np.float32), "ident16": np.eye(P).astype(bf),
        "mask_q": later.astype(bf), "mask_k": later.T.astype(bf),
        "tri8": triangles(8), "tri4": triangles(4),
        "block": block,
        "ones_row": np.ones((1, 512), np.float32), "ones16": np.ones((P, P), bf),
    }


def layouts(inputs, layers=6):
    a = {k: np.asarray(v) for k, v in inputs.items()}
    t = {"x": a["x"]}
    t.update(constants())
    t["a0_dq"], t["a0_uq"] = a["L0_attn_W_dq"].T, a["L0_attn_W_uq"]
    t["a0_dkv"], t["a0_uk"] = a["L0_attn_W_dkv"].T, a["L0_attn_W_uk"]
    t["a0_uv"], t["a0_o"] = a["L0_attn_W_uv"], a["L0_attn_W_o"]
    t["a1_qkv"] = np.concatenate([a["L1_attn_W" + n].T for n in "qkv"], axis=1)
    t["a1_o"] = np.tile(a["L1_attn_Wo"].T.reshape(HEADS, HD, D), (P // HEADS, 1, 1))
    t["a1_b"] = a["L1_attn_bo"][None]
    t["a1_rows"] = (np.arange(P)[:, None] // HEADS == np.arange(P // HEADS)).astype(np.float32)
    t["ctx"] = a["ctx_1024"].transpose(2, 0, 1)
    inner = a["L0_xattn_w_q"].shape[1]
    per_head = lambda w: w.T.reshape(HEADS, inner // HEADS, D).transpose(1, 0, 2)
    t["x0_q"], t["x0_k"] = per_head(a["L0_xattn_w_q"]), per_head(a["L0_xattn_w_kv"][:, :inner])
    t["x0_v"] = a["L0_xattn_w_kv"][:, inner:]
    t["x0_out"] = a["L0_xattn_w_out"].reshape(HEADS // 2, P, D).transpose(1, 0, 2)
    t["x0_bias"] = a["L0_xattn_b_out"][None]
    t["x0_gate"] = np.broadcast_to(a["L0_xattn_gate"][None], (P, 1))
    E, H = a["L0_ffn_W1"].shape[:2]
    t["f0_router"] = a["L0_ffn_Wg"].T
    t["late_f0_1"], t["late_f0_2"] = (a["L0_ffn_W" + n].reshape(E * H, D).T for n in "12")
    down = np.zeros((E, 3 * P, D), np.float32)
    down[:, :H] = a["L0_ffn_W3"].transpose(0, 2, 1)
    t["late_f0_3"] = down.reshape(E, 3, P, D).transpose(2, 0, 1, 3)
    t["x1_q"], t["x1_k"], t["x1_v"], t["x1_o"] = (a["L1_xattn_W" + n].T for n in "qkvo")
    t["x1_bias"] = np.stack([a["L1_xattn_bq"], a["L1_xattn_bk"]], axis=1)
    t["x1_bv"], t["x1_bo"] = a["L1_xattn_bv"][None], a["L1_xattn_bo"][None]
    t["x1_w1"], t["x1_w2"] = a["L1_xattn_w1"].T, a["L1_xattn_w2"].T
    t["x1_w3"] = np.broadcast_to(a["L1_xattn_w3"].T, (a["L1_xattn_w3"].shape[1], P))
    t["x1_mlp_b"] = np.stack([a["L1_xattn_b1"], a["L1_xattn_b2"]], axis=1)
    t["x1_b3"] = np.broadcast_to(a["L1_xattn_b3"][None], (P, 1))
    t["x1_heads"] = np.arange(P)[:, None] // HD == np.arange(HEADS)
    t["x1_heads"] = t["x1_heads"].astype(np.float32)
    keys = a["ctx_1024"].shape[1]
    pick = np.zeros((P, 3, 3), np.float32)
    pick[:, 0, 0] = HD ** -0.5 / (P * keys)
    pick[:, 1, 1] = HD ** -0.5 / P
    pick[:, 2, 2] = 1.0 / (P * (keys - 1))
    t["x1_pick"] = pick.reshape(P, 9)
    t["x1_less"] = np.array([[0.0, 0.0, -1.0 / (keys * (keys - 1))]], np.float32)
    place = np.arange(STRIP)[None] // HD == np.arange(GROUP)[:, None]
    t["x1_place"] = np.broadcast_to(place.astype(np.float32), (P, GROUP, STRIP))
    f = lambda n: a["L1_ffn_" + n]
    units = lambda w: w.reshape(D, -1, P)
    down = lambda w: w.reshape(-1, P, w.shape[1]).transpose(1, 0, 2)
    col = lambda b: b.reshape(-1, P).T
    late = {
        "router": f("router_w"),
        "router_b": np.broadcast_to(np.stack([f("router_b"), f("load_balancer")]), (P, 2, 4)),
        "sw_1": units(f("sw_w1")), "sw_3": units(f("sw_w3")), "sw_2": down(f("sw_w2")),
        "me_eqT": f("me_eq_w").T, "me_vT": f("me_wv").T, "me_oT": f("me_wo").T, "me_v": f("me_wv"), "me_o": f("me_wo"),
        "c1": units(f("me_c1w")), "c1b": col(f("me_c1b")), "c2": down(f("me_c2w")), "c2b": f("me_c2b")[None],
        "cols": np.stack([f(n) for n in ("me_eq_b", "me_bv", "me_bo", "ce_syn_b", "ce_bv")], axis=1),
        "ce_vT": f("ce_wv").T, "ce_o": f("ce_wo"), "ce_synT": f("ce_syn_w").T, "ce_bo": f("ce_bo")[None],
        "norms": np.stack([f(n) for n in ("ce_n1g", "ce_n1b", "ce_n2g", "ce_n2b")], axis=1),
        "f1": units(f("ce_f1w")), "f1b": col(f("ce_f1b")), "f2": down(f("ce_f2w")), "f2b": f("ce_f2b")[None],
        "gen": f("ce_gen_w"), "genb": f("ce_gen_b")[None],
        "ml_1": units(f("ml_w1")), "ml_b1": col(f("ml_b1")), "ml_2": down(f("ml_w2")), "ml_b2": f("ml_b2")[None],
    }
    t.update({"late_f1_" + n: v for n, v in late.items()})
    t["x0_ln"] = np.stack([a["L0_xattn_ln_gamma"], a["L0_xattn_ln_beta"]], axis=1)
    return {k: np.ascontiguousarray(v) for k, v in t.items()}


def kernel(**inputs):
    import concourse.bacc as bacc
    from concourse.bass_utils import run_bass_kernel_spmd

    nc = bacc.Bacc("TRN2", target_bir_lowering=False, num_devices=1)
    arrays = layouts(inputs)
    B = arrays["x"].shape[0]
    aps = {k: nc.dram_tensor("in_" + k, v.shape, mybir.dt.from_np(v.dtype), kind="ExternalInput").ap() for k, v in arrays.items()}
    out = nc.dram_tensor("out", (B, P, D), F32, kind="ExternalOutput").ap()
    decoder(nc, aps, out, B)
    r = run_bass_kernel_spmd(nc, [{"in_" + k: v for k, v in arrays.items()}], core_ids=[0])
    return r.results[0]["out"]
```

```python
from contextlib import ExitStack

import numpy as np

import concourse.bass as bass
import concourse.mybir as mybir

F32 = mybir.dt.float32
F32R = mybir.dt.float32r
BF16 = mybir.dt.bfloat16
ALU = mybir.AluOpType
ACT = mybir.ActivationFunctionType
AX = mybir.AxisListType

P = 128
D = 128
HEADS = 16
HD = 8
GROUPS = 4
GROUP = 4
STRIP = 32
EPS = 1e-5
MASKED = -1e30
UNROLL = 4


class Slot:

    def __init__(self, t, odd, steps, fixed, ring):
        self.t, self.odd, self.steps, self.fixed, self.ring = t, odd, steps, fixed, ring

    def step(self, lag):
        if self.fixed and not 0 <= self.t - lag < self.steps:
            return None
        return self.t - lag, (self.odd - lag) % self.ring


def run_slots(eng, slot, steps, lag, unroll=UNROLL):
    ring = max(unroll, UNROLL)
    first = min(-(-(lag + 2) // unroll) * unroll, steps)
    last = steps - (steps - first) % unroll
    for t in range(first):
        slot(Slot(t, t % ring, steps, True, ring))
    if last > first:
        with eng.Fori(first // unroll, last // unroll) as i:
            for k in range(unroll):
                slot(Slot(i * unroll + k, k, steps, False, ring))
    for t in range(last, steps + lag):
        slot(Slot(t, t % ring, steps, True, ring))


def wait(eng, sem, value):
    if not (isinstance(value, int) and value <= 0):
        eng.wait_ge(sem, value)


class Core:

    def __init__(self, nc, inputs, out, batches):
        self.nc, self.inp, self.out, self.B = nc, inputs, out, batches


def stage_scope(c):
    ctx = ExitStack()

    def sb(name, shape, dt=F32):
        return ctx.enter_context(c.nc.sbuf_tensor(f"{stage}_{name}", shape, dt))

    def ps(name, shape=(P, 512), dt=F32):
        return ctx.enter_context(c.nc.psum_tensor(f"{stage}_{name}", list(shape), dt))

    sems = []

    def sem(name):
        sems.append(c.nc.alloc_semaphore(name=f"{stage}_{name}"))
        return sems[-1]

    stage = c.stage

    def clear():
        c.nc.clear_and_free_semaphores(sems)
        c.nc.all_engine_barrier()

    ctx.callback(clear)
    return ctx, sb, ps, sem


def norm_scalars(c, second):
    nc = c.nc
    ctx, sb, ps, sem = stage_scope(c)
    with ctx:
        dif, var, vpe, root, rec, t1, t2 = (sb(n, [P, c.B]) for n in ("dif", "var", "vpe", "root", "rec", "t1", "t2"))
        dv = sem("dv")
        var_ready, root_ready = sem("var_ready"), sem("root_ready")
        block = ctx.enter_context(nc.Block())
        me, mo, ve, vo = (c.stats[:, :, k] for k in (1, 4, 2, 5))

        @block.vector
        def _(dve):
            n = [0]

            def own(ins):
                n[0] += 1
                ins.then_inc(dv, 1)
                dve.wait_ge(dv, n[0])

            def rsqrt(out, x, k):
                nc.vector.tensor_copy(vpe[:, :], x).then_inc(var_ready, 1)
                dve.wait_ge(root_ready, k)
                own(nc.vector.reciprocal(rec[:, :], root[:, :]))
                own(nc.vector.tensor_tensor(t1[:, :], rec[:, :], rec[:, :], ALU.mult))
                own(nc.vector.tensor_tensor(t2[:, :], t1[:, :], vpe[:, :], ALU.mult))
                own(nc.vector.tensor_scalar(t1[:, :], t2[:, :], -0.5, 1.5, ALU.mult, ALU.add))
                own(nc.vector.tensor_tensor(out, t1[:, :], rec[:, :], ALU.mult))

            own(nc.vector.tensor_tensor(t1[:, :], me, mo, ALU.add))
            own(nc.vector.tensor_scalar(c.mean[:, :], t1[:, :], 0.5, None, ALU.mult))
            own(nc.vector.tensor_tensor(dif[:, :], me, mo, ALU.subtract))
            own(nc.vector.tensor_tensor(t1[:, :], dif[:, :], dif[:, :], ALU.mult))
            own(nc.vector.tensor_tensor(t2[:, :], ve, vo, ALU.add))
            own(nc.vector.scalar_tensor_tensor(out=dif[:, :], in0=t1[:, :], scalar=D / 4, in1=t2[:, :],
                                               op0=ALU.mult, op1=ALU.add))
            own(nc.vector.tensor_scalar(var[:, :], dif[:, :], 1.0 / D, None, ALU.mult))
            own(nc.vector.tensor_scalar(t1[:, :], var[:, :], EPS, None, ALU.add))
            rsqrt(c.rstd[:, :], t1[:, :], 1)
            if second:
                own(nc.vector.tensor_tensor(t1[:, :], c.rstd[:, :], c.rstd[:, :], ALU.mult))
                own(nc.vector.tensor_tensor(t2[:, :], t1[:, :], var[:, :], ALU.mult))
                own(nc.vector.tensor_scalar(t1[:, :], t2[:, :], EPS, None, ALU.add))
                rsqrt(dif[:, :], t1[:, :], 2)
                own(nc.vector.tensor_tensor(t1[:, :], c.rstd[:, :], dif[:, :], ALU.mult))
                own(nc.vector.tensor_copy(c.rstd[:, :], t1[:, :]))

        @block.scalar
        def _(act):
            for k in range(2 if second else 1):
                act.wait_ge(var_ready, k + 1)
                nc.scalar.activation(root[:, :], vpe[:, :], ACT.Sqrt).then_inc(root_ready, 1)


def load_inputs(c, keep):
    nc = c.nc
    ctx, sb, ps, sem = stage_scope(c)
    with ctx:
        parts = max(1, c.B // 16)
        per = c.B // parts
        x_in = [sem(f"x_in{n}") for n in range(parts)]
        w_in, made = sem("w_in"), sem("made")
        block = ctx.enter_context(nc.Block())
        xs = c.inp["x"].rearrange("b p d -> p b d")
        later = ("ctx", "x0_", "a1_", "x1_", "f0_", "f1_")
        soon = [k for k in keep if not k[0].startswith(later)]
        c.later = [k for k in keep if k[0].startswith(later)]
        c.rest_count = 16 * len(c.later)

        @block.sync
        def _(sp):
            for n in range(parts):
                sp.dma_start(c.x[:, n * per:(n + 1) * per, :], xs[:, n * per:(n + 1) * per, :]).then_inc(x_in[n], 16)
            for name, tile in soon:
                sp.dma_start(tile, c.inp[name]).then_inc(w_in, 16)
            sp.wait_ge(w_in, 16 * len(soon))

        @block.vector
        def _(dve):
            for n in range(parts):
                dve.wait_ge(x_in[n], 16)
                for s in range(n * per, (n + 1) * per):
                    ins = nc.vector.bn_stats(c.stats[:, s, :], c.x[:, s, :])
            ins.then_inc(made, 1)
            dve.wait_ge(made, 1)


def self_attention(c, scale):
    nc, B = c.nc, c.B
    ctx, sb, ps, sem = stage_scope(c)
    with ctx:
        xn = sb("xn", [P, 2, D])
        xT = sb("xT", [P, 2, P])
        signed = [sb(f"signed_{n}", [P, GROUPS, P], F32R) for n in "qk"]
        q, k = (sb(n, [P, UNROLL, GROUP, P], F32R) for n in "qk")
        q_shift = sb("q_shift", [P, 2, GROUPS, P], F32R)
        v1 = sb("v1", [P, UNROLL, HEADS, STRIP])
        nmax = sb("nmax", [P, HEADS])
        rest = sb("rest", [P, 2, HEADS])
        part = sb("part", [P, 2, HEADS], BF16)
        pad = sb("pad", [P, 2, GROUP, GROUPS, STRIP])
        e = sb("e", [P, 2, HEADS, P])
        oz = sb("oz", [P, 512])
        rz = sb("rz", [P, HEADS])
        o = sb("o", [P, 2, D])
        oT = sb("oT", [D, P])

        ps_misc, ps_qk, ps_o, ps_z = ps("ps_misc"), ps("ps_qk"), ps("ps_o"), ps("ps_z")
        ps_x, ps_v, ps_oT, ps_y = (ps_misc[:, n * P:n * P + P] for n in range(4))
        ps_n = [ps(f"ps_n{i}") for i in range(2)]
        ps_t = [ps(f"ps_t{i}") for i in range(2)]

        made = sem("made")
        names = ("xn_ready", "xT_ps", "xT_ready", "q_ps", "k_ps", "v_ps", "q_signed", "k_signed", "q_ready", "k_ready", "v_ready",
                 "nat_ps", "max_done", "own", "pad_ready", "pad_ps", "shift_ready", "sT_ps", "exp_done", "o_ps", "oz_ready",
                 "z_ps", "rz_ready", "o_ready", "oT_ps", "oT_ready", "y_ps", "x_done")
        (xn_ready, xT_ps, xT_ready, q_ps, k_ps, v_ps, q_signed, k_signed, q_ready, k_ready, v_ready,
         nat_ps, max_done, own, pad_ready, pad_ps, shift_ready, sT_ps, exp_done, o_ps, oz_ready,
         z_ps, rz_ready, o_ready, oT_ps, oT_ready, y_ps, x_done) = (sem(n) for n in names)
        block = ctx.enter_context(nc.Block())
        TURN, PROJECT, SCORE, SHIFT, WEIGH, VALUE, LAST = 1, 2, 3, 4, 5, 6, 7
        LAG = LAST

        def strip(t):
            return slice(STRIP * t, STRIP * t + STRIP)

        def upto(sl, n):
            return min(n, B) if sl.fixed else n

        @block.tensor
        def _(pe):
            def scores(at, g):
                s, u = at
                if g == 0:
                    pe.wait_ge(q_ready, s + 1)
                    pe.wait_ge(k_ready, s + 1)
                wait(pe, max_done, s * GROUPS + g - 1)
                bank = ps_n[g % 2]
                for j in range(GROUP):
                    nc.tensor.matmul(bank[:, j * P:j * P + P], q[strip(g), u, j, :], k[strip(g), u, j, :], start=j == 0, stop=False)
                nc.tensor.matmul(bank[:, :].rearrange("p (t k) -> p t k", t=GROUP), c.ident16[:, :],
                                 c.mask_q[:, :].unsqueeze(1).broadcast_to([P, GROUP, P]), start=False, stop=True).then_inc(nat_ps, 1)

            def shifted(at, g):
                s, u = at
                if g == 0:
                    pe.wait_ge(shift_ready, s + 1)
                wait(pe, exp_done, s * GROUPS + g - 1)
                bank = ps_t[g % 2]
                for j in range(GROUP):
                    nc.tensor.matmul(bank[:, j * P:j * P + P], k[strip(g), u, j, :], q_shift[strip(g), u % 2, j, :],
                                     start=j == 0, stop=False)
                nc.tensor.matmul(bank[:, :].rearrange("p (t q) -> p t q", t=GROUP), c.ident16[:, :],
                                 c.mask_k[:, :].unsqueeze(1).broadcast_to([P, GROUP, P]), start=False, stop=True).then_inc(sT_ps, 1)

            def project(at, w):
                s, u = at
                for g in range(GROUPS):
                    ins = nc.tensor.matmul(ps_qk[:, g * P:g * P + P], w[:, g, :], xT[:, u % 2, :], start=True, stop=True)
                return ins

            def slot(sl):
                scored, weighed, projected = sl.step(SCORE), sl.step(WEIGH), sl.step(PROJECT)
                if scored:
                    scores(scored, 0)
                    scores(scored, 1)
                if weighed:
                    shifted(weighed, 0)
                    shifted(weighed, 1)
                if projected:
                    s, u = projected
                    pe.wait_ge(xT_ready, s + 1)
                    wait(pe, k_ready, s)
                    wait(pe, shift_ready, s + PROJECT - SHIFT)
                    project(projected, c.a0_q).then_inc(q_ps, 1)
                if at := sl.step(VALUE):
                    s, u = at
                    pe.wait_ge(exp_done, (s + 1) * GROUPS)
                    pe.wait_ge(v_ready, s + 1)
                    wait(pe, oz_ready, s)
                    for n in range(HEADS):
                        j, g = divmod(n, GROUPS)
                        h = GROUP * g + j
                        ins = nc.tensor.matmul(ps_o[strip(g), j * P:j * P + P], v1[:, u, h, :], e[:, u % 2, h, :],
                                               start=True, stop=True)
                    ins.then_inc(o_ps, 1)
                if at := sl.step(TURN):
                    s, u = at
                    pe.wait_ge(xn_ready, s + 1)
                    wait(pe, xT_ready, s)
                    wait(pe, v_ready, s - 1)
                    wait(pe, x_done, s + TURN - LAST)
                    nc.tensor.transpose(ps_x, xn[:, u % 2, :], c.ident[:, :]).then_inc(xT_ps, 1)
                if scored:
                    scores(scored, 2)
                if weighed:
                    shifted(weighed, 2)
                if projected:
                    s, u = projected
                    pe.wait_ge(q_ready, s + 1)
                    project(projected, c.a0_k).then_inc(k_ps, 1)
                    wait(pe, xT_ready, upto(sl, s + PROJECT - TURN + 1))
                    wait(pe, x_done, s + PROJECT - LAST)
                    nc.tensor.matmul(ps_v, xT[:, u % 2, :], c.a0_v[:, :], start=True, stop=True).then_inc(v_ps, 1)
                if scored:
                    scores(scored, 3)
                if weighed:
                    shifted(weighed, 3)
                if at := sl.step(VALUE):
                    s, u = at
                    pe.wait_ge(oz_ready, s + 1)
                    wait(pe, o_ready, s)
                    for j in range(GROUP):
                        ins = nc.tensor.transpose(ps_z[:, j * P:j * P + P], oz[:, j * P:j * P + P], c.ident[:, :])
                    ins.then_inc(z_ps, 1)
                if at := sl.step(LAST):
                    s, u = at
                    pe.wait_ge(o_ready, s + 1)
                    wait(pe, v_ready, upto(sl, s + LAST - PROJECT + 1))
                    wait(pe, x_done, s)
                    nc.tensor.transpose(ps_oT, o[:, u % 2, :], c.ident[:, :]).then_inc(oT_ps, 1)
                if at := sl.step(SHIFT):
                    s, u = at
                    pe.wait_ge(pad_ready, s + 1)
                    wait(pe, k_ready, upto(sl, s + SHIFT - PROJECT + 1))
                    wait(pe, shift_ready, s)
                    for g in range(GROUPS):
                        ins = nc.tensor.transpose(ps_qk[:, g * P:g * P + P],
                                                  pad[:, u % 2, g, :, :].rearrange("p t r -> p (t r)"), c.ident[:, :])
                    ins.then_inc(pad_ps, 1)
                if at := sl.step(LAST):
                    s, u = at
                    pe.wait_ge(oT_ready, s + 1)
                    nc.tensor.matmul(ps_y, oT[:, :], c.w["a0_o"][:, :], start=True, stop=True).then_inc(y_ps, 1)

            run_slots(pe, slot, B, LAG)

        def grouped(bank):
            return bank[:, :].rearrange("p (g t) -> p g t", g=GROUPS)

        @block.scalar
        def _(act):
            act.wait_ge(made, 1)

            def exponentials(at, groups):
                s, u = at
                for g in groups:
                    act.wait_ge(sT_ps, s * GROUPS + g + 1)
                    if g == 0:
                        wait(act, o_ps, s - 1)
                    nc.scalar.activation(e[:, u % 2, GROUP * g:GROUP * g + GROUP, :],
                                         ps_t[g % 2][:, :].rearrange("p (t q) -> p t q", t=GROUP),
                                         ACT.Exp, scale=scale).then_inc(exp_done, 1)

            def slot(sl):
                weighed, projected = sl.step(WEIGH), sl.step(PROJECT)
                if weighed:
                    exponentials(weighed, (0, 1))
                if projected:
                    s, u = projected
                    act.wait_ge(q_ps, s + 1)
                    wait(act, q_ready, s)
                    nc.scalar.activation(signed[0][:, :, :], grouped(ps_qk), ACT.Identity, scale=c.w["a0_split"][:, 0:1],
                                         bias=c.w["a0_split"][:, 2:3]).then_inc(q_signed, 1)
                if at := sl.step(VALUE):
                    s, u = at
                    act.wait_ge(o_ps, s + 1)
                    wait(act, z_ps, s)
                    nc.scalar.activation(oz[:, :], ps_o[:, :], ACT.Copy).then_inc(oz_ready, 1)
                if at := sl.step(TURN):
                    s, u = at
                    act.wait_ge(xT_ps, s + 1)
                    wait(act, v_ps, s - 1)
                    nc.scalar.activation(xT[:, u % 2, :], ps_x, ACT.Copy).then_inc(xT_ready, 1)
                if weighed:
                    exponentials(weighed, (2,))
                if projected:
                    s, u = projected
                    act.wait_ge(k_ps, s + 1)
                    wait(act, k_ready, s)
                    nc.scalar.activation(signed[1][:, :, :], grouped(ps_qk), ACT.Identity, scale=c.w["a0_split"][:, 3:4],
                                         bias=c.w["a0_split"][:, 5:6]).then_inc(k_signed, 1)
                    act.wait_ge(v_ps, s + 1)
                    wait(act, o_ps, s - 3)
                    nc.scalar.activation(v1[:, u, :, 0:HD], ps_v.rearrange("p (h d) -> p h d", d=HD), ACT.Copy).then_inc(v_ready, 1)
                if weighed:
                    exponentials(weighed, (3,))
                if at := sl.step(LAST):
                    s, u = at
                    act.wait_ge(oT_ps, s + 1)
                    wait(act, y_ps, s)
                    nc.scalar.activation(oT[:, :], ps_oT, ACT.Copy).then_inc(oT_ready, 1)

            run_slots(act, slot, B, LAG)

        @block.sync
        def _(sp):
            for name, tile in c.later:
                sp.dma_start(tile, c.inp[name]).then_inc(c.rest, 16)

        @block.gpsimd
        def _(pool):
            nc.gpsimd.memset(v1[:, :, :, :], 1.0).then_inc(made, 1)

        @block.vector
        def _(dve):
            nc.vector.memset(pad[:, :, :, :, :], 0.0)

            def strips(t):
                return t.rearrange("p (t j) -> p j t", t=GROUPS)

            def maxima(at, groups):
                s, u = at
                for g in groups:
                    dve.wait_ge(nat_ps, s * GROUPS + g + 1)
                    nc.vector.tensor_reduce(nmax[:, GROUP * g:GROUP * g + GROUP],
                                            ps_n[g % 2][:, :].rearrange("p (t k) -> p t k", t=GROUP),
                                            AX.X, ALU.max, negate=True).then_inc(max_done, 1)

            def parts(at, n, out, done, ready):
                s, u = at
                dve.wait_ge(done, s + 1)
                nc.vector.scalar_tensor_tensor(out=out[:, u, :, :], in0=grouped(ps_qk), scalar=c.w["a0_split"][:, 3 * n + 1:3 * n + 2],
                                               in1=signed[n][:, :, :].bitcast(F32), op0=ALU.mult, op1=ALU.add).then_inc(ready, 1)

            def slot(sl):
                scored, projected = sl.step(SCORE), sl.step(PROJECT)
                if scored:
                    maxima(scored, (0, 1))
                if projected:
                    wait(dve, shift_ready, projected[0] - 3)
                    parts(projected, 0, q, q_signed, q_ready)
                if scored:
                    maxima(scored, (2,))
                if projected:
                    wait(dve, sT_ps, GROUPS * (projected[0] - 3))
                    parts(projected, 1, k, k_signed, k_ready)
                if scored:
                    maxima(scored, (3,))
                if at := sl.step(VALUE):
                    s, u = at
                    dve.wait_ge(z_ps, s + 1)
                    z = ps_z[:, :].rearrange("p (j g r) -> p g j r", j=GROUP, g=GROUPS)
                    heads = rz[:, :].rearrange("p (g j) -> p g j", g=GROUPS)
                    nc.vector.reciprocal(heads, z[:, :, :, HD]).then_inc(rz_ready, 1)
                    dve.wait_ge(rz_ready, s + 1)
                    wait(dve, oT_ps, s - 1)
                    nc.vector.tensor_tensor(o[:, u % 2, :].rearrange("p (g j d) -> p g j d", g=GROUPS, j=GROUP), z[:, :, :, 0:HD],
                                            heads.unsqueeze(3).broadcast_to([P, GROUPS, GROUP, HD]), ALU.mult).then_inc(o_ready, 1)
                if at := sl.step(SHIFT):
                    s, u = at
                    dve.wait_ge(pad_ps, s + 1)
                    wait(dve, sT_ps, GROUPS * (s - 1))
                    nc.vector.tensor_tensor(q_shift[:, u % 2, :, :], q[:, u, :, :].bitcast(F32), grouped(ps_qk),
                                            ALU.add).then_inc(shift_ready, 1)
                if scored:
                    s, u = scored
                    dve.wait_ge(max_done, (s + 1) * GROUPS)
                    wait(dve, pad_ps, s - 1)
                    left = nmax[:, :]
                    for n in range(2):
                        nc.vector.tensor_copy(part[:, n, :], left).then_inc(own, 1)
                        dve.wait_ge(own, 4 * s + 2 * n + 1)
                        nc.vector.tensor_copy(pad[:, u % 2, :, :, 3 * HD + n], strips(part[:, n, :]))
                        nc.vector.tensor_tensor(rest[:, n, :], left, part[:, n, :], ALU.subtract).then_inc(own, 1)
                        left = rest[:, n, :]
                        dve.wait_ge(own, 4 * s + 2 * n + 2)
                    nc.vector.tensor_copy(pad[:, u % 2, :, :, 3 * HD + 2], strips(left)).then_inc(pad_ready, 1)
                if at := sl.step(0):
                    s, u = at
                    wait(dve, xT_ps, s - 1)
                    nc.vector.tensor_scalar(xn[:, u % 2, :], c.x[:, s, :], c.mean[:, bass.ds(s, 1)], c.rstd[:, bass.ds(s, 1)],
                                            ALU.subtract, ALU.mult).then_inc(xn_ready, 1)
                if at := sl.step(LAST):
                    s, u = at
                    dve.wait_ge(y_ps, s + 1)
                    nc.vector.tensor_tensor(c.x[:, s, :], c.x[:, s, :], ps_y, ALU.add).then_inc(x_done, 1)
                    dve.wait_ge(x_done, s + 1)
                    nc.vector.bn_stats(c.stats[:, s, :], c.x[:, s, :])

            run_slots(dve, slot, B, LAG)


def wide_weights(c):
    nc = c.nc
    ctx, sb, ps, sem = stage_scope(c)
    with ctx:
        bank = [ps(f"bank{n}") for n in range(4)]
        tg = sb("tg", [P, 1])
        ready, copied, gated, done = sem("ready"), sem("copied"), sem("gated"), sem("done")
        block = ctx.enter_context(nc.Block())

        @block.sync
        def _(sp):
            sp.wait_ge(c.rest, c.rest_count)

        @block.tensor
        def _(pe):
            pe.wait_ge(c.rest, c.rest_count)
            for h in range(HEADS):
                ins = nc.tensor.matmul(bank[h // 4][:, (h % 4) * P:(h % 4) * P + P], c.w["x0_k"][:, h, :], c.w["x0_q"][:, h, :],
                                       start=True, stop=True)
                if h % 4 == 3:
                    ins.then_inc(ready, 1)

        @block.scalar
        def _(act):
            act.wait_ge(c.rest, c.rest_count)
            nc.scalar.activation(tg[:, :], c.w["x0_gate"][:, :], ACT.Tanh).then_inc(gated, 1)
            for n in range(4):
                act.wait_ge(ready, n + 1)
                nc.scalar.activation(c.x0_a[:, 4 * n:4 * n + 4, :], bank[n][:, :].rearrange("p (h d) -> p h d", h=4),
                                     ACT.Copy).then_inc(copied, 1)

        @block.vector
        def _(dve):
            dve.wait_ge(gated, 1)
            nc.vector.tensor_scalar(c.x0_o[:, :, :], c.w["x0_out"][:, :, :], tg[:, 0:1], None, ALU.mult).then_inc(done, 1)
            nc.vector.tensor_scalar(c.x0_b[:, :], c.w["x0_bias"][:, :], tg[:, 0:1], None, ALU.mult).then_inc(done, 1)


def cross_attention_wide(c):
    nc, B = c.nc, c.B
    K = c.keys
    DH = 64
    PAIRS = HEADS // 2
    BATCHES = 4
    ctx, sb, ps, sem = stage_scope(c)
    with ctx:
        cx = sb("cx", [P, 2, K])
        xn = sb("xn", [P, 2, D])
        xT = sb("xT", [P, 2, P])
        uu = sb("uu", [P, 2, HEADS, BATCHES, K])
        v = sb("v", [K, 2, HEADS * DH])
        top = sb("top", [P, HEADS])
        z, rz = sb("z", [P, HEADS]), sb("rz", [P, HEADS])
        p = sb("p", [P, 4, HEADS, K])
        pT = sb("pT", [K, 2, HEADS, P])
        oT = sb("oT", [P, 2, PAIRS, P])

        ps_misc, ps_o = ps("ps_misc"), ps("ps_o")
        ps_x, ps_y = ps_misc[:, 0:P], ps_misc[:, P:2 * P]
        ps_u = [ps(f"ps_u{i}") for i in range(2)]
        ps_n = [ps(f"ps_n{i}") for i in range(2)]
        ps_t = [ps(f"ps_t{i}") for i in range(2)]

        names = ("xn_ready", "xT_ps", "xT_ready", "u_ps", "u_ready", "v_ps", "v_ready", "s_ps", "max_done", "d_ready",
                 "exp_done", "z_done", "rz_done", "p_ready", "pT_ps", "pT_ready", "o_ps", "oT_ready", "y_ps", "x_done", "cx_ready", "biased")
        (xn_ready, xT_ps, xT_ready, u_ps, u_ready, v_ps, v_ready, s_ps, max_done, d_ready,
         exp_done, z_done, rz_done, p_ready, pT_ps, pT_ready, o_ps, oT_ready, y_ps, x_done, cx_ready, biased) = (sem(n) for n in names)
        block = ctx.enter_context(nc.Block())
        NORM, TURN, SCORE, WEIGH, SPREAD, VALUE, LAST = 2, 3, 4, 5, 6, 7, 8
        LAG, BODY = LAST, 2 * BATCHES

        def four(t, g):
            return t[:, 4 * g:4 * g + 4]

        def bank_heads(bank, rows=P, cols=K):
            return bank[0:rows, 0:4 * cols].rearrange("p (h k) -> p h k", h=4)

        @block.tensor
        def _(pe):
            def scores(at, g):
                s, u = at
                if g == 0:
                    pe.wait_ge(xT_ready, s + 1)
                    pe.wait_ge(u_ready, 4 * (s - u % 4 + 4))
                wait(pe, d_ready, 4 * s + g - 1)
                nc.tensor.matmul(ps_n[g % 2][:, 0:4 * K], xT[:, u % 2, :], four(uu[:, u // 4], g)[:, :, u % 4, :],
                                 start=True, stop=True).then_inc(s_ps, 1)

            def outputs(at, half):
                s, u = at
                if half == 0:
                    pe.wait_ge(pT_ready, (s + 1) * 4)
                    pe.wait_ge(v_ready, 2 * (s + 1))
                wait(pe, oT_ready, 2 * s + half)
                for n in range(PAIRS // 2):
                    for odd in range(2):
                        h = half * PAIRS + 2 * n + odd
                        ins = nc.tensor.matmul(ps_o[DH * odd:DH * odd + DH, n * P:n * P + P], v[:, u % 2, h * DH:h * DH + DH],
                                               pT[:, u % 2, h, :], start=True, stop=True)
                ins.then_inc(o_ps, 1)

            def transposes(at, g):
                s, u = at
                if g == 0:
                    pe.wait_ge(p_ready, s + 1)
                wait(pe, pT_ready, 4 * s + g - 1)
                for n in range(4):
                    ins = nc.tensor.transpose(ps_t[g % 2][0:K, n * P:n * P + P], p[:, u % 4, 4 * g + n, :], c.ident[:, :])
                ins.then_inc(pT_ps, 1)

            def slot(sl):
                scored, spread, valued = sl.step(SCORE), sl.step(SPREAD), sl.step(VALUE)
                if scored:
                    scores(scored, 0)
                    scores(scored, 1)
                if valued:
                    outputs(valued, 0)
                if at := sl.step(TURN):
                    s, u = at
                    pe.wait_ge(xn_ready, s + 1)
                    wait(pe, x_done, s + TURN - LAST)
                    nc.tensor.transpose(ps_x, xn[:, u % 2, :], c.ident[:, :]).then_inc(xT_ps, 1)
                if scored:
                    scores(scored, 2)
                if spread:
                    transposes(spread, 0)
                    transposes(spread, 1)
                if valued:
                    outputs(valued, 1)
                if scored:
                    scores(scored, 3)
                if spread:
                    transposes(spread, 2)
                    transposes(spread, 3)
                if at := sl.step(0):
                    s, u = at
                    for n in range(4):
                        if n < 2 and not (sl.fixed and s <= SPREAD):
                            pe.wait_ge(v_ready, 2 * (s - SPREAD - 1) + n + 1)
                        else:
                            wait(pe, u_ready, 4 * s + n - 1)
                        nc.tensor.matmul(ps_u[n % 2][:, 0:BATCHES * K], c.x0_a[:, 4 * (u % 4) + n, :],
                                         c.ctx[:, bass.ds(s - u % 4, BATCHES), :], start=True, stop=True).then_inc(u_ps, 1)
                if spread:
                    s, u = spread
                    pe.wait_ge(cx_ready, s + 1)
                    for half in range(2):
                        done = 4 * (s + SPREAD + 1) - 1 + half
                        pe.wait_ge(u_ready, min(done, 4 * B) if sl.fixed else done)
                        wait(pe, v_ready, 2 * (s - 1) + half + 1)
                        nc.tensor.matmul(ps_u[half][0:K, :], cx[:, u % 2, :], c.w["x0_v"][:, half * 512:half * 512 + 512],
                                         start=True, stop=True).then_inc(v_ps, 1)
                if at := sl.step(LAST):
                    s, u = at
                    pe.wait_ge(oT_ready, 2 * (s + 1))
                    turned = s + LAST - TURN + 1
                    wait(pe, xT_ready, min(turned, B) if sl.fixed else turned)
                    wait(pe, x_done, s)
                    for n in range(PAIRS):
                        ins = nc.tensor.matmul(ps_y, oT[:, u % 2, n, :], c.x0_o[:, n, :], start=n == 0, stop=n == PAIRS - 1)
                    ins.then_inc(y_ps, 1)

            run_slots(pe, slot, B, LAG, BODY)

        @block.scalar
        def _(act):
            def outputs(at, half):
                s, u = at
                act.wait_ge(o_ps, 2 * s + half + 1)
                if half == 0:
                    wait(act, y_ps, s - 1)
                nc.scalar.activation(oT[:, u % 2, 4 * half:4 * half + 4, :], ps_o[:, :].rearrange("p (n q) -> p n q", n=4),
                                     ACT.Copy).then_inc(oT_ready, 1)

            def transposed(at, groups):
                s, u = at
                for g in groups:
                    act.wait_ge(pT_ps, 4 * s + g + 1)
                    if g == 0:
                        wait(act, o_ps, 2 * (s - 1))
                    nc.scalar.activation(four(pT[:, u % 2], g), bank_heads(ps_t[g % 2], K, P), ACT.Copy).then_inc(pT_ready, 1)

            def slot(sl):
                spread, valued = sl.step(SPREAD), sl.step(VALUE)
                if valued:
                    outputs(valued, 0)
                if at := sl.step(TURN):
                    s, u = at
                    act.wait_ge(xT_ps, s + 1)
                    wait(act, s_ps, 4 * (s - 1))
                    nc.scalar.activation(xT[:, u % 2, :], ps_x, ACT.Identity, scale=c.w["x0_ln"][:, 0:1],
                                         bias=c.w["x0_ln"][:, 1:2]).then_inc(xT_ready, 1)
                if spread:
                    transposed(spread, (0, 1))
                if valued:
                    outputs(valued, 1)
                if spread:
                    transposed(spread, (2, 3))
                    s, u = spread
                    for half in range(2):
                        act.wait_ge(v_ps, 2 * s + half + 1)
                        wait(act, o_ps, 2 * (s - 1))
                        nc.scalar.activation(v[:, u % 2, half * 512:half * 512 + 512], ps_u[half][0:K, :], ACT.Copy).then_inc(v_ready, 1)
                if at := sl.step(SCORE):
                    s, u = at
                    act.wait_ge(d_ready, 4 * (s + 1))
                    nc.scalar.activation(p[:, u % 4, :, :], p[:, u % 4, :, :], ACT.Exp, scale=DH ** -0.5).then_inc(exp_done, 1)

            run_slots(act, slot, B, LAG, BODY)

        @block.gpsimd
        def _(pool):
            def slot(sl):
                if at := sl.step(TURN):
                    s, u = at
                    pool.wait_ge(xn_ready, s + 1)
                    nc.gpsimd.tensor_tensor(c.x[:, s, :], c.x[:, s, :], c.x0_b[:, :], ALU.add).then_inc(biased, 1)
                if at := sl.step(WEIGH):
                    s, u = at
                    wait(pool, v_ps, 2 * (s - 1))
                    nc.gpsimd.tensor_copy(cx[:, u % 2, :], c.ctx[:, s, :]).then_inc(cx_ready, 1)
                    pool.wait_ge(rz_done, s + 1)
                    nc.gpsimd.tensor_tensor(p[:, u % 4, :, :], p[:, u % 4, :, :], rz[:, :].unsqueeze(2).broadcast_to([P, HEADS, K]),
                                            ALU.mult).then_inc(p_ready, 1)

            run_slots(pool, slot, B, LAG, BODY)

        @block.vector
        def _(dve):
            def differences(at, groups):
                s, u = at
                for g in groups:
                    dve.wait_ge(s_ps, 4 * s + g + 1)
                    if g == 0:
                        wait(dve, pT_ps, 4 * (s - 3))
                    nc.vector.tensor_reduce(four(top, g), bank_heads(ps_n[g % 2]), AX.X, ALU.max).then_inc(max_done, 1)
                    dve.wait_ge(max_done, 4 * s + g + 1)
                    nc.vector.tensor_tensor(four(p[:, u % 4], g), bank_heads(ps_n[g % 2]),
                                            four(top, g).unsqueeze(2).broadcast_to([P, 4, K]), ALU.subtract).then_inc(d_ready, 1)

            def slot(sl):
                scored = sl.step(SCORE)
                if scored:
                    differences(scored, (0, 1))
                if at := sl.step(WEIGH):
                    s, u = at
                    dve.wait_ge(exp_done, s + 1)
                    wait(dve, p_ready, s)
                    nc.vector.tensor_reduce(z[:, :], p[:, u % 4, :, :], AX.X, ALU.add).then_inc(z_done, 1)
                    dve.wait_ge(z_done, s + 1)
                    nc.vector.reciprocal(rz[:, :], z[:, :]).then_inc(rz_done, 1)
                if scored:
                    differences(scored, (2, 3))
                if at := sl.step(NORM):
                    s, u = at
                    wait(dve, xT_ps, s - 1)
                    nc.vector.tensor_scalar(xn[:, u % 2, :], c.x[:, s, :], c.mean[:, bass.ds(s, 1)], c.rstd[:, bass.ds(s, 1)],
                                            ALU.subtract, ALU.mult).then_inc(xn_ready, 1)
                if at := sl.step(0):
                    s, u = at
                    wait(dve, s_ps, 4 * (s - u % 4 - 4))
                    for n in range(4):
                        dve.wait_ge(u_ps, 4 * s + n + 1)
                        nc.vector.tensor_copy(uu[:, u // 4, 4 * (u % 4) + n, :, :],
                                              ps_u[n % 2][:, 0:BATCHES * K].rearrange("p (b k) -> p b k", b=BATCHES)).then_inc(u_ready, 1)
                if at := sl.step(LAST):
                    s, u = at
                    dve.wait_ge(y_ps, s + 1)
                    dve.wait_ge(biased, s + 1)
                    nc.vector.tensor_tensor(c.x[:, s, :], c.x[:, s, :], ps_y, ALU.add).then_inc(x_done, 1)
                    dve.wait_ge(x_done, s + 1)
                    nc.vector.bn_stats(c.stats[:, s, :], c.x[:, s, :])

            run_slots(dve, slot, B, LAG, BODY)


def top_two(c, dve, own, base, score, sel, gt, ge, rank, tri, out):
    nc = c.nc
    T, E = score.shape[1], score.shape[2]
    other = score.unsqueeze(2).broadcast_to([P, T, E, E])
    mine = score.unsqueeze(3).broadcast_to([P, T, E, E])
    behind, ahead = (tri[:, n, :, :].unsqueeze(1).broadcast_to([P, T, E, E]) for n in range(2))
    nc.vector.tensor_tensor(gt, other, mine, ALU.is_gt)
    nc.vector.tensor_tensor(ge, other, mine, ALU.is_ge).then_inc(own, 1)
    dve.wait_ge(own, base + 1)
    nc.vector.tensor_tensor(gt, gt, behind, ALU.mult)
    nc.vector.tensor_tensor(ge, ge, ahead, ALU.mult).then_inc(own, 1)
    dve.wait_ge(own, base + 2)
    nc.vector.tensor_tensor(gt, gt, ge, ALU.add).then_inc(own, 1)
    dve.wait_ge(own, base + 3)
    nc.vector.tensor_reduce(rank, gt, AX.X, ALU.add).then_inc(own, 1)
    dve.wait_ge(own, base + 4)
    return nc.vector.scalar_tensor_tensor(out=out, in0=rank, scalar=2.0, in1=sel, op0=ALU.is_lt, op1=ALU.mult)


def scored_experts(c):
    nc = c.nc
    T = 4
    N = T * P
    steps = c.B // T
    E, H = 8, 352
    CH = [P, P, H - 2 * P]
    ctx, sb, ps, sem = stage_scope(c)
    with ctx:
        w_hi = [sb(f"w{n}_hi", [D, E * H], F32R) for n in range(2)]
        w_lo = [sb(f"w{n}_lo", [D, E * H], F32R) for n in range(2)]
        w3 = sb("w3", [P, E, 3, D])
        raw_in, w3_in, split_hi, split_lo = sem("raw_in0"), sem("w3_in"), sem("split_hi"), sem("split_lo")
        raw_in2 = sem("raw_in1")
        with nc.sbuf_tensor("f0_raw", [D, 2, E * H], F32) as raw, nc.Block() as block:
            @block.sync
            def _(sp):
                for n, (name, arrived) in enumerate((("late_f0_1", raw_in), ("late_f0_2", raw_in2))):
                    sp.dma_start(raw[:, n, :], c.inp[name]).then_inc(arrived, 16)
                sp.dma_start(w3[:, :, :, :], c.inp["late_f0_3"]).then_inc(w3_in, 16)
                sp.wait_ge(w3_in, 16)

            @block.scalar
            def _(act):
                for n, arrived in enumerate((raw_in, raw_in2)):
                    act.wait_ge(arrived, 16)
                    nc.scalar.activation(w_hi[n][:, :], raw[:, n, :], ACT.Copy).then_inc(split_hi, 1)

            @block.vector
            def _(dve):
                for n in range(2):
                    dve.wait_ge(split_hi, n + 1)
                    nc.vector.tensor_tensor(w_lo[n][:, :], raw[:, n, :], w_hi[n][:, :].bitcast(F32), ALU.subtract).then_inc(split_lo, 1)
                dve.wait_ge(split_lo, 2)

        xn = sb("xn", [P, 2, T, D])
        xT = sb("xT", [D, N])
        x_hi, x_lo = sb("x_hi", [D, 2, N], F32R), sb("x_lo", [D, 2, N], F32R)
        sg = sb("sg", [P, 2, N])
        act_in = sb("act", [P, 2, 3, N])
        sc, rank, wt = sb("sc", [P, T, E]), sb("rank", [P, T, E]), sb("wt", [P, 2, T, E])
        gt, ge = sb("gt", [P, T, E, E]), sb("ge", [P, T, E, E])

        ps_g, ps_u, ps_y = ([ps(f"ps_{n}{i}") for i in range(2)] for n in "guy")
        ps_x, ps_r = ps("ps_x"), ps("ps_r")
        names = ("xn_ready", "xT_ps", "xT_ready", "hi_ready", "lo_ready", "r_ps", "sc_ready", "own", "w_ready",
                 "g_ps", "u_ps", "sg_ready", "act_ready", "y_ps", "y_taken", "stats_done")
        (xn_ready, xT_ps, xT_ready, hi_ready, lo_ready, r_ps, sc_ready, own, w_ready,
         g_ps, u_ps, sg_ready, act_ready, y_ps, y_taken, stats_done) = (sem(n) for n in names)
        block = ctx.enter_context(nc.Block())
        LAG, TURN = 2, 4
        NCH = 3 * E
        x4 = c.x[:, :, :].rearrange("p (s i) d -> p s i d", i=T)
        st4 = c.stats[:, :, :].rearrange("p (s i) k -> p s i k", i=T)
        mean4 = c.mean[:, :].rearrange("p (s i) -> p s i", i=T)
        rstd4 = c.rstd[:, :].rearrange("p (s i) -> p s i", i=T)

        @block.tensor
        def _(pe):
            def hidden(at, e):
                s, u = at
                if e == 0:
                    pe.wait_ge(hi_ready, s + 1)
                    pe.wait_ge(lo_ready, s + 1)
                for k, m in enumerate(CH):
                    n = 3 * e + k
                    cols = slice(e * H + k * P, e * H + k * P + m)
                    for w, bank, taken, ready in ((0, ps_g, sg_ready, g_ps), (1, ps_u, act_ready, u_ps)):
                        wait(pe, taken, s * NCH + n - 1)
                        out = bank[n % 2][0:m, :]
                        nc.tensor.matmul(out, w_hi[w][:, cols], x_hi[:, u % 2, :], start=True, stop=False)
                        nc.tensor.matmul(out, w_hi[w][:, cols], x_lo[:, u % 2, :], start=False, stop=False)
                        nc.tensor.matmul(out, w_lo[w][:, cols], x_hi[:, u % 2, :], start=False, stop=True).then_inc(ready, 1)

            def down(at, e):
                s, u = at
                pe.wait_ge(act_ready, s * NCH + 3 * e + 3)
                wait(pe, y_taken, s * E + e - 1)
                for i in range(T):
                    for k, m in enumerate(CH):
                        ins = nc.tensor.matmul(ps_y[e % 2][:, i * P:i * P + P], act_in[0:m, e % 2, k, i * P:i * P + P],
                                               w3[0:m, e, k, :], start=k == 0, stop=k == 2)
                ins.then_inc(y_ps, 1)

            def transposes(at):
                s, u = at
                pe.wait_ge(xn_ready, s + 1)
                wait(pe, lo_ready, s)
                for i in range(T):
                    ins = nc.tensor.transpose(ps_x[:, i * P:i * P + P], xn[:, u % 2, i, :], c.ident[:, :])
                ins.then_inc(xT_ps, 1)

            def router(at):
                s, u = at
                pe.wait_ge(xT_ready, s + 1)
                wait(pe, sc_ready, s)
                for i in range(T):
                    ins = nc.tensor.matmul(ps_r[:, i * E:i * E + E], xT[:, i * P:i * P + P], c.w["f0_router"][:, :],
                                           start=True, stop=True)
                ins.then_inc(r_ps, 1)

            def slot(sl):
                main, ahead = sl.step(2), sl.step(1)
                for e in range(E):
                    if main:
                        hidden(main, e)
                        if e:
                            down(main, e - 1)
                    if ahead and e == TURN:
                        transposes(ahead)
                    if ahead and e == TURN + 2:
                        router(ahead)
                if main:
                    down(main, E - 1)

            run_slots(pe, slot, steps, LAG, 2)

        @block.scalar
        def _(act):
            def slot(sl):
                main, ahead = sl.step(2), sl.step(1)
                for e in range(E):
                    if main:
                        s, u = main
                        for k, m in enumerate(CH):
                            n = 3 * e + k
                            act.wait_ge(g_ps, s * NCH + n + 1)
                            wait(act, act_ready, s * NCH + n - 1)
                            nc.scalar.activation(sg[0:m, n % 2, :], ps_g[n % 2][0:m, :], ACT.Silu).then_inc(sg_ready, 1)
                    if ahead and e == TURN:
                        s, u = ahead
                        act.wait_ge(xT_ps, s + 1)
                        wait(act, r_ps, s)
                        nc.scalar.activation(xT[:, :], ps_x[:, :], ACT.Copy).then_inc(xT_ready, 1)
                        nc.scalar.activation(x_hi[:, u % 2, :], ps_x[:, :], ACT.Copy).then_inc(hi_ready, 1)

            run_slots(act, slot, steps, LAG, 2)

        @block.vector
        def _(dve):
            def add(at, e):
                s, u = at
                dve.wait_ge(y_ps, s * E + e + 1)
                wait(dve, y_taken, s * E + e)
                for i in range(T):
                    ins = nc.vector.scalar_tensor_tensor(out=x4[:, s, i, :], in0=ps_y[e % 2][:, i * P:i * P + P],
                                                         scalar=wt[:, u % 2, i, e:e + 1], in1=x4[:, s, i, :],
                                                         op0=ALU.mult, op1=ALU.add)
                ins.then_inc(y_taken, 1)

            def slot(sl):
                if at := sl.step(0):
                    s, u = at
                    wait(dve, xT_ps, s - 1)
                    for i in range(T):
                        ins = nc.vector.tensor_scalar(xn[:, u % 2, i, :], x4[:, s, i, :], mean4[:, s, i:i + 1], rstd4[:, s, i:i + 1],
                                                      ALU.subtract, ALU.mult)
                    ins.then_inc(xn_ready, 1)
                main, ahead = sl.step(2), sl.step(1)
                for e in range(E):
                    if main:
                        s, u = main
                        if e == 0:
                            dve.wait_ge(w_ready, s + 1)
                        for k, m in enumerate(CH):
                            n = 3 * e + k
                            dve.wait_ge(sg_ready, s * NCH + n + 1)
                            dve.wait_ge(u_ps, s * NCH + n + 1)
                            if k == 0:
                                wait(dve, y_ps, s * E + e - 1)
                            nc.vector.tensor_tensor(act_in[0:m, e % 2, k, :], sg[0:m, n % 2, :], ps_u[n % 2][0:m, :],
                                                    ALU.mult).then_inc(act_ready, 1)
                        if e:
                            add(main, e - 1)
                    if ahead and e == TURN:
                        s, u = ahead
                        dve.wait_ge(hi_ready, s + 1)
                        nc.vector.tensor_tensor(x_lo[:, u % 2, :], ps_x[:, :], x_hi[:, u % 2, :].bitcast(F32),
                                                ALU.subtract).then_inc(lo_ready, 1)
                    if ahead and e == TURN + 2:
                        s, u = ahead
                        dve.wait_ge(r_ps, s + 1)
                        nc.vector.tensor_copy(sc[:, :, :], ps_r[:, 0:T * E].rearrange("p (i e) -> p i e", i=T)).then_inc(sc_ready, 1)
                        dve.wait_ge(sc_ready, s + 1)
                        top_two(c, dve, own, 4 * s, sc[:, :, :], sc[:, :, :], gt[:, :, :, :], ge[:, :, :, :], rank[:, :, :],
                                c.w["tri8"][:, :, :, :], wt[:, u % 2, :, :]).then_inc(w_ready, 1)
                if main:
                    add(main, E - 1)
                    s, u = main
                    dve.wait_ge(y_taken, (s + 1) * E)
                    for i in range(T):
                        nc.vector.bn_stats(st4[:, s, i, :], x4[:, s, i, :])

            run_slots(dve, slot, steps, LAG, 2)


def attention_over_heads(c):
    nc, B = c.nc, c.B
    A = P // HEADS
    ctx, sb, ps, sem = stage_scope(c)
    with ctx:
        xn, xT = sb("xn", [P, 2, D]), sb("xT", [P, 2, P])
        qkv = sb("qkv", [P, UNROLL, 3, HEADS, HD])
        qk = sb("qk", [P, 2, HD, HEADS, HEADS])
        top, dif = sb("top", [P, HEADS]), sb("dif", [P, 2, HEADS, HEADS])
        e = sb("e", [P, 2, HEADS, HEADS])
        z, rz = sb("z", [P, HEADS]), sb("rz", [P, HEADS])
        ev = sb("ev", [P, HEADS, HD, HEADS])
        sums, o = sb("sums", [P, HEADS, HD]), sb("o", [P, 2, HEADS, HD])
        r = sb("r", [P, 2, HD, HEADS, A])
        ps_x, ps_qkv, ps_y = ps("ps_x"), ps("ps_qkv"), ps("ps_y")
        ps_s = [ps(f"ps_s{i}") for i in range(2)]
        names = ("xn_ready", "xT_ps", "xT_ready", "qkv_ps", "qkv_ready", "qk_ready", "s_ps", "top_done", "dif_ready", "exp_done",
                 "z_done", "rz_done", "ev_low", "ev_done", "sums_done", "o_ready", "r_ready", "y_ps", "x_done", "biased")
        (xn_ready, xT_ps, xT_ready, qkv_ps, qkv_ready, qk_ready, s_ps, top_done, dif_ready, exp_done,
         z_done, rz_done, ev_low, ev_done, sums_done, o_ready, r_ready, y_ps, x_done, biased) = (sem(n) for n in names)
        block = ctx.enter_context(nc.Block())
        TURN, PROJECT, MULTIPLY, SCORE, WEIGH, SPREAD, LAST = 1, 2, 3, 4, 5, 6, 7
        LAG = LAST
        full = [P, HD, HEADS, HEADS]
        LOW = 3

        def weighted(eng, u, first, last):
            n = [P, last - first, HD, HEADS]
            return eng.tensor_tensor(ev[:, first:last, :, :], e[:, u % 2, first:last, :].unsqueeze(2).broadcast_to(n),
                                     qkv[:, u, 2, :, :].rearrange("p h d -> p d h").unsqueeze(1).broadcast_to(n), ALU.mult)

        @block.tensor
        def _(pe):
            def slot(sl):
                if at := sl.step(SCORE):
                    s, u = at
                    pe.wait_ge(qk_ready, s + 1)
                    wait(pe, dif_ready, s - 1)
                    for k in range(HD):
                        ins = nc.tensor.matmul(ps_s[u % 2][:, 0:HEADS * HEADS], c.ident[:, :], qk[:, u % 2, k, :, :],
                                               start=k == 0, stop=k == HD - 1)
                    ins.then_inc(s_ps, 1)
                if at := sl.step(TURN):
                    s, u = at
                    pe.wait_ge(xn_ready, s + 1)
                    wait(pe, xT_ready, s)
                    nc.tensor.transpose(ps_x[:, 0:P], xn[:, u % 2, :], c.ident[:, :]).then_inc(xT_ps, 1)
                if at := sl.step(PROJECT):
                    s, u = at
                    pe.wait_ge(xT_ready, s + 1)
                    wait(pe, qkv_ready, s)
                    nc.tensor.matmul(ps_qkv[:, 0:3 * D], xT[:, u % 2, :], c.w["a1_qkv"][:, :], start=True, stop=True).then_inc(qkv_ps, 1)
                if at := sl.step(LAST):
                    s, u = at
                    pe.wait_ge(r_ready, s + 1)
                    wait(pe, x_done, s)
                    for k in range(HD):
                        ins = nc.tensor.matmul(ps_y[:, 0:D], r[:, u % 2, k, :, :], c.w["a1_o"][:, k, :], start=k == 0, stop=k == HD - 1)
                    ins.then_inc(y_ps, 1)

            run_slots(pe, slot, B, LAG)

        @block.scalar
        def _(act):
            def slot(sl):
                if at := sl.step(TURN):
                    s, u = at
                    act.wait_ge(xT_ps, s + 1)
                    wait(act, qkv_ps, s - 1)
                    nc.scalar.activation(xT[:, u % 2, :], ps_x[:, 0:P], ACT.Copy).then_inc(xT_ready, 1)
                if at := sl.step(PROJECT):
                    s, u = at
                    act.wait_ge(qkv_ps, s + 1)
                    wait(act, ev_done, s - 3)
                    wait(act, ev_low, s - 3)
                    nc.scalar.activation(qkv[:, u, :, :, :], ps_qkv[:, 0:3 * D].rearrange("p (n h d) -> p n h d", n=3, h=HEADS),
                                         ACT.Copy).then_inc(qkv_ready, 1)
                if at := sl.step(SPREAD):
                    s, u = at
                    act.wait_ge(o_ready, s + 1)
                    wait(act, y_ps, s - 1)
                    for a in range(A):
                        ins = nc.scalar.activation(r[:, u % 2, :, :, a], o[:, u % 2, :, :].rearrange("p h d -> p d h"), ACT.Copy,
                                                   scale=c.w["a1_rows"][:, a:a + 1])
                    ins.then_inc(r_ready, 1)
                if at := sl.step(SCORE):
                    s, u = at
                    act.wait_ge(dif_ready, s + 1)
                    wait(act, ev_done, s - 1)
                    wait(act, ev_low, s - 1)
                    nc.scalar.activation(e[:, u % 2, :, :], dif[:, u % 2, :, :], ACT.Exp, scale=HD ** -0.5).then_inc(exp_done, 1)

            run_slots(act, slot, B, LAG)

        @block.gpsimd
        def _(pool):
            def slot(sl):
                if at := sl.step(TURN):
                    s, u = at
                    pool.wait_ge(xn_ready, s + 1)
                    nc.gpsimd.tensor_tensor(c.x[:, s, :], c.x[:, s, :], c.w["a1_b"][:, :], ALU.add).then_inc(biased, 1)
                if at := sl.step(WEIGH):
                    s, u = at
                    pool.wait_ge(exp_done, s + 1)
                    wait(pool, sums_done, s)
                    weighted(nc.gpsimd, u, 0, LOW).then_inc(ev_low, 1)
                if at := sl.step(MULTIPLY):
                    s, u = at
                    pool.wait_ge(qkv_ready, s + 1)
                    wait(pool, s_ps, s - 1)
                    nc.gpsimd.tensor_tensor(qk[:, u % 2, :, :, :], qkv[:, u, 0, :, :].rearrange("p h d -> p d h").unsqueeze(3).broadcast_to(full),
                                            qkv[:, u, 1, :, :].rearrange("p h d -> p d h").unsqueeze(2).broadcast_to(full), ALU.mult).then_inc(qk_ready, 1)

            run_slots(pool, slot, B, LAG)

        @block.vector
        def _(dve):
            def slot(sl):
                if at := sl.step(0):
                    s, u = at
                    wait(dve, xT_ps, s - 1)
                    nc.vector.tensor_scalar(xn[:, u % 2, :], c.x[:, s, :], c.mean[:, bass.ds(s, 1)], c.rstd[:, bass.ds(s, 1)],
                                            ALU.subtract, ALU.mult).then_inc(xn_ready, 1)
                if at := sl.step(WEIGH):
                    s, u = at
                    dve.wait_ge(exp_done, s + 1)
                    wait(dve, o_ready, s)
                    nc.vector.tensor_reduce(z[:, :], e[:, u % 2, :, :], AX.X, ALU.add).then_inc(z_done, 1)
                    weighted(nc.vector, u, LOW, HEADS).then_inc(ev_done, 1)
                    dve.wait_ge(z_done, s + 1)
                    nc.vector.reciprocal(rz[:, :], z[:, :]).then_inc(rz_done, 1)
                    dve.wait_ge(ev_done, s + 1)
                    dve.wait_ge(ev_low, s + 1)
                    nc.vector.tensor_reduce(sums[:, :, :], ev[:, :, :, :], AX.X, ALU.add).then_inc(sums_done, 1)
                    dve.wait_ge(rz_done, s + 1)
                    dve.wait_ge(sums_done, s + 1)
                    wait(dve, r_ready, s - 1)
                    nc.vector.tensor_tensor(o[:, u % 2, :, :], sums[:, :, :], rz[:, :].unsqueeze(2).broadcast_to([P, HEADS, HD]),
                                            ALU.mult).then_inc(o_ready, 1)
                if at := sl.step(SCORE):
                    s, u = at
                    dve.wait_ge(s_ps, s + 1)
                    score = ps_s[u % 2][:, 0:HEADS * HEADS].rearrange("p (i j) -> p i j", i=HEADS)
                    nc.vector.tensor_reduce(top[:, :], score, AX.X, ALU.max).then_inc(top_done, 1)
                    dve.wait_ge(top_done, s + 1)
                    wait(dve, exp_done, s - 1)
                    nc.vector.tensor_tensor(dif[:, u % 2, :, :], score, top[:, :].unsqueeze(2).broadcast_to([P, HEADS, HEADS]),
                                            ALU.subtract).then_inc(dif_ready, 1)
                if at := sl.step(LAST):
                    s, u = at
                    dve.wait_ge(y_ps, s + 1)
                    dve.wait_ge(biased, s + 1)
                    nc.vector.tensor_tensor(c.x[:, s, :], c.x[:, s, :], ps_y[:, 0:D], ALU.add).then_inc(x_done, 1)
                    dve.wait_ge(x_done, s + 1)
                    nc.vector.bn_stats(c.stats[:, s, :], c.x[:, s, :])

            run_slots(dve, slot, B, LAG)


def cross_attention_tempered(c):
    B = c.B
    c.stage = "x1"
    ctx, sb, ps, sem = stage_scope(c)
    with ctx:
        c.t_max, c.t_z, c.t_sq = (sb(n, [P, B, HEADS]) for n in ("t_max", "t_z", "t_sq"))
        c.t_q, c.t_k = sb("t_q", [P, B]), sb("t_k", [P, B])
        c.t_g, c.t_qb = sb("t_g", [P, B]), sb("t_qb", [P, B])
        c.t_bias = sb("t_bias", [P, D])
        c.stage = "x1s"
        tempered_pass(c, False)
        c.stage = "x1t"
        temperatures(c)
        c.stage = "x1a"
        tempered_pass(c, True)


def temperatures(c):
    nc, B = c.nc, c.B
    N = B * HEADS
    COLS = min(N, 512)
    parts = N // COLS
    H = c.w["x1_w2"].shape[0]
    ctx, sb, ps, sem = stage_scope(c)
    with ctx:
        z2, rec, ent, prod = sb("z2", [P, N]), sb("rec", [P, N]), sb("ent", [P, N]), sb("prod", [P, B])
        sims = sb("sims", [P, B, HEADS])
        feats = sb("feats", [3, N])
        h1, h2 = sb("h1", [H, N]), sb("h2", [H, N])
        own_t = sb("own_t", [P, B, HEADS])
        lt, t = sb("lt", [P, B]), sb("t", [P, B])
        bank = [ps(f"bank{n}") for n in range(parts)]
        last = [ps(f"last{n}") for n in range(parts)]
        bias_bank = ps("bias_bank")
        dv, in_ready, f_ps, f_ready, h_ps, h_ready, t_ps, lt_ready, t_ready, b_ps = (
            sem(n) for n in ("dv", "in_ready", "f_ps", "f_ready", "h_ps", "h_ready", "t_ps", "lt_ready", "t_ready", "b_ps"))
        block = ctx.enter_context(nc.Block())
        flat = lambda tile: tile[:, :, :].rearrange("p b h -> p (b h)")
        head_mask = c.w["x1_heads"][:, :].unsqueeze(1).broadcast_to([P, B, HEADS])
        cols = lambda n: slice(n * COLS, n * COLS + COLS)

        @block.vector
        def _(dve):
            n_own = [0]

            def own(ins):
                n_own[0] += 1
                ins.then_inc(dv, 1)
                dve.wait_ge(dv, n_own[0])

            dve.wait_ge(b_ps, 1)
            own(nc.vector.tensor_tensor(c.t_bias[:, :], bias_bank[:, 0:D], c.w["x1_bo"][:, :], ALU.add))
            own(nc.vector.tensor_tensor(prod[:, :], c.t_q[:, :], c.t_k[:, :], ALU.mult))
            own(nc.vector.tensor_tensor(sims[:, :, :], prod[:, :].unsqueeze(2).broadcast_to([P, B, HEADS]), head_mask, ALU.mult))
            own(nc.vector.tensor_tensor(z2[:, :], flat(c.t_z), flat(c.t_z), ALU.mult))
            own(nc.vector.reciprocal(rec[:, :], z2[:, :]))
            nc.vector.tensor_tensor(ent[:, :], rec[:, :], flat(c.t_sq), ALU.mult).then_inc(in_ready, 1)
            for n in range(parts):
                dve.wait_ge(t_ps, n + 1)
                b = COLS // HEADS
                own(nc.vector.tensor_tensor(own_t[:, n * b:n * b + b, :], last[n][:, 0:COLS].rearrange("p (b h) -> p b h", h=HEADS),
                                            c.w["x1_heads"][:, :].unsqueeze(1).broadcast_to([P, b, HEADS]), ALU.mult))
            own(nc.vector.tensor_reduce(lt[:, :], own_t[:, :, :], AX.X, ALU.add))
            own(nc.vector.tensor_scalar(t[:, :], lt[:, :], c.w["x1_b3"][:, 0:1], float(np.log(0.1)), ALU.add, ALU.max))
            nc.vector.tensor_scalar(lt[:, :], t[:, :], float(np.log(10.0)), None, ALU.min).then_inc(lt_ready, 1)
            dve.wait_ge(t_ready, 1)
            own(nc.vector.tensor_scalar(lt[:, :], t[:, :], 2.0, None, ALU.mult))
            own(nc.vector.reciprocal(c.t_g[:, :], lt[:, :]))
            own(nc.vector.tensor_scalar(c.t_qb[:, :], c.t_g[:, :], c.w["x1_bias"][:, 0:1], None, ALU.mult))

        @block.tensor
        def _(pe):
            nc.tensor.matmul(bias_bank[:, 0:D], c.w["x1_bv"][:, :], c.w["x1_o"][:, :], start=True, stop=True).then_inc(b_ps, 1)
            pe.wait_ge(in_ready, 1)
            for n in range(parts):
                for k, data in enumerate((flat(sims), flat(c.t_max), ent[:, :])):
                    nc.tensor.matmul(bank[n][0:3, 0:COLS], c.w["x1_pick"][:, 3 * k:3 * k + 3], data[:, cols(n)],
                                     start=k == 0, stop=False)
                nc.tensor.matmul(bank[n][0:3, 0:COLS], c.w["x1_less"][0:1, :], c.ones_row[0:1, 0:COLS],
                                 start=False, stop=True).then_inc(f_ps, 1)
            for layer, (wt, src, dst, ready) in enumerate((("x1_w1", feats, bank, f_ready), ("x1_w2", h1, bank, h_ready))):
                for n in range(parts):
                    pe.wait_ge(ready, parts if ready is f_ready else n + 1)
                    nc.tensor.matmul(dst[n][0:H, 0:COLS], c.w[wt][:, :], src[:, cols(n)], start=True, stop=True).then_inc(h_ps, 1)
            for n in range(parts):
                pe.wait_ge(h_ready, parts + n + 1)
                nc.tensor.matmul(last[n][:, 0:COLS], c.w["x1_w3"][:, :], h2[:, cols(n)], start=True, stop=True).then_inc(t_ps, 1)

        @block.scalar
        def _(act):
            for n in range(parts):
                act.wait_ge(f_ps, n + 1)
                nc.scalar.activation(feats[:, cols(n)], bank[n][0:3, 0:COLS], ACT.Copy).then_inc(f_ready, 1)
            for layer, (dst, col) in enumerate(((h1, 0), (h2, 1))):
                for n in range(parts):
                    act.wait_ge(h_ps, layer * parts + n + 1)
                    nc.scalar.activation(dst[:, cols(n)], bank[n][0:H, 0:COLS], ACT.Gelu,
                                         bias=c.w["x1_mlp_b"][:, col:col + 1]).then_inc(h_ready, 1)
            act.wait_ge(lt_ready, 1)
            nc.scalar.activation(t[:, :], lt[:, :], ACT.Exp).then_inc(t_ready, 1)


def tempered_pass(c, final):
    nc, B = c.nc, c.B
    K = c.keys
    ctx, sb, ps, sem = stage_scope(c)
    with ctx:
        cx = sb("cx", [P, UNROLL, K])
        xn = sb("xn", [P, 2, D])
        xT = sb("xT", [P, 2, P])
        qT, kT = sb("qT", [P, 2, P]), sb("kT", [P, 2, K])
        k_bd = sb("k_bd", [P, 2, GROUP, K])
        nmax = sb("nmax", [P, HEADS])
        SCALE = HD ** -0.5
        DIF = 4 if final else 2
        d = sb("d", [P, 2, 4 * DIF, K])
        shift = sb("shift", [P, 2, 8])
        e = sb("e", [P, 2, HEADS, K])
        sq = sb("sq", [P, 2, HEADS, K])
        if final:
            v_bd = sb("v_bd", [K, UNROLL, GROUPS, GROUP, STRIP])
            z, rz = sb("z", [P, HEADS]), sb("rz", [P, HEADS])
            pT = sb("pT", [K, 2, HEADS, P])
            oT = sb("oT", [P, 2, P])
        ps_x, ps_qk = ps("ps_x"), ps("ps_qk")
        BANKS = 2 if final else 4
        ps_n = [ps(f"ps_n{i}") for i in range(BANKS)]
        if final:
            ps_t = [ps(f"ps_t{i}") for i in range(2)]
            ps_o, ps_y = ps("ps_o"), ps("ps_y")
        names = ("xn_ready", "xT_ps", "xT_ready", "qk_ps", "qk_ready", "k_bd_ready", "made", "s_ps", "max_done", "d_ready",
                 "exp_done", "z_done", "rz_done", "sq_ready", "sq_done", "pT_ps", "pT_ready", "o_ps", "oT_ready", "y_ps",
                 "x_done", "cx_ready", "sums_done", "biased", "direct_done", "shift_ready")
        (xn_ready, xT_ps, xT_ready, qk_ps, qk_ready, k_bd_ready, made, s_ps, max_done, d_ready,
         exp_done, z_done, rz_done, sq_ready, sq_done, pT_ps, pT_ready, o_ps, oT_ready, y_ps,
         x_done, cx_ready, sums_done, biased, direct_done, shift_ready) = (sem(n) for n in names)
        block = ctx.enter_context(nc.Block())
        EVAC = 3 if final else 2

        def strip(g):
            return slice(STRIP * g, STRIP * g + STRIP)

        def four(t, g):
            return t[:, 4 * g:4 * g + 4]

        def bank_heads(bank, rows=P, cols=K):
            return bank[0:rows, 0:4 * cols].rearrange("p (h k) -> p h k", h=4)

        TURN, PROJECT, SCORE, WEIGH, SPREAD, VALUE, LAST = 1, 2, 3, 4, 5, 6, 7
        LAG = LAST if final else SPREAD

        @block.tensor
        def _(pe):
            def scores(at, g):
                s, u = at
                if g == 0:
                    pe.wait_ge(k_bd_ready, s + 1)
                if final:
                    wait(pe, d_ready, 4 * s + g - 1)
                elif g < DIF:
                    wait(pe, d_ready, DIF * (s - 1) + g + 1)
                else:
                    wait(pe, direct_done, 2 * (s - 1) + g - DIF + 1)
                nc.tensor.matmul(ps_n[g % BANKS][:, 0:4 * K], qT[strip(g), u % 2, :], k_bd[strip(g), u % 2, :, :],
                                 start=True, stop=True).then_inc(s_ps, 1)

            def transposes(at, g):
                s, u = at
                if g == 0:
                    pe.wait_ge(sq_ready, s + 1)
                wait(pe, pT_ready, 4 * s + g - 1)
                for n in range(4):
                    ins = nc.tensor.transpose(ps_t[g % 2][0:K, n * P:n * P + P], sq[:, u % 2, 4 * g + n, :], c.ident[:, :])
                ins.then_inc(pT_ps, 1)

            def slot(sl):
                scored, spread = sl.step(SCORE), sl.step(SPREAD) if final else None
                if scored:
                    scores(scored, 0)
                    scores(scored, 1)
                if at := sl.step(PROJECT):
                    s, u = at
                    pe.wait_ge(cx_ready, s + 1)
                    pe.wait_ge(xT_ready, s + 1)
                    wait(pe, qk_ready, EVAC * s)
                    nc.tensor.matmul(ps_qk[:, 0:P], c.w["x1_q"][:, :], xT[:, u % 2, :], start=True, stop=True)
                    ins = nc.tensor.matmul(ps_qk[:, P:P + K], c.w["x1_k"][:, :], cx[:, u, :], start=True, stop=True)
                    if final:
                        ins = nc.tensor.matmul(ps_qk[0:K, 3 * P:4 * P], cx[:, u, :], c.w["x1_v"][:, :], start=True, stop=True)
                    ins.then_inc(qk_ps, 1)
                if final and (at := sl.step(VALUE)):
                    s, u = at
                    pe.wait_ge(pT_ready, 4 * (s + 1))
                    pe.wait_ge(qk_ready, EVAC * (s + 1))
                    wait(pe, oT_ready, s)
                    for j in range(GROUP):
                        for g in range(GROUPS):
                            ins = nc.tensor.matmul(ps_o[strip(g), 0:P], v_bd[:, u, g, j, :], pT[:, u % 2, GROUP * g + j, :],
                                                   start=j == 0, stop=j == GROUP - 1)
                    ins.then_inc(o_ps, 1)
                if at := sl.step(TURN):
                    s, u = at
                    pe.wait_ge(xn_ready, s + 1)
                    wait(pe, xT_ready, s)
                    nc.tensor.transpose(ps_x[:, 0:P], xn[:, u % 2, :], c.ident[:, :]).then_inc(xT_ps, 1)
                if scored:
                    scores(scored, 2)
                if spread:
                    transposes(spread, 0)
                    transposes(spread, 1)
                if scored:
                    scores(scored, 3)
                if spread:
                    transposes(spread, 2)
                    transposes(spread, 3)
                if final and (at := sl.step(LAST)):
                    s, u = at
                    pe.wait_ge(oT_ready, s + 1)
                    wait(pe, x_done, s)
                    nc.tensor.matmul(ps_y[:, 0:D], oT[:, u % 2, :], c.w["x1_o"][:, :], start=True, stop=True).then_inc(y_ps, 1)

            run_slots(pe, slot, B, LAG)

        @block.scalar
        def _(act):
            if final:
                act.wait_ge(made, 1)

            def slot(sl):
                if at := sl.step(PROJECT):
                    s, u = at
                    act.wait_ge(qk_ps, s + 1)
                    wait(act, k_bd_ready, s - 1)
                    wait(act, s_ps, 4 * (s - 1))
                    if not final:
                        wait(act, sums_done, s - 1)
                    q_bias, q_scale = c.w["x1_bias"][:, 0:1], 1.0
                    if final:
                        q_bias, q_scale = c.t_qb[:, bass.ds(s, 1)], c.t_g[:, bass.ds(s, 1)]
                    nc.scalar.activation(qT[:, u % 2, :], ps_qk[:, 0:P], ACT.Identity, scale=q_scale, bias=q_bias).then_inc(qk_ready, 1)
                    nc.scalar.activation(kT[:, u % 2, :], ps_qk[:, P:P + K], ACT.Identity,
                                         bias=c.w["x1_bias"][:, 1:2]).then_inc(qk_ready, 1)
                    if final:
                        wait(act, o_ps, s - 3)
                        for j in range(GROUP):
                            at_j = slice(HD * j, HD * j + HD)
                            ins = nc.scalar.activation(v_bd[:, u, :, j, at_j],
                                                       ps_qk[0:K, 3 * P:4 * P].rearrange("p (g r) -> p g r", g=GROUPS)[:, :, at_j], ACT.Copy)
                        ins.then_inc(qk_ready, 1)
                if final and (at := sl.step(VALUE)):
                    s, u = at
                    act.wait_ge(o_ps, s + 1)
                    wait(act, y_ps, s - 1)
                    nc.scalar.activation(oT[:, u % 2, :], ps_o[:, 0:P], ACT.Copy).then_inc(oT_ready, 1)
                if at := sl.step(TURN):
                    s, u = at
                    act.wait_ge(xT_ps, s + 1)
                    wait(act, qk_ps, s - 1)
                    nc.scalar.activation(xT[:, u % 2, :], ps_x[:, 0:P], ACT.Copy).then_inc(xT_ready, 1)
                spread = sl.step(SPREAD) if final else None

                def transposed(groups):
                    s, u = spread
                    for g in groups:
                        act.wait_ge(pT_ps, 4 * s + g + 1)
                        nc.scalar.activation(four(pT[:, u % 2], g), bank_heads(ps_t[g % 2], K, P), ACT.Copy).then_inc(pT_ready, 1)

                if spread:
                    transposed(range(4))
                if at := sl.step(SCORE):
                    s, u = at
                    act.wait_ge(d_ready, DIF * (s + 1))
                    wait(act, sq_ready, s - 1)
                    ins = nc.scalar.activation(e[:, u % 2, 0:4 * DIF, :], d[:, u % 2, :, :], ACT.Exp, scale=1.0 if final else SCALE)
                    for g in range(DIF, 4):
                        act.wait_ge(shift_ready, 2 * s + g - 1)
                        for h in range(4 * g, 4 * g + 4):
                            ins = nc.scalar.activation(e[:, u % 2, h, :], ps_n[g % BANKS][:, (h % 4) * K:(h % 4) * K + K], ACT.Exp, scale=SCALE,
                                                       bias=shift[:, u % 2, h - 8:h - 7], accum_out=c.t_z[:, s, h:h + 1])
                        ins.then_inc(direct_done, 1)
                    if final:
                        ins.then_inc(exp_done, 1)

            run_slots(act, slot, B, LAG)

        @block.gpsimd
        def _(pool):
            if final:
                nc.gpsimd.memset(v_bd[:, :, :, :, :], 0.0).then_inc(made, 1)

            def slot(sl):
                if at := sl.step(PROJECT):
                    s, u = at
                    pool.wait_ge(qk_ready, EVAC * (s + 1))
                    wait(pool, s_ps, 4 * (s - 1))
                    nc.gpsimd.tensor_tensor(k_bd[:, u % 2, :, :], kT[:, u % 2, :].unsqueeze(1).broadcast_to([P, GROUP, K]),
                                            c.block[:, 0:GROUP].unsqueeze(2).broadcast_to([P, GROUP, K]),
                                            ALU.mult).then_inc(k_bd_ready, 1)
                if at := sl.step(0):
                    s, u = at
                    wait(pool, qk_ps, s - 3)
                    nc.gpsimd.tensor_copy(cx[:, u, :], c.ctx[:, s, :]).then_inc(cx_ready, 1)
                if final and (at := sl.step(TURN)):
                    s, u = at
                    pool.wait_ge(xn_ready, s + 1)
                    nc.gpsimd.tensor_tensor(c.x[:, s, :], c.x[:, s, :], c.t_bias[:, :], ALU.add).then_inc(biased, 1)
                if at := sl.step(WEIGH):
                    s, u = at
                    pool.wait_ge(rz_done if final else direct_done, s + 1 if final else 2 * (s + 1))
                    wait(pool, pT_ps if final else sq_done, 4 * (s - 1) if final else s - 1)
                    other = rz[:, :].unsqueeze(2).broadcast_to([P, HEADS, K]) if final else e[:, u % 2, :, :]
                    nc.gpsimd.tensor_tensor(sq[:, u % 2, :, :], e[:, u % 2, :, :], other, ALU.mult).then_inc(sq_ready, 1)

            run_slots(pool, slot, B, LAG)

        @block.vector
        def _(dve):
            def slot(sl):
                if at := sl.step(0):
                    s, u = at
                    wait(dve, xT_ps, s - 1)
                    nc.vector.tensor_scalar(xn[:, u % 2, :], c.x[:, s, :], c.mean[:, bass.ds(s, 1)], c.rstd[:, bass.ds(s, 1)],
                                            ALU.subtract, ALU.mult).then_inc(xn_ready, 1)
                scored = sl.step(SCORE)

                def differences(groups):
                    s, u = scored
                    top = nmax[:, :] if final else c.t_max[:, s, :]
                    for g in groups:
                        dve.wait_ge(s_ps, 4 * s + g + 1)
                        nc.vector.tensor_reduce(four(top, g), bank_heads(ps_n[g % BANKS]), AX.X, ALU.max).then_inc(max_done, 1)
                        dve.wait_ge(max_done, 4 * s + g + 1)
                        if g >= DIF:
                            wait(dve, direct_done, 2 * (s - 1))
                            nc.vector.tensor_scalar(shift[:, u % 2, 4 * g - 8:4 * g - 4], four(top, g), -SCALE, None,
                                                    ALU.mult).then_inc(shift_ready, 1)
                            continue
                        nc.vector.tensor_tensor(four(d[:, u % 2], g), bank_heads(ps_n[g % BANKS]),
                                                four(top, g).unsqueeze(2).broadcast_to([P, 4, K]),
                                                ALU.subtract).then_inc(d_ready, 1)

                if scored:
                    wait(dve, exp_done if final else direct_done, (scored[0] - 1) * (1 if final else 2))
                    differences((0, 1))
                if at := sl.step(WEIGH):
                    s, u = at
                    dve.wait_ge(exp_done if final else direct_done, s + 1 if final else 2 * (s + 1))
                    if final:
                        wait(dve, sq_ready, s)
                    nc.vector.tensor_reduce(z[:, :] if final else c.t_z[:, s, 0:4 * DIF], e[:, u % 2, 0:4 * DIF, :], AX.X, ALU.add).then_inc(z_done, 1)
                    if final:
                        dve.wait_ge(z_done, s + 1)
                        nc.vector.reciprocal(rz[:, :], z[:, :]).then_inc(rz_done, 1)
                if scored:
                    differences((2, 3))
                if final and (at := sl.step(LAST)):
                    s, u = at
                    dve.wait_ge(y_ps, s + 1)
                    dve.wait_ge(biased, s + 1)
                    nc.vector.tensor_tensor(c.x[:, s, :], c.x[:, s, :], ps_y[:, 0:D], ALU.add).then_inc(x_done, 1)
                    dve.wait_ge(x_done, s + 1)
                    nc.vector.bn_stats(c.stats[:, s, :], c.x[:, s, :])
                if not final and (at := sl.step(SPREAD)):
                    s, u = at
                    dve.wait_ge(sq_ready, s + 1)
                    nc.vector.tensor_reduce(c.t_sq[:, s, :], sq[:, u % 2, :, :], AX.X, ALU.add).then_inc(sq_done, 1)
                if not final and (at := sl.step(SCORE)):
                    s, u = at
                    dve.wait_ge(qk_ready, 2 * (s + 1))
                    nc.vector.tensor_reduce(c.t_q[:, bass.ds(s, 1)], qT[:, u % 2, :], AX.X, ALU.add)
                    nc.vector.tensor_reduce(c.t_k[:, bass.ds(s, 1)], kT[:, u % 2, :], AX.X, ALU.add).then_inc(sums_done, 1)

            run_slots(dve, slot, B, LAG)


T6 = 4


def mixed_experts(c):
    nc, B = c.nc, c.B
    c.stage = "f1"
    ctx, sb, ps, sem = stage_scope(c)
    with ctx:
        c.f1_hi, c.f1_lo = sb("hi", [D, B, P], F32R), sb("lo", [D, B, P], F32R)
        c.f1_wt = sb("wt", [P, B, 4])
        c.f1 = {name[3:]: tile for name, tile in c.w.items() if name.startswith("f1_")}
        c.f1_me, c.f1_me_b = sb("me", [D, 2, D]), sb("me_b", [P, 2])
        c.f1_rows = {name: sb("row_" + name, [P, D]) for name in ("ce", "f2b", "genb", "c2b", "ml_b2")}
        c.f1_parts = {name: [sb(f"{name}_{part}", [D, n, P], F32R) for part in ("hi", "lo")]
                      for name, n in (("sw_1", 4), ("sw_3", 4), ("me", 2), ("ml_1", 4))}
        c.f1_ce, c.f1_ce_b = sb("ce", [D, D]), sb("ce_b", [1, D])
        c.stage = "f1w"
        chain_weights(c)
        c.stage = "f1r"
        route(c)
        f = c.f1
        c.stage = "f1a"
        hidden_expert(c, 0, ACT.Silu, "sw_1", "sw_3", None, f["sw_2"], None)
        c.stage = "f1b"
        hidden_expert(c, 1, ACT.Gelu, "me", None, c.f1_me_b, f["c2"], c.f1_rows["c2b"])
        c.stage = "f1d"
        hidden_expert(c, 3, ACT.Gelu, "ml_1", None, f["ml_b1"], f["ml_2"], c.f1_rows["ml_b2"])
        c.stage = "f1c"
        normed_expert(c, 2)


def chain_weights(c):
    nc, f = c.nc, c.f1
    ctx, sb, ps, sem = stage_scope(c)
    with ctx:
        m1, m2, mo = sb("m1", [D, 2 * D]), sb("m2", [D, 2 * D]), sb("mo", [D, D])
        col1, col2 = sb("col1", [P, 1]), sb("col2", [P, 1])
        pm, pv, po, pb = ps("pm"), ps("pv"), ps("po"), ps("pb")
        pr = [ps(f"pr{n}") for n in range(2)]
        m_ps, m_done, v_ps, v_done, o_ps, o_done, b_ps, b_done, r_ps, r_done, hi_done, lo_done = (
            sem(n) for n in ("m_ps", "m_done", "v_ps", "v_done", "o_ps", "o_done", "b_ps", "b_done", "r_ps", "r_done",
                             "hi_done", "lo_done"))
        row_of = (("f2b", f["f2b"]), ("genb", f["genb"]), ("c2b", f["c2b"]), ("ml_b2", f["ml_b2"]), ("ce", c.f1_ce_b))
        split = (("sw_1", f["sw_1"]), ("sw_3", f["sw_3"]), ("ml_1", f["ml_1"]), ("me", c.f1_me))
        block = ctx.enter_context(nc.Block())
        c1 = f["c1"][:, :, :].rearrange("p n d -> p (n d)")
        me = c.f1_me[:, :, :].rearrange("p n d -> p (n d)")

        @block.tensor
        def _(pe):
            for n, (left, right) in enumerate((("me_oT", c1), ("me_vT", m1[:, :]), ("me_eqT", m2[:, :]))):
                wait(pe, m_done, n)
                nc.tensor.matmul(pm[:, 0:2 * D], f[left][:, :], right, start=True, stop=True).then_inc(m_ps, 1)
            for n, (left, right) in enumerate((("me_v", f["cols"][:, 0:1]), ("me_o", col1[:, :]))):
                wait(pe, v_done, n)
                nc.tensor.matmul(pv[:, n:n + 1], f[left][:, :], right, start=True, stop=True).then_inc(v_ps, 1)
            pe.wait_ge(v_done, 2)
            for n in range(2):
                nc.tensor.matmul(pv[:, 2 + n:3 + n], f["c1"][:, n, :], col2[:, :], start=True, stop=True).then_inc(v_ps, 1)
            nc.tensor.matmul(po[:, 0:D], f["ce_vT"][:, :], f["ce_o"][:, :], start=True, stop=True).then_inc(o_ps, 1)
            pe.wait_ge(o_done, 1)
            nc.tensor.matmul(po[:, 0:D], f["ce_synT"][:, :], mo[:, :], start=True, stop=True).then_inc(o_ps, 1)
            nc.tensor.matmul(pb[0:1, 0:D], f["cols"][:, 3:4], mo[:, :], start=True, stop=False)
            nc.tensor.matmul(pb[0:1, 0:D], f["cols"][:, 4:5], f["ce_o"][:, :], start=False, stop=False)
            nc.tensor.matmul(pb[0:1, 0:D], c.ones_row[0:1, 0:1], f["ce_bo"][0:1, :], start=False, stop=True).then_inc(b_ps, 1)
            pe.wait_ge(b_done, 1)
            for n, (name, row) in enumerate(row_of):
                nc.tensor.matmul(pr[n // 4][:, (n % 4) * D:(n % 4) * D + D], c.ones_row[0:1, 0:P], row[0:1, :],
                                 start=True, stop=True).then_inc(r_ps, 1)

        @block.scalar
        def _(act):
            for n, out in enumerate((m1[:, :], m2[:, :], me)):
                act.wait_ge(m_ps, n + 1)
                nc.scalar.activation(out, pm[:, 0:2 * D], ACT.Copy).then_inc(m_done, 1)
            act.wait_ge(m_done, 3)
            for name, w in split:
                nc.scalar.activation(c.f1_parts[name][0][:, :, :], w[:, :, :], ACT.Copy).then_inc(hi_done, 1)

        @block.vector
        def _(dve):
            for n, out in enumerate((col1, col2)):
                dve.wait_ge(v_ps, n + 1)
                nc.vector.tensor_tensor(out[:, :], pv[:, n:n + 1], f["cols"][:, 1 + n:2 + n], ALU.add).then_inc(v_done, 1)
            dve.wait_ge(v_ps, 4)
            nc.vector.tensor_tensor(c.f1_me_b[:, :], pv[:, 2:4], f["c1b"][:, :], ALU.add).then_inc(v_done, 1)
            dve.wait_ge(o_ps, 1)
            nc.vector.tensor_tensor(mo[:, :], po[:, 0:D], c.ident[:, :], ALU.add).then_inc(o_done, 1)
            dve.wait_ge(o_ps, 2)
            nc.vector.tensor_copy(c.f1_ce[:, :], po[:, 0:D]).then_inc(o_done, 1)
            dve.wait_ge(b_ps, 1)
            nc.vector.tensor_copy(c.f1_ce_b[:, :], pb[0:1, 0:D]).then_inc(b_done, 1)
            dve.wait_ge(r_ps, len(row_of))
            for n, (name, row) in enumerate(row_of):
                nc.vector.tensor_copy(c.f1_rows[name][:, :], pr[n // 4][:, (n % 4) * D:(n % 4) * D + D]).then_inc(r_done, 1)
            for n, (name, w) in enumerate(split):
                dve.wait_ge(hi_done, n + 1)
                hi, lo = c.f1_parts[name]
                nc.vector.tensor_tensor(lo[:, :, :], w[:, :, :], hi[:, :, :].bitcast(F32), ALU.subtract).then_inc(lo_done, 1)


def tiled(c, t):
    return t[:, :, :].rearrange("p (s i) d -> p s i d", i=T6)


def route(c):
    nc = c.nc
    B, T, E = c.B, T6, 4
    steps = B // T
    ctx, sb, ps, sem = stage_scope(c)
    with ctx:
        xn = sb("xn", [P, 2, T, D])
        xT = sb("xT", [D, 2, T, P])
        lg, sc, top, dif, e = (sb(n, [P, B, k]) for n, k in (("lg", E), ("sc", E), ("top", 1), ("dif", E), ("e", E)))
        rank, best, z, rz = (sb(n, [P, B, k]) for n, k in (("rank", E), ("best", E), ("z", 1), ("rz", 1)))
        gt, ge = sb("gt", [P, B, E, E]), sb("ge", [P, B, E, E])
        ps_x, ps_r = ps("ps_x"), ps("ps_r")
        xn_ready, xT_ps, xT_ready, hi_ready, lo_done, r_ps, dif_ready, exp_done, own = (
            sem(n) for n in ("xn_ready", "xT_ps", "xT_ready", "hi_ready", "lo_done", "r_ps", "dif_ready", "exp_done", "own"))
        lg_done = sem("lg_done")
        block = ctx.enter_context(nc.Block())
        LAG = 3
        x4, lg4, hi4, lo4 = (tiled(c, t) for t in (c.x, lg, c.f1_hi, c.f1_lo))
        mean4, rstd4 = (t[:, :].rearrange("p (s i) -> p s i", i=T) for t in (c.mean, c.rstd))

        @block.tensor
        def _(pe):
            def slot(sl):
                if at := sl.step(1):
                    s, u = at
                    pe.wait_ge(xn_ready, s + 1)
                    wait(pe, xT_ready, s)
                    for i in range(T):
                        ins = nc.tensor.transpose(ps_x[:, i * P:i * P + P], xn[:, u % 2, i, :], c.ident[:, :])
                    ins.then_inc(xT_ps, 1)
                if at := sl.step(2):
                    s, u = at
                    pe.wait_ge(xT_ready, s + 1)
                    wait(pe, lg_done, s)
                    for i in range(T):
                        ins = nc.tensor.matmul(ps_r[:, i * E:i * E + E], xT[:, u % 2, i, :], c.f1["router"][:, :], start=True, stop=True)
                    ins.then_inc(r_ps, 1)

            run_slots(pe, slot, steps, LAG)

        @block.scalar
        def _(act):
            def slot(sl):
                if at := sl.step(1):
                    s, u = at
                    act.wait_ge(xT_ps, s + 1)
                    wait(act, r_ps, s - 1)
                    wait(act, lo_done, s - 1)
                    wide = ps_x[:, :].rearrange("p (i t) -> p i t", i=T)
                    nc.scalar.activation(hi4[:, s, :, :], wide, ACT.Copy).then_inc(hi_ready, 1)
                    nc.scalar.activation(xT[:, u % 2, :, :], wide, ACT.Copy).then_inc(xT_ready, 1)

            run_slots(act, slot, steps, LAG)
            act.wait_ge(dif_ready, 1)
            nc.scalar.activation(e[:, :, :], dif[:, :, :], ACT.Exp).then_inc(exp_done, 1)

        @block.vector
        def _(dve):
            def slot(sl):
                if at := sl.step(0):
                    s, u = at
                    wait(dve, xT_ps, s - 1)
                    for i in range(T):
                        ins = nc.vector.tensor_scalar(xn[:, u % 2, i, :], x4[:, s, i, :], mean4[:, s, i:i + 1], rstd4[:, s, i:i + 1],
                                                      ALU.subtract, ALU.mult)
                    ins.then_inc(xn_ready, 1)
                if at := sl.step(2):
                    s, u = at
                    dve.wait_ge(r_ps, s + 1)
                    nc.vector.tensor_copy(lg4[:, s, :, :], ps_r[:, 0:T * E].rearrange("p (i e) -> p i e", i=T)).then_inc(lg_done, 1)
                if at := sl.step(2):
                    s, u = at
                    dve.wait_ge(xT_ready, s + 1)
                    dve.wait_ge(hi_ready, s + 1)
                    nc.vector.tensor_tensor(lo4[:, s, :, :], xT[:, u % 2, :, :], hi4[:, s, :, :].bitcast(F32), ALU.subtract).then_inc(lo_done, 1)

            run_slots(dve, slot, steps, LAG)
            count = [0]

            def after(ins):
                count[0] += 1
                ins.then_inc(own, 1)
                dve.wait_ge(own, count[0])

            def per_token(t):
                return t[:, :, :].broadcast_to([P, B, E])

            dve.wait_ge(lg_done, steps)
            bias = [c.f1["router_b"][:, n, :].unsqueeze(1).broadcast_to([P, B, E]) for n in range(2)]
            after(nc.vector.tensor_tensor(dif[:, :, :], lg[:, :, :], bias[0], ALU.add))
            after(nc.vector.tensor_tensor(sc[:, :, :], dif[:, :, :], bias[1], ALU.add))
            after(nc.vector.tensor_reduce(top[:, :, 0], sc[:, :, :], AX.X, ALU.max))
            nc.vector.tensor_tensor(dif[:, :, :], sc[:, :, :], per_token(top), ALU.subtract).then_inc(dif_ready, 1)
            dve.wait_ge(exp_done, 1)
            best_ins = top_two(c, dve, own, count[0], sc[:, :, :], e[:, :, :], gt[:, :, :, :], ge[:, :, :, :], rank[:, :, :],
                               c.w["tri4"][:, :, :, :], best[:, :, :])
            count[0] += 4
            after(best_ins)
            after(nc.vector.tensor_reduce(z[:, :, 0], best[:, :, :], AX.X, ALU.add))
            after(nc.vector.reciprocal(rz[:, :, :], z[:, :, :]))
            after(nc.vector.tensor_tensor(c.f1_wt[:, :, :], best[:, :, :], per_token(rz), ALU.mult))


def hidden_expert(c, expert, func, w1, w_gated, bias1, w2, bias2):
    nc = c.nc
    T, N = T6, T6 * P
    steps = c.B // T
    C = c.f1_parts[w1][0].shape[1]
    ctx, sb, ps, sem = stage_scope(c)
    with ctx:
        hid = sb("hid", [P, 2, C, N])
        sg = sb("sg", [P, 2, N]) if w_gated is not None else None
        yb = sb("yb", [P, T, D])
        ps_g = [ps(f"ps_g{i}") for i in range(2)]
        ps_u = [ps(f"ps_u{i}") for i in range(2)]
        ps_y = [ps(f"ps_y{i}") for i in range(2)]
        g_ps, u_ps, g_done, h_ready, y_ps, y_done, biased = (
            sem(n) for n in ("g_ps", "u_ps", "g_done", "h_ready", "y_ps", "y_done", "biased"))
        block = ctx.enter_context(nc.Block())
        LAG = 1
        g_freed = h_ready if w_gated is None else g_done
        x4, wt4 = tiled(c, c.x), tiled(c, c.f1_wt)
        hi4, lo4 = tiled(c, c.f1_hi), tiled(c, c.f1_lo)

        @block.tensor
        def _(pe):
            def product(out, name, n, s):
                w_hi, w_lo = c.f1_parts[name]
                nc.tensor.matmul(out, w_hi[:, n, :], hi4[:, s, :, :], start=True, stop=False)
                nc.tensor.matmul(out, w_hi[:, n, :], lo4[:, s, :, :], start=False, stop=False)
                return nc.tensor.matmul(out, w_lo[:, n, :], hi4[:, s, :, :], start=False, stop=True)

            def slot(sl):
                if at := sl.step(0):
                    s, u = at
                    for n in range(C):
                        wait(pe, g_freed, C * s + n - 1)
                        product(ps_g[n % 2][:, :], w1, n, s).then_inc(g_ps, 1)
                        if w_gated is not None:
                            wait(pe, h_ready, C * s + n - 1)
                            product(ps_u[n % 2][:, :], w_gated, n, s).then_inc(u_ps, 1)
                if at := sl.step(1):
                    s, u = at
                    pe.wait_ge(h_ready, C * (s + 1))
                    wait(pe, y_done, s - 1)
                    for i in range(T):
                        part = ps_y[u % 2][:, i * P:i * P + P]
                        for n in range(C):
                            ins = nc.tensor.matmul(part, hid[:, u % 2, n, i * P:i * P + P], w2[:, n, :],
                                                   start=n == 0, stop=n == C - 1)
                    ins.then_inc(y_ps, 1)

            run_slots(pe, slot, steps, LAG)

        @block.scalar
        def _(act):
            def slot(sl):
                if at := sl.step(0):
                    s, u = at
                    for n in range(C):
                        act.wait_ge(g_ps, C * s + n + 1)
                        if w_gated is not None:
                            wait(act, h_ready, C * s + n - 1)
                            nc.scalar.activation(sg[:, n % 2, :], ps_g[n % 2][:, :], func).then_inc(g_done, 1)
                        else:
                            wait(act, y_ps, s - 1)
                            nc.scalar.activation(hid[:, u % 2, n, :], ps_g[n % 2][:, :], func, bias=bias1[:, n:n + 1]).then_inc(h_ready, 1)

            run_slots(act, slot, steps, LAG)

        @block.vector
        def _(dve):
            def slot(sl):
                if w_gated is not None and (at := sl.step(0)):
                    s, u = at
                    for n in range(C):
                        dve.wait_ge(g_done, C * s + n + 1)
                        dve.wait_ge(u_ps, C * s + n + 1)
                        wait(dve, y_ps, s - 1)
                        nc.vector.tensor_tensor(hid[:, u % 2, n, :], sg[:, n % 2, :], ps_u[n % 2][:, :], ALU.mult).then_inc(h_ready, 1)
                if at := sl.step(1):
                    s, u = at
                    dve.wait_ge(y_ps, s + 1)
                    wait(dve, y_done, s)
                    y = ps_y[u % 2][:, :].rearrange("p (i d) -> p i d", i=T)
                    if bias2 is not None:
                        nc.vector.tensor_tensor(yb[:, :, :], y, bias2[:, :].unsqueeze(1).broadcast_to([P, T, D]), ALU.add).then_inc(biased, 1)
                        dve.wait_ge(biased, s + 1)
                        y = yb
                    for i in range(T):
                        ins = nc.vector.scalar_tensor_tensor(out=x4[:, s, i, :], in0=y[:, i, :],
                                                             scalar=wt4[:, s, i, expert:expert + 1], in1=x4[:, s, i, :],
                                                             op0=ALU.mult, op1=ALU.add)
                    ins.then_inc(y_done, 1)

            run_slots(dve, slot, steps, LAG)


def normed_expert(c, expert):
    nc, f = c.nc, c.f1
    T, N = T6, T6 * P
    steps = c.B // T
    ctx, sb, ps, sem = stage_scope(c)
    with ctx:
        xr = sb("xr", [D, 2, T, P])
        full = sb("full", [P, 2, T, D])
        yb = sb("yb", [P, T, D])
        st = sb("st", [P, 2, T, 6])
        both, dif, dif2, sq, mean, var, vpe, root, rstd = (
            sb(n, [P, 2, T]) for n in ("both", "dif", "dif2", "sq", "mean", "var", "vpe", "root", "rstd"))
        rows = [sb(f"rows{k}", [P, 2, T, D]) for k in range(2)]
        hT = [sb(f"hT{k}", [D, 2, N]) for k in range(2)]
        ff = sb("ff", [P, 2, 2, N])
        pre = [ps(f"pre{k}") for k in range(2)]
        ps_h = [ps(f"ps_h{k}") for k in range(2)]
        ps_g = [ps(f"ps_g{k}") for k in range(2)]
        ps_y = ps("ps_y")
        xr_ready, f_ps, f_ready, y_ps, y_done = (sem(n) for n in ("xr_ready", "f_ps", "f_ready", "y_ps", "y_done"))
        full_ready = [sem(f"full_ready{k}") for k in range(2)]
        biased, stored = sem("biased"), sem("stored")
        pre_ps, st_done, ag_done, var_ready, root_ready, rstd_done, rows_ready, h_ps, h_ready = (
            [sem(f"{n}{k}") for k in range(2)] for n in ("pre_ps", "st_done", "ag_done", "var_ready", "root_ready", "rstd_done",
                                                         "rows_ready", "h_ps", "h_ready"))
        block = ctx.enter_context(nc.Block())
        LAG = 4
        x4, wt4, hi4, lo4 = (tiled(c, t) for t in (c.x, c.f1_wt, c.f1_hi, c.f1_lo))

        @block.tensor
        def _(pe):
            def transposes(at, k):
                s, u = at
                pe.wait_ge(rows_ready[k], s + 1)
                wait(pe, h_ready[k], s)
                for i in range(T):
                    ins = nc.tensor.transpose(ps_h[k][:, i * P:i * P + P], rows[k][:, u % 2, i, :], c.ident[:, :])
                ins.then_inc(h_ps[k], 1)

            def slot(sl):
                if at := sl.step(2):
                    transposes(at, 0)
                if at := sl.step(4):
                    transposes(at, 1)
                if at := sl.step(1):
                    s, u = at
                    pe.wait_ge(xr_ready, s + 1)
                    wait(pe, full_ready[0], s)
                    for i in range(T):
                        part = pre[0][:, i * P:i * P + P]
                        ins = nc.tensor.matmul(part, xr[:, u % 2, i, :], c.f1_ce[:, :], start=True, stop=True)
                    ins.then_inc(pre_ps[0], 1)
                if at := sl.step(3):
                    s, u = at
                    pe.wait_ge(f_ready, 2 * (s + 1))
                    wait(pe, full_ready[1], s)
                    for i in range(T):
                        part = pre[1][:, i * P:i * P + P]
                        cols = slice(i * P, i * P + P)
                        nc.tensor.matmul(part, hT[0][:, u % 2, cols], c.ident[:, :], start=True, stop=False)
                        for n in range(2):
                            ins = nc.tensor.matmul(part, ff[:, u % 2, n, cols], f["f2"][:, n, :], start=False, stop=n == 1)
                    ins.then_inc(pre_ps[1], 1)
                if at := sl.step(2):
                    s, u = at
                    pe.wait_ge(h_ready[0], s + 1)
                    for n in range(2):
                        wait(pe, f_ready, 2 * s - 1 + n)
                        nc.tensor.matmul(ps_g[n][:, :], f["f1"][:, n, :], hT[0][:, u % 2, :], start=True, stop=True).then_inc(f_ps, 1)
                if at := sl.step(4):
                    s, u = at
                    pe.wait_ge(h_ready[1], s + 1)
                    wait(pe, y_done, s)
                    for i in range(T):
                        part = ps_y[:, i * P:i * P + P]
                        ins = nc.tensor.matmul(part, hT[1][:, u % 2, i * P:i * P + P], f["gen"][:, :], start=True, stop=True)
                    ins.then_inc(y_ps, 1)

            run_slots(pe, slot, steps, LAG)

        @block.scalar
        def _(act):
            def shifted(at, k):
                s, u = at
                act.wait_ge(h_ps[k], s + 1)
                if k == 0:
                    wait(act, pre_ps[1], s - 1)
                else:
                    wait(act, y_ps, s - 1)
                nc.scalar.activation(hT[k][:, u % 2, :], ps_h[k][:, :], ACT.Identity, scale=f["norms"][:, 2 * k:2 * k + 1],
                                     bias=f["norms"][:, 2 * k + 1:2 * k + 2]).then_inc(h_ready[k], 1)

            def roots(at, k):
                s, u = at
                act.wait_ge(var_ready[k], s + 1)
                nc.scalar.activation(root[:, k, :], vpe[:, k, :], ACT.Sqrt).then_inc(root_ready[k], 1)

            def slot(sl):
                if at := sl.step(2):
                    shifted(at, 0)
                if at := sl.step(4):
                    shifted(at, 1)
                if at := sl.step(1):
                    roots(at, 0)
                if at := sl.step(3):
                    roots(at, 1)
                if at := sl.step(2):
                    s, u = at
                    for n in range(2):
                        act.wait_ge(f_ps, 2 * s + n + 1)
                        nc.scalar.activation(ff[:, u % 2, n, :], ps_g[n][:, :], ACT.Relu, bias=f["f1b"][:, n:n + 1]).then_inc(f_ready, 1)

            run_slots(act, slot, steps, LAG)

        @block.sync
        def _(sp):
            out = c.out.rearrange("(s i) p d -> p s i d", i=T)
            with sp.Fori(0, steps) as s:
                sp.wait_ge(y_done, s + 1)
                sp.dma_start(out[:, s, :, :], x4[:, s, :, :]).then_inc(stored, 16)
            sp.wait_ge(stored, 16 * steps)

        @block.gpsimd
        def _(pool):
            def slot(sl):
                if at := sl.step(0):
                    s, u = at
                    wait(pool, pre_ps[0], s - 1)
                    nc.gpsimd.tensor_tensor(xr[:, u % 2, :, :], hi4[:, s, :, :].bitcast(F32), lo4[:, s, :, :].bitcast(F32), ALU.add).then_inc(xr_ready, 1)

            run_slots(pool, slot, steps, LAG)

        @block.vector
        def _(dve):
            def statistics(at, k):
                s, u = at
                dve.wait_ge(pre_ps[k], s + 1)
                wait(dve, rows_ready[k], s)
                bias = c.f1_rows[("ce", "f2b")[k]][:, :].unsqueeze(1).broadcast_to([P, T, D])
                nc.vector.tensor_tensor(full[:, k, :, :], pre[k][:, :].rearrange("p (i d) -> p i d", i=T), bias, ALU.add).then_inc(full_ready[k], 1)
                dve.wait_ge(full_ready[k], s + 1)
                for i in range(T):
                    ins = nc.vector.bn_stats(st[:, k, i, :], full[:, k, i, :])
                ins.then_inc(st_done[k], 1)
                me, mo, ve, vo = (st[:, k, :, n] for n in (1, 4, 2, 5))
                dve.wait_ge(st_done[k], s + 1)
                nc.vector.tensor_tensor(both[:, k, :], me, mo, ALU.add)
                nc.vector.tensor_tensor(dif[:, k, :], me, mo, ALU.subtract)
                nc.vector.tensor_tensor(sq[:, k, :], ve, vo, ALU.add).then_inc(ag_done[k], 1)
                dve.wait_ge(ag_done[k], 3 * s + 1)
                nc.vector.tensor_scalar(mean[:, k, :], both[:, k, :], 0.5, None, ALU.mult)
                nc.vector.tensor_tensor(dif2[:, k, :], dif[:, k, :], dif[:, k, :], ALU.mult).then_inc(ag_done[k], 1)
                dve.wait_ge(ag_done[k], 3 * s + 2)
                nc.vector.scalar_tensor_tensor(out=var[:, k, :], in0=dif2[:, k, :], scalar=D / 4, in1=sq[:, k, :],
                                               op0=ALU.mult, op1=ALU.add).then_inc(ag_done[k], 1)
                dve.wait_ge(ag_done[k], 3 * s + 3)
                nc.vector.tensor_scalar(vpe[:, k, :], var[:, k, :], 1.0 / D, EPS, ALU.mult, ALU.add).then_inc(var_ready[k], 1)

            def normalised(at, k):
                s, u = at
                dve.wait_ge(root_ready[k], s + 1)
                nc.vector.reciprocal(rstd[:, k, :], root[:, k, :]).then_inc(rstd_done[k], 1)
                dve.wait_ge(rstd_done[k], s + 1)
                wait(dve, h_ps[k], s - 1)
                for i in range(T):
                    ins = nc.vector.tensor_scalar(rows[k][:, u % 2, i, :], full[:, k, i, :], mean[:, k, i:i + 1],
                                                  rstd[:, k, i:i + 1], ALU.subtract, ALU.mult)
                ins.then_inc(rows_ready[k], 1)

            def slot(sl):
                first, second = sl.step(1), sl.step(3)
                if first:
                    statistics(first, 0)
                if second:
                    statistics(second, 1)
                if first:
                    normalised(first, 0)
                if second:
                    normalised(second, 1)
                if at := sl.step(4):
                    s, u = at
                    dve.wait_ge(y_ps, s + 1)
                    wait(dve, y_done, s)
                    nc.vector.tensor_tensor(yb[:, :, :], ps_y[:, :].rearrange("p (i d) -> p i d", i=T),
                                            c.f1_rows["genb"][:, :].unsqueeze(1).broadcast_to([P, T, D]), ALU.add).then_inc(biased, 1)
                    dve.wait_ge(biased, s + 1)
                    for i in range(T):
                        ins = nc.vector.scalar_tensor_tensor(out=x4[:, s, i, :], in0=yb[:, i, :],
                                                             scalar=wt4[:, s, i, expert:expert + 1], in1=x4[:, s, i, :],
                                                             op0=ALU.mult, op1=ALU.add)
                    ins.then_inc(y_done, 1)

            run_slots(dve, slot, steps, LAG)


def latent_weights(c):
    nc = c.nc
    ctx, sb, ps, sem = stage_scope(c)
    with ctx:
        pq = [ps(f"p{n}") for n in range(3)]
        ready, cleared = sem("ready"), sem("cleared")
        block = ctx.enter_context(nc.Block())
        parts = ((c.w["a0_dq"], c.w["a0_uq"], c.a0_q), (c.w["a0_dkv"], c.w["a0_uk"], c.a0_k), (c.w["a0_dkv"], c.w["a0_uv"], c.a0_v))

        @block.tensor
        def _(pe):
            for n, (down, up, out) in enumerate(parts):
                nc.tensor.matmul(pq[n][:, 0:D], down[:, :], up[:, :], start=True, stop=True).then_inc(ready, 1)

        @block.gpsimd
        def _(pool):
            for out in (c.a0_q, c.a0_k):
                nc.gpsimd.memset(out[:, :, :], 0.0).then_inc(cleared, 1)

        @block.scalar
        def _(act):
            act.wait_ge(cleared, 2)
            for n, (down, up, out) in enumerate(parts):
                act.wait_ge(ready, n + 1)
                if n == 2:
                    nc.scalar.activation(out[:, :], pq[n][:, 0:D], ACT.Copy)
                    continue
                for r in range(3):
                    nc.scalar.activation(out[:, :, :].rearrange("p j (t r) -> p j t r", r=STRIP)[:, :, :, r * HD:r * HD + HD],
                                         pq[n][:, 0:D].rearrange("p (t j d) -> p j t d", t=GROUPS, d=HD), ACT.Copy)


def decoder(nc, inp, out, batches):
    c = Core(nc, inp, out, batches)
    B = batches
    whole, most, first, start = ExitStack(), ExitStack(), ExitStack(), ExitStack()
    with whole, most, first, start:
        def sb(name, shape, dt=F32, life=whole):
            return life.enter_context(nc.sbuf_tensor(name, shape, dt))

        c.x = sb("x", [P, B, D])
        c.stats = sb("stats", [P, B, 6])
        c.mean, c.rstd = sb("mean", [P, B]), sb("rstd", [P, B])
        c.w = {}
        tiles = {}

        def life_of(name):
            if name in ("x0_q", "x0_k", "x0_out"):
                return start
            if name.startswith(("a0_", "x0_")):
                return first
            return most if name.startswith(("ctx", "a1_", "x1_")) else whole

        for life in (whole, most, first, start):
            if life is start:
                c.a0_q, c.a0_k = (sb(n, [P, GROUPS, P], life=first) for n in ("a0_wq", "a0_wk"))
                c.a0_v = sb("a0_wv", [P, D], life=first)
                c.x0_a, c.x0_o = sb("x0_a", [P, HEADS, D], life=first), sb("x0_o", [P, HEADS // 2, D], life=first)
                c.x0_b = sb("x0_b", [P, D], life=first)
            for name in inp:
                if name == "x" or name.startswith("late_") or life_of(name) is not life:
                    continue
                shape = list(inp[name].shape)
                c.w[name] = sb("w_" + name, shape, inp[name].dtype, life)
                tiles[name] = c.w[name][(slice(None),) * len(shape)]
        keep = [(name, tiles[name]) for name in inp if name in tiles]
        c.ident, c.ident16, c.ones_row = c.w["ident"], c.w["ident16"], c.w["ones_row"]
        c.mask_q, c.mask_k = c.w["mask_q"], c.w["mask_k"]
        c.block = c.w["block"]
        c.keys = inp["ctx"].shape[2]
        c.ctx = c.w["ctx"]
        c.rest = whole.enter_context(nc.semaphore("rest"))

        c.stage = "load"
        load_inputs(c, keep)

        c.stage = "n0"
        norm_scalars(c, False)
        c.stage = "lat"
        latent_weights(c)
        c.stage = "a0"
        self_attention(c, HD ** -0.5)
        c.stage = "n1"
        norm_scalars(c, True)
        c.stage = "x0"
        wide_weights(c)
        start.close()
        cross_attention_wide(c)
        first.close()
        c.stage = "n2"
        norm_scalars(c, False)
        c.stage = "f0"
        scored_experts(c)
        c.stage = "n3"
        norm_scalars(c, False)
        c.stage = "a1"
        attention_over_heads(c)
        c.stage = "n4"
        norm_scalars(c, False)
        cross_attention_tempered(c)
        most.close()
        c.stage = "n5"
        norm_scalars(c, False)
        mixed_experts(c)



def triangles(experts):
    behind = np.triu(np.ones((experts, experts), np.float32), 1)
    return np.broadcast_to(np.stack([behind, behind.T]), (P, 2, experts, experts))


def constants():
    bf = mybir.dt.np(BF16)
    r = np.arange(P)
    strip = r % STRIP
    block = (strip[:, None] // HD == np.arange(GROUP)).astype(np.float32)
    later = np.where(r[None, :] > r[:, None], MASKED, 0.0)
    return {
        "ident": np.eye(P, dtype=np.float32), "ident16": np.eye(P).astype(bf),
        "mask_q": later.astype(bf), "mask_k": later.T.astype(bf),
        "tri8": triangles(8), "tri4": triangles(4),
        "block": block,
        "ones_row": np.ones((1, 512), np.float32),
    }


def layouts(inputs):
    a = {k: np.asarray(v) for k, v in inputs.items()}
    t = {"x": a["x"]}
    t.update(constants())
    t["a0_dq"], t["a0_uq"] = a["L0_attn_W_dq"].T, a["L0_attn_W_uq"]
    t["a0_dkv"], t["a0_uk"] = a["L0_attn_W_dkv"].T, a["L0_attn_W_uk"]
    t["a0_uv"], t["a0_o"] = a["L0_attn_W_uv"], a["L0_attn_W_o"]
    t["a1_qkv"] = np.concatenate([a["L1_attn_W" + n].T for n in "qkv"], axis=1)
    t["a1_o"] = np.tile(a["L1_attn_Wo"].T.reshape(HEADS, HD, D), (P // HEADS, 1, 1))
    t["a1_b"] = np.broadcast_to(a["L1_attn_bo"][None], (P, D))
    t["a1_rows"] = (np.arange(P)[:, None] // HEADS == np.arange(P // HEADS)).astype(np.float32)
    row = np.arange(P) % STRIP // HD
    shift = (np.arange(P) % STRIP >= 3 * HD) & (np.arange(P) % STRIP < 3 * HD + 3)
    sign = lambda low: np.where(row == low, -1.0, np.where(row < 3, 1.0, 0.0))
    t["a0_split"] = np.stack([sign(2), row == 2, row < 0, sign(1), row == 1, shift], axis=1).astype(np.float32)
    t["ctx"] = a["ctx_1024"].transpose(2, 0, 1)
    inner = a["L0_xattn_w_q"].shape[1]
    per_head = lambda w: w.T.reshape(HEADS, inner // HEADS, D).transpose(1, 0, 2)
    t["x0_q"], t["x0_k"] = per_head(a["L0_xattn_w_q"]), per_head(a["L0_xattn_w_kv"][:, :inner])
    t["x0_v"] = a["L0_xattn_w_kv"][:, inner:]
    t["x0_out"] = a["L0_xattn_w_out"].reshape(HEADS // 2, P, D).transpose(1, 0, 2)
    rows = lambda b: np.broadcast_to(b[None], (P, D))
    t["x0_bias"] = rows(a["L0_xattn_b_out"])
    t["x0_gate"] = np.broadcast_to(a["L0_xattn_gate"][None], (P, 1))
    E, H = a["L0_ffn_W1"].shape[:2]
    t["f0_router"] = a["L0_ffn_Wg"].T
    t["late_f0_1"], t["late_f0_2"] = (a["L0_ffn_W" + n].reshape(E * H, D).T for n in "12")
    down = np.zeros((E, 3 * P, D), np.float32)
    down[:, :H] = a["L0_ffn_W3"].transpose(0, 2, 1)
    t["late_f0_3"] = down.reshape(E, 3, P, D).transpose(2, 0, 1, 3)
    t["x1_q"], t["x1_k"], t["x1_v"], t["x1_o"] = (a["L1_xattn_W" + n].T for n in "qkvo")
    t["x1_bias"] = np.stack([a["L1_xattn_bq"], a["L1_xattn_bk"]], axis=1)
    t["x1_bv"] = np.broadcast_to(a["L1_xattn_bv"][:, None], (D, P))
    t["x1_bo"] = rows(a["L1_xattn_bo"])
    t["x1_w1"], t["x1_w2"] = a["L1_xattn_w1"].T, a["L1_xattn_w2"].T
    t["x1_w3"] = np.broadcast_to(a["L1_xattn_w3"].T, (a["L1_xattn_w3"].shape[1], P))
    t["x1_mlp_b"] = np.stack([a["L1_xattn_b1"], a["L1_xattn_b2"]], axis=1)
    t["x1_b3"] = np.broadcast_to(a["L1_xattn_b3"][None], (P, 1))
    t["x1_heads"] = np.arange(P)[:, None] // HD == np.arange(HEADS)
    t["x1_heads"] = t["x1_heads"].astype(np.float32)
    keys = a["ctx_1024"].shape[1]
    pick = np.zeros((P, 3, 3), np.float32)
    pick[:, 0, 0] = HD ** -0.5 / (P * keys)
    pick[:, 1, 1] = HD ** -0.5 / P
    pick[:, 2, 2] = 1.0 / (P * (keys - 1))
    t["x1_pick"] = pick.reshape(P, 9)
    t["x1_less"] = np.array([[0.0, 0.0, -1.0 / (keys * (keys - 1))]], np.float32)
    place = np.arange(STRIP)[None] // HD == np.arange(GROUP)[:, None]
    t["x1_place"] = np.broadcast_to(place.astype(np.float32), (P, GROUP, STRIP))
    f = lambda n: a["L1_ffn_" + n]
    units = lambda w: w.reshape(D, -1, P)
    down = lambda w: w.reshape(-1, P, w.shape[1]).transpose(1, 0, 2)
    col = lambda b: b.reshape(-1, P).T
    experts = {
        "router": f("router_w"),
        "router_b": np.broadcast_to(np.stack([f("router_b"), f("load_balancer")]), (P, 2, 4)),
        "sw_1": units(f("sw_w1")), "sw_3": units(f("sw_w3")), "sw_2": down(f("sw_w2")),
        "me_eqT": f("me_eq_w").T, "me_vT": f("me_wv").T, "me_oT": f("me_wo").T, "me_v": f("me_wv"), "me_o": f("me_wo"),
        "c1": units(f("me_c1w")), "c1b": col(f("me_c1b")), "c2": down(f("me_c2w")), "c2b": f("me_c2b")[None],
        "cols": np.stack([f(n) for n in ("me_eq_b", "me_bv", "me_bo", "ce_syn_b", "ce_bv")], axis=1),
        "ce_vT": f("ce_wv").T, "ce_o": f("ce_wo"), "ce_synT": f("ce_syn_w").T, "ce_bo": f("ce_bo")[None],
        "norms": np.stack([f(n) for n in ("ce_n1g", "ce_n1b", "ce_n2g", "ce_n2b")], axis=1),
        "f1": units(f("ce_f1w")), "f1b": col(f("ce_f1b")), "f2": down(f("ce_f2w")), "f2b": f("ce_f2b")[None],
        "gen": f("ce_gen_w"), "genb": f("ce_gen_b")[None],
        "ml_1": units(f("ml_w1")), "ml_b1": col(f("ml_b1")), "ml_2": down(f("ml_w2")), "ml_b2": f("ml_b2")[None],
    }
    t.update({"f1_" + n: v for n, v in experts.items()})
    t["x0_ln"] = np.stack([a["L0_xattn_ln_gamma"], a["L0_xattn_ln_beta"]], axis=1)
    return {k: np.ascontiguousarray(v) for k, v in t.items()}


def kernel(**inputs):
    import concourse.bacc as bacc
    from concourse.bass_utils import run_bass_kernel_spmd

    nc = bacc.Bacc("TRN2", target_bir_lowering=False, num_devices=1)
    arrays = layouts(inputs)
    B = arrays["x"].shape[0]
    aps = {k: nc.dram_tensor("in_" + k, v.shape, mybir.dt.from_np(v.dtype), kind="ExternalInput").ap() for k, v in arrays.items()}
    out = nc.dram_tensor("out", (B, P, D), F32, kind="ExternalOutput").ap()
    decoder(nc, aps, out, B)
    r = run_bass_kernel_spmd(nc, [{"in_" + k: v for k, v in arrays.items()}], core_ids=[0])
    return r.results[0]["out"]
```
